# Optimizing a Trainium2 kernel written in Bass

```python
import numpy as np
import jax
import jax.numpy as jnp

def _softmax(x, axis=-1):
    return jax.nn.softmax(x, axis=axis)

def _gelu(x):
    return jax.nn.gelu(x, approximate=True)

def _silu(x):
    return jax.nn.silu(x)

def _sigmoid(x):
    return jax.nn.sigmoid(x)

def _layernorm(x, axis=-1, eps=1e-05):
    m = jnp.mean(x, axis=axis, keepdims=True)
    v = jnp.var(x, axis=axis, keepdims=True)
    return (x - m) / jnp.sqrt(v + eps)

def _scatter_add(tgt, idx, src, axis=0):
    return tgt.at[idx].add(src)

def _segment_sum(src, seg, n):
    return jax.ops.segment_sum(src, seg, n)
kernel_name = 'mk_lm_tower_d2_tok_ids256_r4_82a087'

def setup_inputs(seed: int=0):
    np.random.seed(seed)
    _w = jnp.asarray

    def _rec_inputs():
        import jax
        import jax.numpy as jnp
        _rk = jax.random.key(seed)
        x = jax.random.randint(jax.random.fold_in(_rk, 1), (16, 128), 0, 50257, jnp.int32)
        return x
    x = _rec_inputs()

    def _L0_tok_setup():
        import jax, jax.numpy as jnp
        import numpy as np
        VOCAB = 50257
        DIM = 64

        def _positional_table(seq_len, dim, dtype=jnp.float32):
            pos = jnp.arange(seq_len, dtype=dtype)[:, None]
            d = jnp.arange(dim)
            exponent = (d - d % 2).astype(dtype) / dim
            inv_freq = jnp.power(jnp.asarray(10000.0, dtype), -exponent)
            angle = pos * inv_freq
            return jnp.where(d % 2 == 0, jnp.sin(angle), jnp.cos(angle))
        key = jax.random.key(seed)
        k1, k2 = jax.random.split(key)
        x = jax.random.randint(k1, (32, 1024), 0, VOCAB)
        W = jax.random.normal(k2, (VOCAB, DIM), dtype=jnp.float32)
        return {'x': x, 'W': W}
    _L0_tok_all = _L0_tok_setup()
    _L0_tok_in = {k: v for k, v in _L0_tok_all.items() if k in ('W',)}
    del _L0_tok_all

    def _L0_attn_setup():
        import jax, jax.numpy as jnp
        import numpy as np
        import math
        B, N, D = (4, 1024, 64)
        key = jax.random.key(seed)
        k0, k1, k2, k3 = jax.random.split(key, 4)
        bound = math.sqrt(6.0 / D)
        return {'x': jax.random.normal(k0, (B, N, D), dtype=jnp.float32), 'Wq': jax.random.uniform(k1, (D, D), dtype=jnp.float32, minval=-bound, maxval=bound), 'Wk': jax.random.uniform(k2, (D, D), dtype=jnp.float32, minval=-bound, maxval=bound), 'Wv': jax.random.uniform(k3, (D, D), dtype=jnp.float32, minval=-bound, maxval=bound)}
    _L0_attn_all = _L0_attn_setup()
    _L0_attn_in = {k: v for k, v in _L0_attn_all.items() if k in ('Wq', 'Wk', 'Wv')}
    del _L0_attn_all

    def _L0_ffn_setup():
        import jax, jax.numpy as jnp
        import numpy as np
        E = 8
        K = 2
        D = 64
        H = 128
        DOUT = 64
        EPS = 1e-05
        key = jax.random.key(seed)
        ks = jax.random.split(key, 9)
        s = 0.02
        return {'x': jax.random.normal(ks[0], (4, 2048, D), jnp.float32), 'gamma': 1.0 + 0.05 * jax.random.normal(ks[1], (D,), jnp.float32), 'beta': 0.05 * jax.random.normal(ks[2], (D,), jnp.float32), 'Wr': 0.01 * jax.random.normal(ks[3], (D, E), jnp.float32), 'br': jnp.zeros((E,), jnp.float32), 'W1': s * jax.random.normal(ks[4], (E, D, H), jnp.float32), 'b1': s * jax.random.normal(ks[5], (E, H), jnp.float32), 'W2': s * jax.random.normal(ks[6], (E, H, DOUT), jnp.float32), 'b2': s * jax.random.normal(ks[7], (E, DOUT), jnp.float32)}
    _L0_ffn_all = _L0_ffn_setup()
    _L0_ffn_in = {k: v for k, v in _L0_ffn_all.items() if k in ('gamma', 'beta', 'Wr', 'br', 'W1', 'b1', 'W2', 'b2')}
    del _L0_ffn_all

    def _L1_attn_setup():
        import jax, jax.numpy as jnp
        import numpy as np

        def softcap(x, a=10.0):
            return a * jnp.tanh(x / a)
        key = jax.random.key(seed)
        B, T, D = (4, 512, 64)
        ks = jax.random.split(key, 5)
        w = lambda k, s: jax.random.normal(k, s, dtype=jnp.float32) * 0.02
        return {'x': jax.random.normal(ks[0], (B, T, D), dtype=jnp.float32), 'Wq': w(ks[1], (D, D)), 'bq': jnp.zeros((D,), jnp.float32), 'Wk': w(ks[2], (D, D)), 'bk': jnp.zeros((D,), jnp.float32), 'Wv': w(ks[3], (D, D)), 'bv': jnp.zeros((D,), jnp.float32), 'Wg': w(ks[4], (D, 3 * D)), 'bg': jnp.zeros((3 * D,), jnp.float32), 'input_bias': -jnp.ones((D,), jnp.float32), 'norm_scale': jnp.ones((D,), jnp.float32)}
    _L1_attn_all = _L1_attn_setup()
    _L1_attn_in = {k: v for k, v in _L1_attn_all.items() if k in ('Wq', 'bq', 'Wk', 'bk', 'Wv', 'bv', 'Wg', 'bg', 'input_bias', 'norm_scale')}
    del _L1_attn_all

    def _L1_ffn_setup():
        import jax, jax.numpy as jnp
        import numpy as np
        B, T, IN_DIM = (64, 64, 64)
        HID, OUT_DIM = (128, 64)
        N_LAYERS, N_EXPERTS, N_SHARED = (2, 16, 1)
        key = jax.random.key(seed)
        ks = jax.random.split(key, 10)
        s = 0.02
        x = jax.random.normal(ks[0], (B, T, IN_DIM), dtype=jnp.float32)
        route_id = jax.random.randint(ks[1], (B,), 0, N_EXPERTS)
        Wi = jax.random.normal(ks[2], (HID, IN_DIM), dtype=jnp.float32) * s
        bi = jnp.zeros((HID,), dtype=jnp.float32)
        Wr = jax.random.normal(ks[3], (N_LAYERS, N_EXPERTS, HID, HID), dtype=jnp.float32) * s
        br = jax.random.normal(ks[4], (N_LAYERS, N_EXPERTS, HID), dtype=jnp.float32) * s
        Ws = jax.random.normal(ks[5], (N_LAYERS, N_SHARED, HID, HID), dtype=jnp.float32) * s
        bs = jax.random.normal(ks[6], (N_LAYERS, N_SHARED, HID), dtype=jnp.float32) * s
        Wo = jax.random.normal(ks[7], (OUT_DIM, HID), dtype=jnp.float32) * s
        bo = jnp.zeros((OUT_DIM,), dtype=jnp.float32)
        return {'x': x, 'route_id': route_id, 'Wi': Wi, 'bi': bi, 'Wr': Wr, 'br': br, 'Ws': Ws, 'bs': bs, 'Wo': Wo, 'bo': bo}
    _L1_ffn_all = _L1_ffn_setup()
    _L1_ffn_in = {k: v for k, v in _L1_ffn_all.items() if k in ('route_id', 'Wi', 'bi', 'Wr', 'br', 'Ws', 'bs', 'Wo', 'bo')}
    del _L1_ffn_all
    return {'x': x, 'L0_tok_W': _L0_tok_in['W'], 'L0_attn_Wq': _L0_attn_in['Wq'], 'L0_attn_Wk': _L0_attn_in['Wk'], 'L0_attn_Wv': _L0_attn_in['Wv'], 'L0_ffn_gamma': _L0_ffn_in['gamma'], 'L0_ffn_beta': _L0_ffn_in['beta'], 'L0_ffn_Wr': _L0_ffn_in['Wr'], 'L0_ffn_br': _L0_ffn_in['br'], 'L0_ffn_W1': _L0_ffn_in['W1'], 'L0_ffn_b1': _L0_ffn_in['b1'], 'L0_ffn_W2': _L0_ffn_in['W2'], 'L0_ffn_b2': _L0_ffn_in['b2'], 'L1_attn_Wq': _L1_attn_in['Wq'], 'L1_attn_bq': _L1_attn_in['bq'], 'L1_attn_Wk': _L1_attn_in['Wk'], 'L1_attn_bk': _L1_attn_in['bk'], 'L1_attn_Wv': _L1_attn_in['Wv'], 'L1_attn_bv': _L1_attn_in['bv'], 'L1_attn_Wg': _L1_attn_in['Wg'], 'L1_attn_bg': _L1_attn_in['bg'], 'L1_attn_input_bias': _L1_attn_in['input_bias'], 'L1_attn_norm_scale': _L1_attn_in['norm_scale'], 'L1_ffn_route_id': _L1_ffn_in['route_id'], 'L1_ffn_Wi': _L1_ffn_in['Wi'], 'L1_ffn_bi': _L1_ffn_in['bi'], 'L1_ffn_Wr': _L1_ffn_in['Wr'], 'L1_ffn_br': _L1_ffn_in['br'], 'L1_ffn_Ws': _L1_ffn_in['Ws'], 'L1_ffn_bs': _L1_ffn_in['bs'], 'L1_ffn_Wo': _L1_ffn_in['Wo'], 'L1_ffn_bo': _L1_ffn_in['bo']}

def reference(x, L0_tok_W, L0_attn_Wq, L0_attn_Wk, L0_attn_Wv, L0_ffn_gamma, L0_ffn_beta, L0_ffn_Wr, L0_ffn_br, L0_ffn_W1, L0_ffn_b1, L0_ffn_W2, L0_ffn_b2, L1_attn_Wq, L1_attn_bq, L1_attn_Wk, L1_attn_bk, L1_attn_Wv, L1_attn_bv, L1_attn_Wg, L1_attn_bg, L1_attn_input_bias, L1_attn_norm_scale, L1_ffn_route_id, L1_ffn_Wi, L1_ffn_bi, L1_ffn_Wr, L1_ffn_br, L1_ffn_Ws, L1_ffn_bs, L1_ffn_Wo, L1_ffn_bo):
    import jax
    import jax.numpy as jnp

    def _L0_tok_ref(x, W):
        import jax, jax.numpy as jnp
        import numpy as np
        VOCAB = 50257
        DIM = 64

        def _positional_table(seq_len, dim, dtype=jnp.float32):
            pos = jnp.arange(seq_len, dtype=dtype)[:, None]
            d = jnp.arange(dim)
            exponent = (d - d % 2).astype(dtype) / dim
            inv_freq = jnp.power(jnp.asarray(10000.0, dtype), -exponent)
            angle = pos * inv_freq
            return jnp.where(d % 2 == 0, jnp.sin(angle), jnp.cos(angle))
        seq_len = x.shape[1]
        pe = _positional_table(seq_len, W.shape[1], W.dtype)
        return W[x] + pe[None, :, :]

    def _L0_attn_ref(x, Wq, Wk, Wv):
        import jax, jax.numpy as jnp
        import numpy as np
        import math
        B, N, D = (4, 1024, 64)
        q = x @ Wq.T
        k = x @ Wk.T
        v = x @ Wv.T
        n = x.shape[1]
        d_k = x.shape[2]
        mask = jnp.triu(jnp.ones((n, n), dtype=x.dtype), k=1)
        scale = jnp.asarray(1.0 / math.sqrt(d_k), dtype=x.dtype)
        s = (jnp.einsum('bnd,bmd->bnm', q, k) - (1.0 - mask) * 10000000000.0) * scale
        s = jax.nn.softmax(s, axis=1)
        return jnp.einsum('bnm,bmd->bnd', s, v)

    def _L0_ffn_ref(x, gamma, beta, Wr, br, W1, b1, W2, b2):
        import jax, jax.numpy as jnp
        import numpy as np
        E = 8
        K = 2
        D = 64
        H = 128
        DOUT = 64
        EPS = 1e-05
        mu = jnp.mean(x, axis=-1, keepdims=True)
        var = jnp.mean(jnp.square(x - mu), axis=-1, keepdims=True)
        xn = (x - mu) * jax.lax.rsqrt(var + EPS) * gamma + beta
        logits = jnp.einsum('bsd,de->bse', xn, Wr) + br
        top_vals, top_idx = jax.lax.top_k(logits, K)
        w = jax.nn.softmax(top_vals, axis=-1)
        w_full = jnp.einsum('bsk,bske->bse', w, jax.nn.one_hot(top_idx, E, dtype=w.dtype))
        y = jnp.zeros(x.shape[:-1] + (DOUT,), x.dtype)
        for e in range(E):
            h = jax.nn.gelu(jnp.einsum('bsd,dh->bsh', xn, W1[e]) + b1[e], approximate=False)
            y_e = jnp.einsum('bsh,hd->bsd', h, W2[e]) + b2[e]
            y = y + y_e * w_full[..., e, None]
        return y

    def _L1_attn_ref(x, Wq, bq, Wk, bk, Wv, bv, Wg, bg, input_bias, norm_scale):
        import jax, jax.numpy as jnp
        import numpy as np

        def softcap(x, a=10.0):
            return a * jnp.tanh(x / a)
        B, T, D = x.shape
        inv_sqrt_d = 1.0 / jnp.sqrt(jnp.asarray(D, jnp.float32))
        q = x @ Wq + bq
        k = (x @ Wk + bk) * inv_sqrt_d
        v = x @ Wv + bv
        gates = x @ Wg + bg
        i_pre, f_pre, o_pre = jnp.split(gates, 3, axis=-1)
        log_i = softcap(i_pre + input_bias)
        log_f = -jax.nn.softplus(f_pre)

        def step(carry, inp):
            M, n, m = carry
            qt, kt, vt, li, lf, op = inp
            m_next = jnp.maximum(lf + m, li)
            i_s = jnp.exp(li - m_next)
            f_s = jnp.exp(lf + m - m_next)
            M = f_s[:, :, None] * M + i_s[:, :, None] * (vt[:, :, None] * kt[:, None, :])
            n = f_s * n + i_s * kt
            h_raw = jnp.einsum('bij,bj->bi', M, qt)
            denom = jnp.maximum(jnp.abs(jnp.einsum('bi,bi->b', n, qt))[:, None], 1e-06)
            h = jax.nn.sigmoid(op) * (h_raw / denom)
            return ((M, n, m_next), h)
        M0 = jnp.zeros((B, D, D), jnp.float32)
        n0 = jnp.zeros((B, D), jnp.float32)
        m0 = jnp.zeros((B, D), jnp.float32)
        xs = tuple((jnp.swapaxes(a, 0, 1) for a in (q, k, v, log_i, log_f, o_pre)))
        _, hs = jax.lax.scan(step, (M0, n0, m0), xs)
        out = jnp.swapaxes(hs, 0, 1)
        rms = jnp.sqrt(jnp.mean(out * out, axis=-1, keepdims=True) + 1e-08)
        return out / rms * norm_scale

    def _L1_ffn_ref(x, route_id, Wi, bi, Wr, br, Ws, bs, Wo, bo):
        import jax, jax.numpy as jnp
        import numpy as np
        B, T, IN_DIM = (64, 64, 64)
        HID, OUT_DIM = (128, 64)
        N_LAYERS, N_EXPERTS, N_SHARED = (2, 16, 1)
        flat = x.reshape(-1, x.shape[-1])
        n_tok = flat.shape[0]
        route = jnp.repeat(route_id, n_tok // route_id.shape[0])
        h = jax.nn.relu(flat @ Wi.T + bi)
        n_layers, n_experts = (Wr.shape[0], Wr.shape[1])
        for l in range(n_layers):
            shared = (jnp.einsum('nd,shd->snh', h, Ws[l]) + bs[l][:, None, :]).mean(axis=0)
            routed = jnp.zeros_like(h)
            for e in range(n_experts):
                ye = h @ Wr[l, e].T + br[l, e]
                routed = routed + jnp.where((route == e)[:, None], ye, 0.0)
            h = jax.nn.relu(shared + routed + h)
        out = h @ Wo.T + bo
        return out.reshape(*x.shape[:-1], out.shape[-1])
    h = _L0_tok_ref(x, L0_tok_W)
    h = h + _L0_attn_ref(_layernorm(h, axis=-1), L0_attn_Wq, L0_attn_Wk, L0_attn_Wv)
    h = h + _L0_ffn_ref(_layernorm(h, axis=-1), L0_ffn_gamma, L0_ffn_beta, L0_ffn_Wr, L0_ffn_br, L0_ffn_W1, L0_ffn_b1, L0_ffn_W2, L0_ffn_b2)
    h = h + _L1_attn_ref(_layernorm(h, axis=-1), L1_attn_Wq, L1_attn_bq, L1_attn_Wk, L1_attn_bk, L1_attn_Wv, L1_attn_bv, L1_attn_Wg, L1_attn_bg, L1_attn_input_bias, L1_attn_norm_scale)
    h = h + _L1_ffn_ref(_layernorm(h, axis=-1), L1_ffn_route_id, L1_ffn_Wi, L1_ffn_bi, L1_ffn_Wr, L1_ffn_br, L1_ffn_Ws, L1_ffn_bs, L1_ffn_Wo, L1_ffn_bo)
    return h

_drawn_inputs = setup_inputs


def setup_inputs(seed=0):
    import zlib

    import numpy as np

    out = dict(_drawn_inputs(seed))
    spreads = {'L0_ffn_br': (0.0, 0.295),
     'L1_attn_bq': (0.0, 0.1),
     'L1_attn_bk': (0.0, 0.1),
     'L1_attn_bv': (0.0, 0.1),
     'L1_attn_bg': (0.0, 0.335),
     'L1_attn_input_bias': (-1.0, 0.6),
     'L1_attn_norm_scale': (1.0, 0.2),
     'L1_ffn_bi': (0.0, 0.8),
     'L1_ffn_bo': (0.0, 0.323)}
    factors = {'L0_ffn_gamma': 8.0,
     'L0_ffn_beta': 8.0,
     'L0_ffn_Wr': 5.308,
     'L0_ffn_W1': 3.577,
     'L0_ffn_b1': 8.0,
     'L0_ffn_W2': 3.472,
     'L0_ffn_b2': 3.223,
     'L1_ffn_Wi': 5.054,
     'L1_ffn_Wr': 8.0,
     'L1_ffn_br': 8.0,
     'L1_ffn_Ws': 8.0,
     'L1_ffn_bs': 8.0,
     'L1_ffn_Wo': 3.27}
    for name, (base, spread) in spreads.items():
        noise = np.random.default_rng([zlib.crc32(name.encode()), seed]).standard_normal(out[name].shape)
        drawn = base * np.exp(spread * noise) if base else spread * noise
        out[name] = jnp.asarray(drawn.astype(out[name].dtype))
    for name, factor in factors.items():
        out[name] = (out[name] * factor).astype(out[name].dtype)
    return out
```

```python
from contextlib import ExitStack

import numpy as np
import concourse.bass as bass
from concourse import mybir


P = 128
B = 16
D = 64
HALVES = 2
Q = 4
BQ = B // Q
PQ = BQ // HALVES
C = BQ * D
E = 8
HID = 128
NE1 = 16
L1 = 2
GROUPS = 64
GT = B * P // GROUPS
GQ = GROUPS // Q
SLOT = HID + 1
LEVELS = 7
EPS = 1e-5
SCALE = D ** -0.5
MASKED = 1e10

ALU = mybir.AluOpType
ACT = mybir.ActivationFunctionType
F32 = mybir.dt.float32
I32 = mybir.dt.int32
AX = mybir.AxisListType

C_ID = 0
C_CAUSAL = C_ID + P
C_SUM = C_CAUSAL + P
C_MASK = C_SUM + LEVELS * P
C_TIE = C_MASK + (LEVELS + 1) * P
C_RANK = C_TIE + E * E
C_POS = C_RANK + E
C_HALF = C_POS + D
C_POW = C_HALF + HALVES
N_CONST = C_POW + BQ

(M_V0, M_F, M_I, M_Q, M_K, M_V, M_O) = range(7)
NM = 7
(K_GAMMA, K_BETA, K_BGI, K_IB, K_BGF, K_BQ, K_BK) = range(7)
NK = 7
R_BR = 0
R_NS = R_BR + E
R_BO = R_NS + D
R_BV = R_BO + D
R_BG = R_BV + D
NR = R_BG + D
W_W2 = 0
W_WO = W_W2 + E * D
W_B1 = W_WO + D
W_BI = W_B1 + E
NW = W_BI + 1


def shape_constants():
    c = np.zeros((P, N_CONST), np.float32)
    r = np.arange(P)[:, None]
    t = np.arange(P)[None, :]
    c[:, C_ID:C_ID + P] = r == t
    c[:, C_CAUSAL:C_CAUSAL + P] = np.where(t >= r, np.float32(MASKED), np.float32(0))
    for n in range(LEVELS):
        half = P >> (n + 1)
        mid = t // (2 * half) * (2 * half) + half
        left = t < mid
        span = np.where(left, (r > t) & (r < mid), (r >= mid) & (r <= t))
        c[:, C_SUM + n * P:C_SUM + (n + 1) * P] = span
        same = r // (2 * half) == t // (2 * half)
        c[:, C_MASK + n * P:C_MASK + (n + 1) * P] = same & (r % (2 * half) < half) & (t % (2 * half) >= half)
    c[:, C_MASK + LEVELS * P:C_MASK + (LEVELS + 1) * P] = r == t
    e = np.arange(E)
    c[:, C_TIE:C_TIE + E * E] = (e[None, :] < e[:, None]).astype(np.float32).reshape(1, E * E)
    c[:, C_RANK:C_RANK + E] = (e - (E - 1) + 2).astype(np.float32)[None, :]
    d = np.arange(D)
    freq = np.power(np.float32(10000.0), -((d - d % 2).astype(np.float32) / np.float32(D)))
    angle = np.arange(P, dtype=np.float32)[:, None] * freq[None, :]
    c[:, C_POS:C_POS + D] = np.where(d % 2 == 0, np.sin(angle), np.cos(angle))
    for h in range(HALVES):
        c[h * D:(h + 1) * D, C_HALF + h] = 1.0
    c[:, C_POW:C_POW + BQ] = -0.5
    return c


def tower(nc, table, tokens, route, consts_d, wqk_d, diag_d, wr_d, first_d, cols_d, rows_d, hid_d, b2_d,
          routed_d, shared_d, out):
    with ExitStack() as ctx:
        def sb(name, shape, dt=F32):
            return ctx.enter_context(nc.sbuf_tensor(name, shape, dt))

        def sem(name):
            return ctx.enter_context(nc.semaphore(name))

        psum = ctx.enter_context(nc.psum_tensor("psum", [P, 8, 512], F32))

        consts = sb("consts", [P, N_CONST])
        wqk = sb("wqk", [D, 2, D])
        diag = sb("diag", [P, NM, P])
        score_w = sb("score_w", [P, P])
        router_w = sb("router_w", [P, HALVES * E])
        first = sb("first", [P, E + 1, HID])
        cols = sb("cols", [P, NK])
        cols2 = sb("cols2", [P, 3])
        rows = sb("rows", [P, NR])
        gate_bias = sb("gate_bias", [P, 2 * HALVES * D])
        hidw = sb("hidw", [P, NW])
        b2 = sb("b2", [1, E * D])
        ones = sb("ones", [1, P])
        routed = sb("routed", [P, L1 * NE1 * SLOT])
        shared = sb("shared", [P, L1 * SLOT])
        slots = sb("slots", [P, 2 * L1 * GQ * SLOT])
        route_sb = sb("route_sb", [1, GROUPS], I32)
        tok_sb = sb("tok_sb", [P, B], I32)
        ident = consts[:, C_ID:C_ID + P]

        h = sb("h", [P, B * D])
        bn = sb("bn", [P, B, 6])
        mv = sb("mv", [P, 4, B, 2])
        var = sb("var", [P, 5, B])
        rstd = sb("rstd", [P, 5, B])
        xn = sb("xn", [P, B * D])
        xT = sb("xT", [P, B * D])

        work = sb("work", [P, 5, B * D])
        zT = work[:, 0, :]
        sc = work[:, 1, :].rearrange("p (a b t) -> p a b t", a=2, b=BQ)
        prob = work[:, 2, :].rearrange("p (a b t) -> p a b t", a=2, b=BQ)
        nmax = sb("nmax", [P, B])
        nbias = sb("nbias", [P, B])
        psums = sb("psums", [P, B])
        rsum = sb("rsum", [P, B])
        vs = sb("vs", [P, 2, C])

        logit = sb("logit", [P, B, E])
        lmax = sb("lmax", [P, B])
        ge = work[:, 3, :].rearrange("p (b e j) -> p b e j", b=B, e=E)
        rank = sb("rank", [P, B, E])
        sel = sb("sel", [P, B, E])
        lexp = sb("lexp", [P, B, E])
        lsum = sb("lsum", [P, B])
        wfull = sb("wfull", [P, B, E])
        big = sb("big", [P, 2 * 8 * 512])
        hid = big[:, :].rearrange("p (a e h c) -> p a e h c", a=2, e=E, h=HALVES)
        ye = work[:, 4, :].rearrange("p (a c) -> p a c", a=2)
        ysum = sb("ysum", [P, 2, D])

        qT = work[:, 0, :]
        kT = work[:, 1, :]
        li = work[:, 2, :]
        neg_f = work[:, 3, :]
        fs = work[:, 4, :]
        vo = sb("vo", [P, B // 2, 2 * HALVES * D])
        m = sb("m", [P, B // 2, P + 1])
        phi = sb("phi", [P, B * D])
        phi_t = sb("phi_t", [P, Q, C])
        iota_t = sb("iota_t", [P, 2, C])
        rden = sb("rden", [P, B])
        score = sb("score", [P, 2, BQ * P])
        level_s = big[:, :].rearrange("p (a n c) -> p a n c", a=2, n=LEVELS + 1)
        G = sb("G", [P, 2, LEVELS + 1, C])
        vg = sb("vg", [P, 4, 2, C])
        ug = sb("ug", [P, LEVELS + 1, C])
        acc = sb("acc", [P, C])
        gated = sb("gated", [P, 2, C])
        sq = sb("sq", [P, C])

        feed = G[:, :, :, :].rearrange("p a n c -> p (a n c)").rearrange("p (f a c) -> p f a c", f=4, a=2)
        f0, fb, f1, f2 = (feed[:, n, :, :] for n in range(4))
        outs = kT

        tok_in = sem("tok_in")
        consts_in = sem("consts_in")
        small_in = sem("small_in")
        diag_in = sem("diag_in")
        first_in = sem("first_in")
        hid_in = sem("hid_in")
        route_in = sem("route_in")
        slots_in = sem("slots_in")
        embed_in = [sem(f"embed_in{q}") for q in range(Q)]
        out_done = sem("out_done")
        zeroed = sem("zeroed")
        score_w_ps = sem("score_w_ps")
        score_w_ok = sem("score_w_ok")
        setup_ok = sem("setup_ok")
        ln_stats = sem("ln_stats")
        ln_rstd = sem("ln_rstd")
        ln_out = sem("ln_out")
        xT_ps = sem("xT_ps")
        xT_ok = sem("xT_ok")
        z_ps = sem("z_ps")
        z_ok = sem("z_ok")
        v_ps = sem("v_ps")
        s_ps = sem("s_ps")
        s_masked = sem("s_masked")
        s_bias = sem("s_bias")
        prob_ok = sem("prob_ok")
        vs_ok = sem("vs_ok")
        av_ps = sem("av_ps")
        av_added = sem("av_added")
        logit_ps = sem("logit_ps")
        logit_off = sem("logit_off")
        logit_exp = sem("logit_exp")
        up_ps = sem("up_ps")
        up_ok = sem("up_ok")
        down_ps = sem("down_ps")
        down_ok = sem("down_ok")
        gates_ps = sem("gates_ps")
        gates_read = sem("gates_read")
        vo_ps = sem("vo_ps")
        vo_ok = sem("vo_ok")
        sig_ok = sem("sig_ok")
        absf_ok = sem("absf_ok")
        softplus_ok = sem("softplus_ok")
        expo_ok = sem("expo_ok")
        decay_ok = sem("decay_ok")
        nq_ok = sem("nq_ok")
        score_ps = sem("score_ps")
        score_ok = sem("score_ok")
        decay_ps = sem("decay_ps")
        decay_t = sem("decay_t")
        den_ps = sem("den_ps")
        vi_ok = sem("vi_ok")
        level_s_ok = sem("level_s_ok")
        arg_ps = sem("arg_ps")
        G_ok = sem("G_ok")
        vg_ok = sem("vg_ok")
        u_ps = sem("u_ps")
        u_read = sem("u_read")
        ms_ok = sem("ms_ok")
        rms_ok = sem("rms_ok")
        slot_ok = sem("slot_ok")
        f0_ps = sem("f0_ps")
        f0_ok = sem("f0_ok")
        fl_ps = sem("fl_ps")
        fl_biased = sem("fl_biased")
        fl_ok = sem("fl_ok")
        fo_ps = sem("fo_ps")
        out_ok = sem("out_ok")
        v_order = sem("v_order")
        g_order = sem("g_order")
        a_order = sem("a_order")

        def qs(q):
            return slice(q * C, (q + 1) * C)

        def per_seq(ap, n=BQ, k=D):
            return ap.unsqueeze(2).to_broadcast([P, n, k])

        def repeated(ap, n, k):
            return ap.unsqueeze(1).to_broadcast([P, n, k])

        block = ctx.enter_context(nc.Block())

        @block.sync
        def _(sp):
            sp.dma_start(tok_sb[:, :], tokens).then_inc(tok_in, 16)
            sp.dma_start(wqk[:, :, :], wqk_d).then_inc(small_in, 16)
            sp.dma_start(consts[:, :], consts_d).then_inc(consts_in, 16)
            sp.dma_start(rows[:, :], rows_d.partition_broadcast(P)).then_inc(small_in, 16)
            sp.dma_start(b2[:, :], b2_d).then_inc(small_in, 16)
            sp.wait_ge(zeroed, 2)
            for n in range(HALVES):
                part = slice(n * D, (n + 1) * D)
                sp.dma_start(diag[part, :, part], diag_d).then_inc(diag_in, 16)
                sp.dma_start(router_w[part, n * E:(n + 1) * E], wr_d).then_inc(diag_in, 16)
                sp.dma_start(cols[part, :], cols_d).then_inc(diag_in, 16)
                sp.dma_start(first[part, :, :], first_d).then_inc(first_in, 16)
            sp.dma_start(hidw[:, :], hid_d).then_inc(hid_in, 16)
            sp.dma_start(route_sb[:, :], route).then_inc(route_in, 16)
            sp.dma_start(shared[:, :], shared_d).then_inc(slots_in, 16)
            sp.dma_start(routed[:, :], routed_d).then_inc(slots_in, 16)
            for q in range(Q):
                sp.wait_ge(out_ok, q + 1)
                sp.dma_start(out[q * BQ:(q + 1) * BQ].rearrange("b t d -> t b d"),
                             outs[:, qs(q)].rearrange("p (b d) -> p b d", b=BQ)).then_inc(out_done, 16)
            sp.wait_ge(out_done, 16 * Q)

        @block.gpsimd
        def _(gp):
            def power(n, q, scale, shift, src, wait, done):
                seqs = slice(q * BQ, (q + 1) * BQ)
                gp.wait_ge(*wait)
                nc.gpsimd.tensor_scalar(var[:, n, seqs], src, scale, shift, ALU.mult, ALU.add).then_inc(g_order, 1)
                count[0] += 1
                gp.wait_ge(g_order, count[0])
                nc.gpsimd.tensor_tensor(rstd[:, n, seqs], var[:, n, seqs], consts[:, C_POW:C_POW + BQ],
                                        ALU.pow).then_inc(done, 1)

            count = [0]

            def norm_power(n, q):
                scale, shift = (1.0 + EPS, EPS * EPS) if n == 1 else (1.0, EPS)
                power(n, q, scale, shift, mv[:, n, q * BQ:(q + 1) * BQ, 1], (ln_stats, n * Q + q + 1), ln_rstd)

            gp.wait_ge(tok_in, 16)
            gp.wait_ge(consts_in, 16)
            for q in range(Q):
                for b in range(q * BQ, (q + 1) * BQ):
                    nc.gpsimd.indirect_dma_start(
                        out=h[:, b * D:(b + 1) * D], out_offset=None, in_=table,
                        in_offset=bass.IndirectOffsetOnAxis(ap=tok_sb[:, b:b + 1], axis=0),
                    ).then_inc(embed_in[q], 16)
                if q >= 1:
                    norm_power(0, q - 1)
            norm_power(0, Q - 1)
            for q in range(Q):
                norm_power(1, q)
            gp.wait_ge(slots_in, 32)
            gp.wait_ge(route_in, 16)
            for n in range(L1):
                nc.gpsimd.tensor_tensor(shared[:, n * SLOT:n * SLOT + HID], shared[:, n * SLOT:n * SLOT + HID],
                                        ident, ALU.add).then_inc(g_order, 1)
            count[0] += L1
            gp.wait_ge(g_order, count[0])

            def merge(q):
                if q >= 2:
                    gp.wait_ge(fl_biased, L1 * (q - 1))
                with gp.Fori(0, GQ) as g:
                    expert = gp.value_load(route_sb[0:1, bass.ds(g + q * GQ, 1)], min_val=0, max_val=NE1 - 1)
                    for n in range(L1):
                        nc.gpsimd.tensor_tensor(
                            slots[:, bass.ds(g * SLOT + (q % 2 * L1 + n) * GQ * SLOT, SLOT)],
                            routed[:, bass.ds(expert * SLOT + n * NE1 * SLOT, SLOT)],
                            shared[:, n * SLOT:(n + 1) * SLOT], ALU.add).then_inc(slot_ok, 1)

            merge(0)
            merge(1)
            for q in range(Q):
                norm_power(2, q)

            def mask_levels(q):
                gp.wait_ge(score_ok, q + 1)
                if q >= 2:
                    gp.wait_ge(u_ps, 4 * (q - 1))
                if q < 2:
                    gp.wait_ge(down_ps, B)
                for n in range(LEVELS + 1):
                    mask = consts[:, C_MASK + n * P:C_MASK + (n + 1) * P]
                    last = nc.gpsimd.tensor_tensor(
                        level_s[:, q % 2, n, :].rearrange("p (b t) -> p b t", b=BQ),
                        score[:, q % 2, :].rearrange("p (b t) -> p b t", b=BQ),
                        repeated(mask, BQ, P), ALU.mult)
                last.then_inc(level_s_ok, 1)

            for i in range(Q + 1):
                if i < Q:
                    mask_levels(i)
                if i >= 1:
                    q = i - 1
                    power(4, q, 1.0 / D, 1e-8, var[:, 3, q * BQ:(q + 1) * BQ], (ms_ok, q + 1), rms_ok)
            for q in range(Q):
                norm_power(3, q)
            for q in range(2, Q):
                merge(q)

        @block.scalar
        def _(act):
            def copy_xT(n, q):
                act.wait_ge(xT_ps, n * Q + q + 1)
                dst, src = xT[:, qs(q)], psum[:, q % 2, 0:C]
                if n == 1:
                    nc.scalar.activation(dst, src, ACT.Identity, bias=cols[:, K_BETA:K_BETA + 1],
                                         scale=cols[:, K_GAMMA:K_GAMMA + 1]).then_inc(xT_ok, 1)
                else:
                    nc.scalar.activation(dst, src, ACT.Copy).then_inc(xT_ok, 1)

            def copy_z(q):
                act.wait_ge(z_ps, q + 1)
                nc.scalar.activation(zT[:, qs(q)], psum[:, 2, 0:C], ACT.Copy).then_inc(z_ok, 1)

            def softmax_exp(q):
                act.wait_ge(s_bias, q + 1)
                if q >= 2:
                    act.wait_ge(av_ps, q - 1)
                for j in range(BQ):
                    k = q * BQ + j
                    last = nc.scalar.activation(prob[:, q % 2, j, :], sc[:, q % 2, j, :], ACT.Exp,
                                                bias=nbias[:, k:k + 1], scale=SCALE,
                                                accum_out=psums[:, k:k + 1])
                last.then_inc(prob_ok, 1)

            act.wait_ge(diag_in, 16 * 6)
            for i in range(Q + 2):
                if i < Q:
                    copy_xT(0, i)
                if 0 <= i - 1 < Q:
                    copy_z(i - 1)
                if 0 <= i - 2 < Q:
                    softmax_exp(i - 2)

            for q in range(Q):
                copy_xT(1, q)
            act.wait_ge(logit_off, 1)
            nc.scalar.activation(lexp[:, :, :], rank[:, :, :], ACT.Exp).then_inc(logit_exp, 1)
            act.wait_ge(hid_in, 16)
            for q in range(Q):
                for e in range(E):
                    n = q * E + e
                    pair = 3 + 2 * (n % 2)
                    act.wait_ge(up_ps, n + 1)
                    if q >= 2 and e == 0:
                        act.wait_ge(down_ps, BQ * (q - 1))
                    nc.scalar.activation(hid[:, q % 2, e, :, :], psum[:, pair:pair + 2, 0:C], ACT.Gelu,
                                         bias=hidw[:, W_B1 + e:W_B1 + e + 1]).then_inc(up_ok, 1)

            act.wait_ge(setup_ok, 1)

            def gates(q):
                act.wait_ge(gates_ps, q + 1)
                nc.scalar.activation(li[:, qs(q)], psum[:, 2, 0:C], ACT.Tanh, bias=cols2[:, 0:1], scale=0.1)
                nc.scalar.activation(neg_f[:, qs(q)], psum[:, 2, C:2 * C], ACT.Identity, bias=cols2[:, 1:2],
                                     scale=-1.0)
                nc.scalar.activation(qT[:, qs(q)], psum[:, 3, 0:C], ACT.Identity, bias=cols[:, K_BQ:K_BQ + 1])
                nc.scalar.activation(kT[:, qs(q)], psum[:, 3, C:2 * C], ACT.Identity, bias=cols2[:, 2:3],
                                     scale=SCALE).then_inc(gates_read, 1)

            def sigmoid_o(q):
                act.wait_ge(vo_ok, q + 1)
                nc.scalar.activation(vo[:, q * PQ:(q + 1) * PQ, P:2 * P], vo[:, q * PQ:(q + 1) * PQ, P:2 * P],
                                     ACT.Sigmoid).then_inc(sig_ok, 1)

            def copy_score(q):
                act.wait_ge(score_ps, q + 1)
                if q >= 2:
                    act.wait_ge(level_s_ok, q - 1)
                nc.scalar.activation(score[:, q % 2, :].rearrange("p (h c) -> p h c", h=HALVES),
                                     psum[:, 5:7, 0:C], ACT.Copy).then_inc(score_ok, 1)

            for i in range(Q + 2):
                if i < Q:
                    copy_xT(2, i)
                if 0 <= i - 1 < Q:
                    gates(i - 1)
                if 0 <= i - 2 < Q:
                    sigmoid_o(i - 2)
                    if i - 2 < 2:
                        copy_score(i - 2)

            def softplus(q):
                act.wait_ge(absf_ok, q + 1)
                nc.scalar.activation(fs[:, qs(q)], fs[:, qs(q)], ACT.Exp).then_inc(a_order, 1)
                act.wait_ge(a_order, q + 1)
                nc.scalar.activation(fs[:, qs(q)], fs[:, qs(q)], ACT.Ln, bias=1.0).then_inc(softplus_ok, 1)

            def decays(q):
                act.wait_ge(expo_ok, q + 1)
                nc.scalar.activation(fs[:, qs(q)], phi[:, qs(q)], ACT.Exp)
                nc.scalar.activation(li[:, qs(q)], li[:, qs(q)], ACT.Exp).then_inc(decay_ok, 1)

            def copy_decays(q):
                act.wait_ge(decay_ps, q + 1)
                if q >= 2:
                    act.wait_ge(vi_ok, q - 1)
                nc.scalar.activation(phi_t[:, q, :], psum[:, 4, 0:C], ACT.Copy)
                nc.scalar.activation(iota_t[:, q % 2, :], psum[:, 4, C:2 * C], ACT.Copy).then_inc(decay_t, 1)

            for i in range(Q + 2):
                if i < Q:
                    softplus(i)
                if 0 <= i - 1 < Q:
                    decays(i - 1)
                if 0 <= i - 2 < Q:
                    copy_decays(i - 2)
            for q in range(Q):
                if q >= 2:
                    copy_score(q)
                for n in range(4):
                    k = 4 * q + n
                    act.wait_ge(arg_ps, k + 1)
                    if q >= 2:
                        act.wait_ge(u_read, 4 * (q - 2) + n + 1)
                    wide = min(2, LEVELS - 2 * n)
                    nc.scalar.activation(G[:, q % 2, 2 * n:2 * n + wide, :].rearrange("p n c -> p (n c)"),
                                         psum[:, k % 2, 0:wide * C], ACT.Exp).then_inc(G_ok, 1)

            def relu_first(q):
                act.wait_ge(f0_ps, q + 1)
                if q == 0:
                    act.wait_ge(u_read, 4 * Q)
                if q >= 2:
                    act.wait_ge(fl_ps, 2 * (q - 2) + 1)
                nc.scalar.activation(f0[:, q % 2, :].rearrange("p (h c) -> p h c", h=HALVES),
                                     psum[:, 2:4, 0:C], ACT.Relu, bias=hidw[:, W_BI:W_BI + 1]).then_inc(f0_ok, 1)

            def relu_layer(n, q):
                k = L1 * q + n
                act.wait_ge(fl_biased, k + 1)
                if n == 0 and q >= 2:
                    act.wait_ge(fl_ps, L1 * (q - 2) + 2)
                if n == 1 and q >= 2:
                    act.wait_ge(fo_ps, q - 1)
                nc.scalar.activation((f1, f2)[n][:, q % 2, :], fb[:, n, :], ACT.Relu).then_inc(fl_ok, 1)

            for q in range(Q):
                copy_xT(3, q)
                relu_first(q)
                relu_layer(0, q)
                relu_layer(1, q)

        @block.tensor
        def _(pe):
            def transpose_x(n, q):
                k = n * Q + q
                pe.wait_ge(ln_out, k + 1)
                if k >= 2:
                    pe.wait_ge(xT_ok, k - 1)
                for b in range(PQ):
                    last = nc.tensor.transpose(psum[:, q % 2, b * P:(b + 1) * P],
                                               xn[:, q * C + b * P:q * C + (b + 1) * P], ident)
                last.then_inc(xT_ps, 1)

            pe.wait_ge(consts_in, 16)
            pe.wait_ge(small_in, 48)
            for n in range(HALVES):
                last = nc.tensor.matmul(psum[n * D:(n + 1) * D, 7, 0:D], wqk[:, 0, :], wqk[:, 1, :],
                                        start=True, stop=True)
            last.then_inc(score_w_ps, 1)

            def project(q):
                pe.wait_ge(xT_ok, q + 1)
                if q >= 1:
                    pe.wait_ge(z_ok, q)
                nc.tensor.matmul(psum[:, 2, 0:C], score_w[:, :], xT[:, qs(q)], start=True, stop=True).then_inc(z_ps, 1)

            def scores(q):
                pe.wait_ge(z_ok, q + 1)
                if q >= 1:
                    pe.wait_ge(s_masked, q)
                for n in range(HALVES):
                    part = slice(n * D, (n + 1) * D)
                    for b in range(PQ):
                        at = slice(q * C + b * P, q * C + (b + 1) * P)
                        last = nc.tensor.matmul(psum[:, 5 + n, b * P:(b + 1) * P], xT[part, at], zT[part, at],
                                                start=True, stop=True)
                last.then_inc(s_ps, 1)
                if q >= 2:
                    pe.wait_ge(vs_ok, q - 1)
                for b in range(PQ):
                    last = nc.tensor.matmul(psum[:, 3 + q % 2, b * P:(b + 1) * P],
                                            xT[:, q * C + b * P:q * C + (b + 1) * P], diag[:, M_V0, :],
                                            start=True, stop=True)
                last.then_inc(v_ps, 1)

            def attend(q):
                pe.wait_ge(prob_ok, q + 1)
                pe.wait_ge(vs_ok, q + 1)
                if q >= 1:
                    pe.wait_ge(av_added, q)
                for b in range(PQ):
                    for n in range(HALVES):
                        at = slice(b * P + n * D, b * P + (n + 1) * D)
                        last = nc.tensor.matmul(psum[:, 7, at], prob[:, q % 2, n * PQ + b, :],
                                                vs[:, q % 2, at], start=True, stop=True)
                last.then_inc(av_ps, 1)

            pe.wait_ge(score_w_ok, 2)
            pe.wait_ge(diag_in, 16 * 6)
            for i in range(Q + 3):
                if i < Q:
                    transpose_x(0, i)
                if 0 <= i - 1 < Q:
                    project(i - 1)
                if 0 <= i - 2 < Q:
                    scores(i - 2)
                if 0 <= i - 3 < Q:
                    attend(i - 3)

            def router(q):
                pe.wait_ge(xT_ok, Q + q + 1)
                if q == 0:
                    pe.wait_ge(z_ok, Q)
                for b in range(PQ):
                    k = (q * PQ + b) * HALVES * E
                    last = nc.tensor.matmul(psum[:, 2, k:k + HALVES * E],
                                            xT[:, q * C + b * P:q * C + (b + 1) * P], router_w[:, :],
                                            start=True, stop=True)
                last.then_inc(logit_ps, 1)

            def up(q):
                if q == 0:
                    pe.wait_ge(first_in, 32)
                    pe.wait_ge(vs_ok, Q)
                    pe.wait_ge(s_masked, Q)
                for e in range(E):
                    k = q * E + e
                    pair = 3 + 2 * (k % 2)
                    if k >= 2:
                        pe.wait_ge(up_ok, k - 1)
                    for n in range(HALVES):
                        part = slice(n * D, (n + 1) * D)
                        last = nc.tensor.matmul(psum[:, pair + n, 0:C], first[part, e, :], xT[part, qs(q)],
                                                start=True, stop=True)
                    last.then_inc(up_ps, 1)

            def down(q):
                pe.wait_ge(up_ok, E * (q + 1))
                for j in range(BQ):
                    b, n = j // HALVES, j % HALVES
                    k = q * BQ + j
                    bank = (7, 2)[k % 2]
                    if k == 0:
                        pe.wait_ge(av_added, Q)
                        pe.wait_ge(hid_in, 16)
                    if k == 1:
                        pe.wait_ge(logit_off, 1)
                    if k >= 2:
                        pe.wait_ge(down_ok, k - 1)
                    nc.tensor.matmul(psum[:, bank, :], ones[:, :], b2[:, :], start=True, stop=False,
                                     skip_group_check=True)
                    for e in range(E):
                        last = nc.tensor.matmul(psum[:, bank, e * D:(e + 1) * D],
                                                hid[:, q % 2, e, n, b * P:(b + 1) * P],
                                                hidw[:, W_W2 + e * D:W_W2 + (e + 1) * D],
                                                start=False, stop=e == E - 1, skip_group_check=True)
                    last.then_inc(down_ps, 1)

            for i in range(Q + 1):
                if i < Q:
                    transpose_x(1, i)
                if i >= 1:
                    router(i - 1)
            for i in range(Q + 1):
                if i < Q:
                    up(i)
                if i >= 1:
                    down(i - 1)

            def gates(q):
                pe.wait_ge(xT_ok, 2 * Q + q + 1)
                if q == 0:
                    pe.wait_ge(down_ok, B)
                    pe.wait_ge(up_ok, Q * E)
                else:
                    pe.wait_ge(gates_read, q)
                    pe.wait_ge(vo_ok, q)
                for k, (bank, at) in zip((M_I, M_F, M_Q, M_K), ((2, 0), (2, C), (3, 0), (3, C))):
                    last = nc.tensor.matmul(psum[:, bank, at:at + C], diag[:, k, :], xT[:, qs(q)],
                                            start=True, stop=True)
                last.then_inc(gates_ps, 1)
                for b in range(PQ):
                    last = nc.tensor.matmul(psum[:, 7, b * 2 * P:(b + 1) * 2 * P],
                                            xT[:, q * C + b * P:q * C + (b + 1) * P],
                                            diag[:, M_V:M_O + 1, :].rearrange("p m c -> p (m c)"),
                                            start=True, stop=True)
                last.then_inc(vo_ps, 1)

            def score(q):
                pe.wait_ge(gates_read, q + 1)
                if q >= 1:
                    pe.wait_ge(score_ok, q)
                for n in range(HALVES):
                    part = slice(n * D, (n + 1) * D)
                    for b in range(PQ):
                        at = slice(q * C + b * P, q * C + (b + 1) * P)
                        last = nc.tensor.matmul(psum[:, 5 + n, b * P:(b + 1) * P], kT[part, at], qT[part, at],
                                                start=True, stop=True)
                last.then_inc(score_ps, 1)

            def decays(q):
                pe.wait_ge(decay_ok, q + 1)
                if q >= 1:
                    pe.wait_ge(decay_t, q)
                for k, src in enumerate((phi, li)):
                    for b in range(PQ):
                        last = nc.tensor.transpose(psum[:, 4, k * C + b * P:k * C + (b + 1) * P],
                                                   src[:, q * C + b * P:q * C + (b + 1) * P], ident)
                last.then_inc(decay_ps, 1)

            def normaliser(q):
                pe.wait_ge(nq_ok, q + 1)
                if q == 0:
                    pe.wait_ge(vo_ok, Q)
                for b in range(PQ):
                    k = q * BQ + b * HALVES
                    last = nc.tensor.matmul(psum[:, 7, k:k + HALVES],
                                            neg_f[:, q * C + b * P:q * C + (b + 1) * P],
                                            consts[:, C_HALF:C_HALF + HALVES], start=True, stop=True)
                last.then_inc(den_ps, 1)

            for i in range(Q + 2):
                if i < Q:
                    transpose_x(2, i)
                if 0 <= i - 1 < Q:
                    gates(i - 1)
                if 0 <= i - 2 < 2:
                    score(i - 2)
            for q in range(Q):
                decays(q)
            for q in range(Q):
                normaliser(q)

            def arguments(q, n):
                k = 4 * q + n
                if q == 0 and n == 0:
                    pe.wait_ge(decay_t, Q)
                    pe.wait_ge(xT_ok, 3 * Q)
                if k >= 2:
                    pe.wait_ge(G_ok, k - 1)
                for j in range(min(2, LEVELS - 2 * n)):
                    at = C_SUM + (2 * n + j) * P
                    last = nc.tensor.matmul(psum[:, k % 2, j * C:(j + 1) * C], consts[:, at:at + P],
                                            phi_t[:, q, :], start=True, stop=True)
                last.then_inc(arg_ps, 1)

            def recall(q, n):
                k = 4 * q + n
                if n == 0:
                    pe.wait_ge(level_s_ok, q + 1)
                pe.wait_ge(vg_ok, k + 1)
                if k >= 2:
                    pe.wait_ge(u_read, k - 1)
                for j in range(2):
                    lv = 2 * n + j
                    for b in range(PQ):
                        for s in range(HALVES):
                            at = slice(b * P + s * D, b * P + (s + 1) * D)
                            rhs = (vg[:, k % 4, j, at] if lv < LEVELS else
                                   vo[:, q * PQ + b, s * D:(s + 1) * D])
                            w = (s * PQ + b) * P
                            last = nc.tensor.matmul(psum[:, 2 + k % 2, j * C + b * P + s * D:
                                                         j * C + b * P + (s + 1) * D],
                                                    level_s[:, q % 2, lv, w:w + P], rhs, start=True, stop=True)
                last.then_inc(u_ps, 1)

            for i in range(Q + 1):
                for n in range(4):
                    if i < Q:
                        arguments(i, n)
                    if i >= 1:
                        recall(i - 1, n)
                if i < 2:
                    score(i + 2)

            def feed_first(q):
                pe.wait_ge(xT_ok, 3 * Q + q + 1)
                if q == 0:
                    pe.wait_ge(u_read, 4 * Q)
                else:
                    pe.wait_ge(f0_ok, q)
                for n in range(HALVES):
                    part = slice(n * D, (n + 1) * D)
                    last = nc.tensor.matmul(psum[:, 2 + n, 0:C], first[part, E, :], xT[part, qs(q)],
                                            start=True, stop=True)
                last.then_inc(f0_ps, 1)

            def feed_layer(n, q):
                k = L1 * q + n
                if k == 0:
                    pe.wait_ge(decay_t, Q)
                if q == 0 and n == 1:
                    pe.wait_ge(score_ok, Q)
                pe.wait_ge(slot_ok, L1 * GQ * (q + 1))
                if k >= 2:
                    pe.wait_ge(fl_biased, k - 1)
                if n == 0:
                    pe.wait_ge(f0_ok, q + 1)
                else:
                    pe.wait_ge(fl_ok, k)
                src = (f0, f1)[n]
                for g in range(GQ):
                    w = ((q % 2 * L1 + n) * GQ + g) * SLOT
                    last = nc.tensor.matmul(psum[:, 4 + n, g * GT:(g + 1) * GT], slots[:, w:w + HID],
                                            src[:, q % 2, g * GT:(g + 1) * GT], start=True, stop=True)
                last.then_inc(fl_ps, 1)

            def feed_last(q):
                pe.wait_ge(fl_ok, L1 * q + 2)
                if q == 0:
                    pe.wait_ge(score_ok, Q)
                else:
                    pe.wait_ge(out_ok, q)
                for b in range(PQ):
                    for n in range(HALVES):
                        at = b * P + n * D
                        last = nc.tensor.matmul(psum[:, 6, at:at + D], f2[:, q % 2, n * C + b * P:n * C + (b + 1) * P],
                                                hidw[:, W_WO:W_WO + D], start=True, stop=True)
                last.then_inc(fo_ps, 1)

            for q in range(Q):
                transpose_x(3, q)
                feed_first(q)
                feed_layer(0, q)
                feed_layer(1, q)
                feed_last(q)

        @block.vector
        def _(dve):
            count = [0]

            def link(ins):
                count[0] += 1
                ins.then_inc(v_order, 1)
                dve.wait_ge(v_order, count[0])

            nc.vector.memset(diag[:, :, :], 0.0).then_inc(zeroed, 1)
            nc.vector.memset(router_w[:, :], 0.0).then_inc(zeroed, 1)
            nc.vector.memset(score_w[:, :], 0.0).then_inc(score_w_ok, 1)
            nc.vector.memset(ones[:, :], 1.0)
            nc.vector.memset(m[:, :, 0:1], 0.0)
            link(nc.vector.memset(G[:, :, LEVELS:LEVELS + 1, :], 1.0))
            dve.wait_ge(score_w_ps, 1)
            dve.wait_ge(score_w_ok, 1)
            nc.vector.tensor_copy(score_w[0:D, 0:D], psum[0:D, 7, 0:D])
            nc.vector.tensor_copy(score_w[D:P, D:P], psum[D:P, 7, 0:D]).then_inc(score_w_ok, 1)
            dve.wait_ge(small_in, 48)
            dve.wait_ge(diag_in, 16 * 6)
            for n in range(2):
                for s in range(HALVES):
                    nc.vector.tensor_copy(gate_bias[:, (n * HALVES + s) * D:(n * HALVES + s + 1) * D],
                                          rows[:, R_BV + n * D:R_BV + (n + 1) * D])
            link(nc.vector.tensor_tensor(cols2[:, 0:1], cols[:, K_BGI:K_BGI + 1], cols[:, K_IB:K_IB + 1], ALU.add))
            link(nc.vector.tensor_scalar(cols2[:, 0:1], cols2[:, 0:1], 0.1, None, ALU.mult))
            nc.vector.tensor_scalar(cols2[:, 1:2], cols[:, K_BGF:K_BGF + 1], -1.0, None, ALU.mult)
            nc.vector.tensor_scalar(cols2[:, 2:3], cols[:, K_BK:K_BK + 1], SCALE, None, ALU.mult).then_inc(setup_ok, 1)

            def stats(n, q):
                for b in range(q * BQ, (q + 1) * BQ):
                    last = nc.vector.bn_stats(bn[:, b, :], h[:, b * D:(b + 1) * D])
                link(last)
                for b in range(q * BQ, (q + 1) * BQ):
                    last = nc.vector.bn_aggr(mv[:, n, b, :], bn[:, b, :])
                last.then_inc(ln_stats, 1)

            def normalise(n, q):
                dve.wait_ge(ln_rstd, n * Q + q + 1)
                for b in range(q * BQ, (q + 1) * BQ):
                    last = nc.vector.tensor_scalar(xn[:, b * D:(b + 1) * D], h[:, b * D:(b + 1) * D],
                                                   mv[:, n, b, 0:1], rstd[:, n, b:b + 1], ALU.subtract, ALU.mult)
                last.then_inc(ln_out, 1)

            def embed(q):
                dve.wait_ge(embed_in[q], 16 * BQ)
                link(nc.vector.tensor_tensor(h[:, qs(q)].rearrange("p (b d) -> p b d", b=BQ),
                                             h[:, qs(q)].rearrange("p (b d) -> p b d", b=BQ),
                                             repeated(consts[:, C_POS:C_POS + D], BQ, D), ALU.add))
                stats(0, q)

            def softmax_bias(q):
                dve.wait_ge(s_ps, q + 1)
                if q >= 2:
                    dve.wait_ge(prob_ok, q - 1)
                nc.vector.tensor_tensor(sc[:, q % 2, :, :].rearrange("p (h b) t -> p h b t", h=HALVES),
                                        psum[:, 5:7, 0:C].rearrange("p h (b t) -> p h b t", b=PQ),
                                        consts[:, C_CAUSAL:C_CAUSAL + P].unsqueeze(1).unsqueeze(1)
                                        .to_broadcast([P, HALVES, PQ, P]), ALU.subtract).then_inc(s_masked, 1)
                dve.wait_ge(s_masked, q + 1)
                seqs = slice(q * BQ, (q + 1) * BQ)
                link(nc.vector.tensor_reduce(nmax[:, seqs], sc[:, q % 2, :, :], AX.X, ALU.max, negate=True))
                nc.vector.tensor_scalar(nbias[:, seqs], nmax[:, seqs], SCALE, None, ALU.mult).then_inc(s_bias, 1)

            def scale_v(q):
                seqs = slice(q * BQ, (q + 1) * BQ)
                dve.wait_ge(prob_ok, q + 1)
                link(nc.vector.reciprocal(rsum[:, seqs], psums[:, seqs]))
                dve.wait_ge(v_ps, q + 1)
                if q >= 2:
                    dve.wait_ge(av_ps, q - 1)
                nc.vector.tensor_tensor(
                    vs[:, q % 2, :].rearrange("p (b h d) -> p b h d", b=PQ, h=HALVES),
                    psum[:, 3 + q % 2, 0:C].rearrange("p (b h d) -> p b h d", b=PQ, h=HALVES),
                    rsum[:, seqs].rearrange("p (h b) -> p b h", h=HALVES).unsqueeze(3)
                    .to_broadcast([P, PQ, HALVES, D]), ALU.mult).then_inc(vs_ok, 1)

            def add_attention(q):
                dve.wait_ge(av_ps, q + 1)
                nc.vector.tensor_tensor(h[:, qs(q)], psum[:, 7, 0:C], h[:, qs(q)], ALU.add).then_inc(av_added, 1)
                dve.wait_ge(av_added, q + 1)
                stats(1, q)

            dve.wait_ge(consts_in, 16)
            for i in range(Q + 4):
                if i < Q:
                    embed(i)
                if 0 <= i - 1 < Q:
                    normalise(0, i - 1)
                if 0 <= i - 3 < Q:
                    softmax_bias(i - 3)
                if 0 <= i - 4 < Q:
                    scale_v(i - 4)
                    add_attention(i - 4)
                if 0 <= i - 5 < Q:
                    normalise(1, i - 5)
            normalise(1, Q - 1)

            dve.wait_ge(logit_ps, Q)
            link(nc.vector.tensor_tensor(logit[:, :, :], psum[:, 2, 0:B * E].rearrange("p (b e) -> p b e", b=B),
                                         repeated(rows[:, R_BR:R_BR + E], B, E), ALU.add))
            link(nc.vector.tensor_reduce(lmax[:, :], logit[:, :, :], AX.X, ALU.max))
            nc.vector.tensor_tensor(rank[:, :, :], logit[:, :, :], per_seq(lmax[:, :], B, E),
                                    ALU.subtract).then_inc(logit_off, 1)
            link(nc.vector.tensor_tensor(ge[:, :, :, :], repeated3(logit), repeated4(logit), ALU.is_ge))
            link(nc.vector.tensor_tensor(
                ge[:, :, :, :].rearrange("p b e j -> p b (e j)"), ge[:, :, :, :].rearrange("p b e j -> p b (e j)"),
                repeated(consts[:, C_TIE:C_TIE + E * E], B, E * E), ALU.mult))
            nc.vector.tensor_reduce(sel[:, :, :], ge[:, :, :, :], AX.X, ALU.add)
            link(nc.vector.tensor_reduce(wfull[:, :, :], ge[:, :, :, :].rearrange("p b e j -> p b j e"), AX.X, ALU.add))
            link(nc.vector.tensor_tensor(sel[:, :, :], sel[:, :, :], wfull[:, :, :], ALU.subtract))
            link(nc.vector.tensor_tensor(sel[:, :, :], sel[:, :, :],
                                         repeated(consts[:, C_RANK:C_RANK + E], B, E), ALU.is_lt))
            dve.wait_ge(logit_exp, 1)
            link(nc.vector.tensor_tensor(sel[:, :, :], sel[:, :, :], lexp[:, :, :], ALU.mult))
            link(nc.vector.tensor_reduce(lsum[:, :], sel[:, :, :], AX.X, ALU.add))
            link(nc.vector.reciprocal(lmax[:, :], lsum[:, :]))
            link(nc.vector.tensor_tensor(wfull[:, :, :], sel[:, :, :], per_seq(lmax[:, :], B, E), ALU.mult))

            def combine(k):
                dve.wait_ge(down_ps, k + 1)
                bank = (7, 2)[k % 2]
                nc.vector.tensor_tensor(ye[:, k % 2, :].rearrange("p (e d) -> p e d", e=E),
                                        psum[:, bank, :].rearrange("p (e d) -> p e d", e=E),
                                        per_seq(wfull[:, k, :], E, D), ALU.mult).then_inc(down_ok, 1)
                dve.wait_ge(down_ok, k + 1)
                link(nc.vector.tensor_reduce(ysum[:, k % 2, :], ye[:, k % 2, :].rearrange("p (e d) -> p d e", e=E),
                                             AX.X, ALU.add))
                link(nc.vector.tensor_tensor(h[:, k * D:(k + 1) * D], h[:, k * D:(k + 1) * D], ysum[:, k % 2, :],
                                             ALU.add))

            for i in range(Q + 1):
                if i < Q:
                    for j in range(BQ):
                        combine(i * BQ + j)
                    stats(2, i)
                if i >= 1:
                    normalise(2, i - 1)

            def add_vo_bias(q):
                dve.wait_ge(vo_ps, q + 1)
                nc.vector.tensor_tensor(vo[:, q * PQ:(q + 1) * PQ, :],
                                        psum[:, 7, :].rearrange("p (b c) -> p b c", b=PQ),
                                        repeated(gate_bias[:, :], PQ, 2 * HALVES * D), ALU.add).then_inc(vo_ok, 1)

            def abs_f(q):
                dve.wait_ge(gates_read, q + 1)
                nc.vector.tensor_scalar(li[:, qs(q)], li[:, qs(q)], 10.0, None, ALU.mult)
                nc.vector.scalar_tensor_tensor(fs[:, qs(q)], neg_f[:, qs(q)], -1.0, neg_f[:, qs(q)], ALU.mult,
                                               ALU.min).then_inc(absf_ok, 1)

            def stabiliser(q):
                dve.wait_ge(softplus_ok, q + 1)
                link(nc.vector.scalar_tensor_tensor(neg_f[:, qs(q)], neg_f[:, qs(q)], 0.0, fs[:, qs(q)],
                                                    ALU.min, ALU.subtract))
                for b in range(q * PQ, (q + 1) * PQ):
                    at = slice(b * P, (b + 1) * P)
                    last = nc.vector.tensor_tensor_scan(m[:, b, 1:P + 1], neg_f[:, at], li[:, at], 0.0, ALU.add, ALU.max)
                link(last)
                pairs = slice(q * PQ, (q + 1) * PQ)

                def two(tile):
                    return tile[:, qs(q)].rearrange("p (b t) -> p b t", b=PQ)

                link(nc.vector.tensor_tensor(two(phi), two(neg_f), m[:, pairs, 0:P], ALU.add))
                nc.vector.tensor_tensor(two(phi), two(phi), m[:, pairs, 1:P + 1], ALU.subtract)
                nc.vector.tensor_tensor(two(li), two(li), m[:, pairs, 1:P + 1], ALU.subtract).then_inc(expo_ok, 1)

            def normaliser(q):
                dve.wait_ge(decay_ok, q + 1)
                link(nc.vector.tensor_tensor(neg_f[:, qs(q)], li[:, qs(q)], kT[:, qs(q)], ALU.mult))
                for b in range(q * PQ, (q + 1) * PQ):
                    at = slice(b * P, (b + 1) * P)
                    last = nc.vector.tensor_tensor_scan(neg_f[:, at], fs[:, at], neg_f[:, at], 0.0, ALU.mult, ALU.add)
                link(last)
                nc.vector.tensor_tensor(neg_f[:, qs(q)], neg_f[:, qs(q)], qT[:, qs(q)], ALU.mult).then_inc(nq_ok, 1)

            def weigh_v(q):
                dve.wait_ge(decay_t, q + 1)
                nc.vector.tensor_tensor(vo[:, q * PQ:(q + 1) * PQ, 0:P],
                                        vo[:, q * PQ:(q + 1) * PQ, 0:P],
                                        iota_t[:, q % 2, :].rearrange("p (b c) -> p b c", b=PQ),
                                        ALU.mult).then_inc(vi_ok, 1)

            for i in range(Q + 1):
                if i < Q:
                    add_vo_bias(i)
                    abs_f(i)
            for i in range(Q + 2):
                if i < Q:
                    stabiliser(i)
                if 0 <= i - 1 < Q:
                    normaliser(i - 1)
                if 0 <= i - 2 < Q:
                    weigh_v(i - 2)
            dve.wait_ge(vi_ok, Q)
            dve.wait_ge(den_ps, Q)
            link(nc.vector.tensor_copy(rden[:, :], psum[:, 7, 0:B]))
            link(nc.vector.scalar_tensor_tensor(rden[:, :], rden[:, :], -1.0, rden[:, :], ALU.mult, ALU.max))
            link(nc.vector.tensor_scalar(rden[:, :], rden[:, :], 1e-6, None, ALU.max))
            link(nc.vector.reciprocal(rden[:, :], rden[:, :]))
            dve.wait_ge(sig_ok, Q)

            def level_v(q, n):
                k = 4 * q + n
                dve.wait_ge(G_ok, k + 1)
                if k >= 4:
                    dve.wait_ge(u_ps, k - 3)
                wide = min(2, LEVELS - 2 * n)
                nc.vector.tensor_tensor(
                    vg[:, k % 4, 0:wide, :].rearrange("p n (b c) -> p n b c", b=PQ),
                    G[:, q % 2, 2 * n:2 * n + wide, :].rearrange("p n (b c) -> p n b c", b=PQ),
                    vo[:, q * PQ:(q + 1) * PQ, 0:P].unsqueeze(1).to_broadcast([P, wide, PQ, P]),
                    ALU.mult).then_inc(vg_ok, 1)

            def level_u(q, n):
                k = 4 * q + n
                dve.wait_ge(u_ps, k + 1)
                nc.vector.tensor_tensor(ug[:, 2 * n:2 * n + 2, :].rearrange("p n c -> p (n c)"),
                                        psum[:, 2 + k % 2, :],
                                        G[:, q % 2, 2 * n:2 * n + 2, :].rearrange("p n c -> p (n c)"),
                                        ALU.mult).then_inc(u_read, 1)

            def gate_out(q):
                seqs = slice(q * BQ, (q + 1) * BQ)
                dve.wait_ge(u_read, 4 * q + 4)
                link(nc.vector.tensor_reduce(acc[:, :], ug[:, :, :].rearrange("p n c -> p c n"), AX.X, ALU.add))
                a3 = acc[:, :].rearrange("p (b c) -> p b c", b=PQ)
                link(nc.vector.tensor_tensor(a3, a3, vo[:, q * PQ:(q + 1) * PQ, P:2 * P], ALU.mult))
                link(nc.vector.tensor_tensor(gated[:, q % 2, :].rearrange("p (b d) -> p b d", b=BQ),
                                             acc[:, :].rearrange("p (b d) -> p b d", b=BQ),
                                             per_seq(rden[:, seqs]), ALU.mult))
                link(nc.vector.tensor_tensor(sq[:, :], gated[:, q % 2, :], gated[:, q % 2, :], ALU.mult))
                nc.vector.tensor_reduce(var[:, 3, seqs], sq[:, :].rearrange("p (b d) -> p b d", b=BQ), AX.X,
                                        ALU.add).then_inc(ms_ok, 1)

            def add_recurrence(q):
                seqs = slice(q * BQ, (q + 1) * BQ)
                g3 = gated[:, q % 2, :].rearrange("p (b d) -> p b d", b=BQ)
                dve.wait_ge(rms_ok, q + 1)
                link(nc.vector.tensor_tensor(g3, g3, per_seq(rstd[:, 4, seqs]), ALU.mult))
                link(nc.vector.tensor_tensor(g3, g3, repeated(rows[:, R_NS:R_NS + D], BQ, D), ALU.mult))
                link(nc.vector.tensor_tensor(h[:, qs(q)], h[:, qs(q)], gated[:, q % 2, :], ALU.add))
                stats(3, q)

            for i in range(Q + 2):
                for n in range(4):
                    if i < Q:
                        level_v(i, n)
                    if 1 <= i <= Q:
                        level_u(i - 1, n)
                if 1 <= i <= Q:
                    gate_out(i - 1)
                if 2 <= i:
                    add_recurrence(i - 2)

            for q in range(Q):
                normalise(3, q)
                dve.wait_ge(ln_out, 3 * Q + q + 1)
                nc.vector.tensor_tensor(h[:, qs(q)].rearrange("p (b d) -> p b d", b=BQ),
                                        h[:, qs(q)].rearrange("p (b d) -> p b d", b=BQ),
                                        repeated(rows[:, R_BO:R_BO + D], BQ, D), ALU.add).then_inc(v_order, 1)
            count[0] += Q
            dve.wait_ge(v_order, count[0])
            for q in range(Q):
                for n in range(L1):
                    k = L1 * q + n
                    dve.wait_ge(fl_ps, k + 1)
                    if k >= 2:
                        dve.wait_ge(fl_ok, k - 1)
                    at = (q % 2 * L1 + n) * GQ * SLOT
                    bias = slots[:, at:at + GQ * SLOT].rearrange("p (g c) -> p g c", g=GQ)[:, :, HID:SLOT]
                    nc.vector.tensor_tensor(fb[:, n, :].rearrange("p (g t) -> p g t", g=GQ),
                                            psum[:, 4 + n, :].rearrange("p (g t) -> p g t", g=GQ),
                                            bias.to_broadcast([P, GQ, GT]), ALU.add).then_inc(fl_biased, 1)
                dve.wait_ge(fo_ps, q + 1)
                nc.vector.tensor_tensor(outs[:, qs(q)], psum[:, 6, 0:C], h[:, qs(q)], ALU.add).then_inc(out_ok, 1)


def repeated3(logit):
    return logit[:, :, :].unsqueeze(2).to_broadcast([P, B, E, E])


def repeated4(logit):
    return logit[:, :, :].unsqueeze(3).to_broadcast([P, B, E, E])


def kernel(**inputs):
    import concourse.bacc as bacc
    from concourse.bass_utils import run_bass_kernel_spmd

    a = {k: np.asarray(v) for k, v in inputs.items()}
    wg, bg = a["L1_attn_Wg"], a["L1_attn_bg"]
    arrays = {
        "table": a["L0_tok_W"],
        "tokens": a["x"].T,
        "route": a["L1_ffn_route_id"].reshape(Q, PQ, HALVES, P // GT).transpose(0, 2, 1, 3).reshape(1, GROUPS),
        "consts": shape_constants(),
        "wqk": np.stack([a["L0_attn_Wq"], a["L0_attn_Wk"]], 1),
        "diag": np.stack([a["L0_attn_Wv"].T, wg[:, D:2 * D], wg[:, 0:D], a["L1_attn_Wq"], a["L1_attn_Wk"],
                          a["L1_attn_Wv"], wg[:, 2 * D:]], 1),
        "wr": a["L0_ffn_Wr"],
        "first": np.concatenate([a["L0_ffn_W1"].transpose(1, 0, 2), a["L1_ffn_Wi"].T[:, None, :]], 1),
        "cols": np.stack([a["L0_ffn_gamma"], a["L0_ffn_beta"], bg[0:D], a["L1_attn_input_bias"], bg[D:2 * D],
                          a["L1_attn_bq"], a["L1_attn_bk"]], 1),
        "rows": np.concatenate([a["L0_ffn_br"], a["L1_attn_norm_scale"], a["L1_ffn_bo"], a["L1_attn_bv"],
                                bg[2 * D:]]),
        "hid": np.concatenate([a["L0_ffn_W2"].transpose(1, 0, 2).reshape(HID, E * D), a["L1_ffn_Wo"].T,
                               a["L0_ffn_b1"].T, a["L1_ffn_bi"][:, None]], 1),
        "b2": a["L0_ffn_b2"].reshape(1, E * D),
        "routed": np.concatenate([a["L1_ffn_Wr"].transpose(3, 0, 1, 2), a["L1_ffn_br"].transpose(2, 0, 1)[..., None]],
                                 3).reshape(HID, L1 * NE1 * SLOT),
        "shared": np.concatenate([a["L1_ffn_Ws"][:, 0].transpose(2, 0, 1), a["L1_ffn_bs"][:, 0].T[..., None]],
                                 2).reshape(HID, L1 * SLOT),
    }
    nc = bacc.Bacc("TRN2", target_bir_lowering=False, num_devices=1)
    feeds, args = {}, []
    for name, x in arrays.items():
        x = np.ascontiguousarray(x)
        feeds[f"in_{name}"] = x
        args.append(nc.dram_tensor(f"in_{name}", x.shape, mybir.dt.from_np(x.dtype), kind="ExternalInput").ap())
    out = nc.dram_tensor("out_0", (B, P, D), F32, kind="ExternalOutput").ap()
    tower(nc, *args, out)
    r = run_bass_kernel_spmd(nc, [feeds], core_ids=[0])
    return r.results[0]["out_0"]
```

```python
from contextlib import ExitStack

import numpy as np
import concourse.bass as bass
from concourse import mybir


P = 128
B = 16
D = 64
HALVES = 2
Q = 4
BQ = B // Q
PQ = BQ // HALVES
C = BQ * D
E = 8
HID = 128
NE1 = 16
L1 = 2
GROUPS = 64
GT = B * P // GROUPS
GQ = GROUPS // Q
STEP = 4
PARTS = 3
LEVELS = 7
EPS = 1e-5
SCALE = D ** -0.5
MASKED = 1e10

ALU = mybir.AluOpType
ACT = mybir.ActivationFunctionType
F32 = mybir.dt.float32
BF16 = mybir.dt.bfloat16
I32 = mybir.dt.int32
AX = mybir.AxisListType

C_ID = 0
C_CAUSAL = C_ID + P
C_TIE = C_CAUSAL + P
C_RANK = C_TIE + E * E
C_POS = C_RANK + E
C_HALF = C_POS + D
C_POW = C_HALF + HALVES
C_ROW = C_POW + BQ
C_SUM = C_ROW + 1
C_MASK = C_SUM + LEVELS * P
N_CONST = C_MASK + (LEVELS + 1) * P

U_BANKS = (2, 3, 4, 7)

(M_V0, M_F, M_I, M_Q, M_K, M_V, M_O) = range(7)
NM = 7
(K_GAMMA, K_BETA, K_BGI, K_IB, K_BGF, K_BQ, K_BK) = range(7)
NK = 7
R_BR = 0
R_NS = R_BR + E
R_BO = R_NS + D
R_BV = R_BO + D
R_BG = R_BV + D
NR = R_BG + D
W_WO = 0
W_B1 = W_WO + D
W_BI = W_B1 + E
NW = W_BI + 1


def shape_constants():
    c = np.zeros((P, N_CONST), np.float32)
    r = np.arange(P)[:, None]
    t = np.arange(P)[None, :]
    c[:, C_ID:C_ID + P] = r == t
    c[:, C_CAUSAL:C_CAUSAL + P] = np.where(t >= r, np.float32(MASKED), np.float32(0))
    for n in range(LEVELS):
        half = P >> (n + 1)
        mid = t // (2 * half) * (2 * half) + half
        left = t < mid
        span = np.where(left, (r > t) & (r < mid), (r >= mid) & (r <= t))
        c[:, C_SUM + n * P:C_SUM + (n + 1) * P] = span
        same = r // (2 * half) == t // (2 * half)
        c[:, C_MASK + n * P:C_MASK + (n + 1) * P] = same & (r % (2 * half) < half) & (t % (2 * half) >= half)
    c[:, C_MASK + LEVELS * P:C_MASK + (LEVELS + 1) * P] = r == t
    e = np.arange(E)
    c[:, C_TIE:C_TIE + E * E] = (e[None, :] < e[:, None]).astype(np.float32).reshape(1, E * E)
    c[:, C_RANK:C_RANK + E] = (e - (E - 1) + 2).astype(np.float32)[None, :]
    d = np.arange(D)
    freq = np.power(np.float32(10000.0), -((d - d % 2).astype(np.float32) / np.float32(D)))
    angle = np.arange(P, dtype=np.float32)[:, None] * freq[None, :]
    c[:, C_POS:C_POS + D] = np.where(d % 2 == 0, np.sin(angle), np.cos(angle))
    for h in range(HALVES):
        c[h * D:(h + 1) * D, C_HALF + h] = 1.0
    c[:, C_POW:C_POW + BQ] = -0.5
    row = np.arange(P)
    c[:, C_ROW] = np.where((row % 32 < NE1) & (row < 32 * PARTS), row % 32, -1)
    return c


def shape_constants_bf16():
    c = np.zeros((P, E + 1, P), np.float32)
    for e in range(E):
        for p in range(PARTS):
            c[p * E + e, e, :] = 1
    c[:, E, :] = np.eye(P)
    return c.reshape(P, (E + 1) * P).astype(mybir.dt.np(BF16))


def tower(nc, table, tokens, route, consts_d, pick_d, wqk_d, diag_d, wr_d, first_d, cols_d, rows_d, w2_d, hid_d, b2_d,
          routed_d, shared_d, bias_d, shared_bias_d, out):
    with ExitStack() as ctx:
        def sb(name, shape, dt=F32):
            return ctx.enter_context(nc.sbuf_tensor(name, shape, dt))

        def sem(name):
            return ctx.enter_context(nc.semaphore(name))

        psum = ctx.enter_context(nc.psum_tensor("psum", [P, 8, 512], F32))

        turned_w = psum[:, 1, :].bitcast(BF16)

        consts = sb("consts", [P, N_CONST])
        wqk = sb("wqk", [D, 2, D])
        diag = sb("diag", [P, NM, P])
        score_w = sb("score_w", [P, P])
        router_w = sb("router_w", [P, HALVES * E])
        wi = sb("wi", [P, HID])
        early = sb("early", [P, GQ * L1 * HID])
        taken = [0]

        def carve(n):
            taken[0] += n
            return early[:, taken[0] - n:taken[0]]

        first = carve(E * HID).rearrange("p (e c) -> p e c", e=E)
        w2 = carve(E * D)
        yT = carve(2 * C).rearrange("p (a c) -> p a c", a=2)
        wT_b = carve(2 * 512 // 2).bitcast(BF16).rearrange("p (a c) -> p a c", a=2)
        wT_f = carve(2 * P).rearrange("p (a c) -> p a c", a=2)
        b2 = carve(C)
        phi = carve(B * D)
        cols = sb("cols", [P, NK])
        cols2 = sb("cols2", [P, 3])
        rows = sb("rows", [P, NR])
        gate_bias = sb("gate_bias", [P, 2 * HALVES * D])
        hidw = sb("hidw", [P, NW])
        pick = sb("pick", [P, E + 1, P], BF16)
        ident_b = pick[:, E, :]
        routed = sb("routed", [P, NE1 * L1 * HID])
        shared = sb("shared", [P, L1 * HID])
        slots_a = sb("slots_a", [P, 2 * GQ * L1 * HID])
        bias_rows = sb("bias_rows", [P, L1 * HID])
        bias_sh = sb("bias_sh", [P, L1 * HID])
        bias_b = sb("bias_b", [P, L1 * HID], BF16)
        route_sb = sb("route_sb", [P, GROUPS], I32)
        route_f = sb("route_f", [P, GROUPS])
        one_hot = sb("one_hot", [P, B * P], BF16)
        tok_sb = sb("tok_sb", [P, B], I32)
        ident = consts[:, C_ID:C_ID + P]

        h = sb("h", [P, B * D])
        bn = sb("bn", [P, B, 6])
        mv = sb("mv", [P, 4, B, 2])
        var = sb("var", [P, 5, B])
        rstd = sb("rstd", [P, 5, B])
        norm = sb("norm", [P, 3, B * D])
        xn = norm[:, 0, :]
        xT = norm[:, 1, :]
        apart = sb("apart", [P, Q, HALVES, C])

        work = sb("work", [P, 5, B * D])
        sc = work[:, 1, :].rearrange("p (a b t) -> p a b t", a=2, b=BQ)
        prob = work[:, 2, :].rearrange("p (a b t) -> p a b t", a=2, b=BQ)
        nmax = sb("nmax", [P, B])
        nbias = sb("nbias", [P, B])
        psums = sb("psums", [P, B])
        rsum = sb("rsum", [P, B])
        vs = sb("vs", [P, 2, C])

        logit = sb("logit", [P, 2, BQ, E])
        ge = work[:, 3, 0:2 * BQ * E * E].rearrange("p (a b e j) -> p a b e j", a=2, b=BQ, e=E)
        sel = sb("sel", [P, 2, BQ, E])
        back = sb("back", [P, 2, BQ, E])
        lsum = sb("lsum", [P, 2, BQ])
        off = sb("off", [P, 2, BQ, E])
        wfull = sb("wfull", [P, 2, BQ, E])
        wrest = sb("wrest", [P, 2, BQ, E])
        wsplit = sb("wsplit", [P, 2, BQ, PARTS, E], BF16)
        hid = sb("hid", [P, 4, 512])

        qT = work[:, 0, :]
        kT = work[:, 4, :]
        li = work[:, 2, :]
        sp = work[:, 3, :]
        fs = work[:, 1, :]
        vo = sb("vo", [P, B // 2, 2 * HALVES * D])
        nm = sb("nm", [P, B // 2, P + 1])
        phi_t = sb("phi_t", [P, Q, C])
        iota_t = sb("iota_t", [P, 2, C])
        rden = sb("rden", [P, B])
        rden2 = sb("rden2", [P, B])
        factor = sb("factor", [P, B])
        score = sb("score", [P, 2, BQ * P])
        level_s = sb("level_s", [P, 2, LEVELS + 1, BQ * P])
        slots_b = level_s[:, 0, :, :].rearrange("p n t -> p (n t)")
        G = work[:, 0:4, :].rearrange("p (a n) (m c) -> p a (n m) c", a=2, c=C)
        vg = hid[:, :, :].rearrange("p k (m c) -> p k m c", m=2)
        ug = norm[:, 1:3, :].rearrange("p n (m c) -> p (n m) c", c=C)
        acc = sb("acc", [P, C])
        gated = sb("gated", [P, 2, C])
        sq = sb("sq", [P, C])

        feed = G[:, :, :, :].rearrange("p a n c -> p (a n c)").rearrange("p (f c) -> p f c", f=8)
        f0 = feed[:, 0:2, :]
        token = feed[:, 2:4, :]
        f1 = feed[:, 4:6, :]
        f2 = feed[:, 6:8, :]
        outs = kT

        tok_in = sem("tok_in")
        consts_in = sem("consts_in")
        levels_in = sem("levels_in")
        small_in = sem("small_in")
        diag_in = sem("diag_in")
        first_in = sem("first_in")
        hid_in = sem("hid_in")
        route_in = sem("route_in")
        slots_in = sem("slots_in")
        embed_in = [sem(f"embed_in{q}") for q in range(Q)]
        out_done = sem("out_done")
        zeroed = sem("zeroed")
        score_w_ps = sem("score_w_ps")
        score_w_ok = sem("score_w_ok")
        setup_ok = sem("setup_ok")
        ln_stats = [sem(f"ln_stats{n}") for n in range(4)]
        ln_rstd = [sem(f"ln_rstd{n}") for n in range(4)]
        ln_out = [sem(f"ln_out{n}") for n in range(4)]
        xT_ps = [sem(f"xT_ps{n}") for n in range(4)]
        xT_ok = [sem(f"xT_ok{n}") for n in range(4)]
        z_ps = sem("z_ps")
        z_ok = sem("z_ok")
        pick_in = sem("pick_in")
        bias_in = sem("bias_in")
        hot_ok = sem("hot_ok")
        v_ps = sem("v_ps")
        s_ps = sem("s_ps")
        s_masked = sem("s_masked")
        s_bias = sem("s_bias")
        prob_ok = sem("prob_ok")
        vs_ok = sem("vs_ok")
        av_ps = sem("av_ps")
        av_added = sem("av_added")
        logit_ps = sem("logit_ps")
        logit_off = sem("logit_off")
        tanh_ok = sem("tanh_ok")
        weights_ok = sem("weights_ok")
        wT_ps = sem("wT_ps")
        wT_ok = sem("wT_ok")
        up_ps = sem("up_ps")
        up_ok = sem("up_ok")
        spread_ps = sem("spread_ps")
        weigh_ok = sem("weigh_ok")
        down_ps = sem("down_ps")
        yT_ok = sem("yT_ok")
        y_ps = sem("y_ps")
        y_added = sem("y_added")
        gates_ps = sem("gates_ps")
        gates_read = sem("gates_read")
        vo_ps = sem("vo_ps")
        vo_ok = sem("vo_ok")
        sig_ok = sem("sig_ok")
        q_ok = sem("q_ok")
        ln_f_ok = sem("ln_f_ok")
        expo_ok = sem("expo_ok")
        decay_ok = sem("decay_ok")
        nq_ok = sem("nq_ok")
        score_ps = sem("score_ps")
        score_ok = sem("score_ok")
        decay_ps = sem("decay_ps")
        decay_t = sem("decay_t")
        den_ps = sem("den_ps")
        vi_ok = sem("vi_ok")
        level_s_ok = sem("level_s_ok")
        arg_ps = sem("arg_ps")
        G_ok = sem("G_ok")
        vg_ok = sem("vg_ok")
        u_ps = sem("u_ps")
        u_read = sem("u_read")
        gated_ok = sem("gated_ok")
        rden_ok = sem("rden_ok")
        ms_ok = sem("ms_ok")
        rms_ok = sem("rms_ok")
        shared_ok = sem("shared_ok")
        slot_ok = [sem(f"slot_ok{q}") for q in range(Q)]
        f0_ps = sem("f0_ps")
        f0_ok = sem("f0_ok")
        layer_ps = [sem(f"layer_ps{n}") for n in range(L1)]
        token_ok = [sem(f"token_ok{n}") for n in range(L1)]
        turned_ps = [sem(f"turned_ps{n}") for n in range(L1)]
        turned_ok = [sem(f"turned_ok{n}") for n in range(L1)]
        fo_ps = sem("fo_ps")
        biased = sem("biased")
        out_ok = sem("out_ok")
        v_order = sem("v_order")
        g_order = sem("g_order")
        a_order = sem("a_order")

        def qs(q):
            return slice(q * C, (q + 1) * C)

        def slots_of(q):
            return ((slots_a, 0), (slots_a, GQ * L1 * HID), (slots_b, 0), (early, 0))[q]

        def per_seq(ap, n=BQ, k=D):
            return ap.unsqueeze(2).to_broadcast([P, n, k])

        def repeated(ap, n, k):
            return ap.unsqueeze(1).to_broadcast([P, n, k])

        block = ctx.enter_context(nc.Block())

        @block.sync
        def _(sp):
            sp.dma_start(tok_sb[:, :], tokens).then_inc(tok_in, 16)
            sp.dma_start(wqk[:, :, :], wqk_d).then_inc(small_in, 16)
            sp.dma_start(consts[:, 0:C_SUM], consts_d[:, 0:C_SUM]).then_inc(consts_in, 16)
            sp.dma_start(rows[:, :], rows_d.partition_broadcast(P)).then_inc(small_in, 16)
            sp.wait_ge(zeroed, 4)
            for n in range(HALVES):
                part = slice(n * D, (n + 1) * D)
                sp.dma_start(diag[part, :, part], diag_d).then_inc(diag_in, 16)
                sp.dma_start(router_w[part, n * E:(n + 1) * E], wr_d).then_inc(diag_in, 16)
                sp.dma_start(cols[part, :], cols_d).then_inc(diag_in, 16)
                sp.dma_start(first[part, :, :], first_d[:, 0:E]).then_inc(first_in, 16)
                sp.dma_start(wi[part, :], first_d[:, E]).then_inc(first_in, 16)
            sp.dma_start(w2, w2_d).then_inc(hid_in, 16)
            sp.dma_start(hidw[:, :], hid_d).then_inc(hid_in, 16)
            sp.dma_start(pick[:, :, :].rearrange("p e m -> p (e m)"), pick_d).then_inc(pick_in, 16)
            sp.wait_ge(embed_in[Q - 1], 16 * BQ)
            for n in range(BQ):
                sp.dma_start(b2[n * E:(n + 1) * E, n * D:(n + 1) * D], b2_d).then_inc(pick_in, 16)
            sp.dma_start(route_sb[:, :], route.partition_broadcast(P)).then_inc(route_in, 16)
            sp.dma_start(shared[:, :], shared_d).then_inc(slots_in, 16)
            sp.dma_start(routed[:, :], routed_d).then_inc(slots_in, 16)
            for n in range(PARTS):
                sp.dma_start(bias_rows[32 * n:32 * n + NE1, :], bias_d).then_inc(bias_in, 16)
            sp.dma_start(bias_sh[:, :], shared_bias_d.partition_broadcast(P)).then_inc(bias_in, 16)
            sp.dma_start(consts[:, C_SUM:], consts_d[:, C_SUM:]).then_inc(levels_in, 16)
            for q in range(Q):
                sp.wait_ge(out_ok, q + 1)
                sp.dma_start(out[q * BQ:(q + 1) * BQ].rearrange("b t d -> t b d"),
                             outs[:, qs(q)].rearrange("p (b d) -> p b d", b=BQ)).then_inc(out_done, 16)
            sp.wait_ge(out_done, 16 * Q)

        @block.gpsimd
        def _(gp):
            def power(n, q, scale, shift, src, wait, done):
                seqs = slice(q * BQ, (q + 1) * BQ)
                gp.wait_ge(*wait)
                nc.gpsimd.tensor_scalar(var[:, n, seqs], src, scale, shift, ALU.mult, ALU.add).then_inc(g_order, 1)
                count[0] += 1
                gp.wait_ge(g_order, count[0])
                nc.gpsimd.tensor_tensor(rstd[:, n, seqs], var[:, n, seqs], consts[:, C_POW:C_POW + BQ],
                                        ALU.pow).then_inc(done, 1)

            count = [0]

            def norm_power(n, q):
                scale, shift = (1.0 + EPS, EPS * EPS) if n == 1 else (1.0, EPS)
                power(n, q, scale, shift, mv[:, n, q * BQ:(q + 1) * BQ, 1], (ln_stats[n], q + 1), ln_rstd[n])

            def gather(q):
                for b in range(q * BQ, (q + 1) * BQ):
                    nc.gpsimd.indirect_dma_start(
                        out=h[:, b * D:(b + 1) * D], out_offset=None, in_=table,
                        in_offset=bass.IndirectOffsetOnAxis(ap=tok_sb[:, b:b + 1], axis=0),
                    ).then_inc(embed_in[q], 16)

            gp.wait_ge(tok_in, 16)
            gather(0)
            gather(1)
            gp.wait_ge(consts_in, 16)
            norm_power(0, 0)
            gather(2)
            norm_power(0, 1)
            gather(3)
            norm_power(0, 2)
            norm_power(1, 0)
            norm_power(0, 3)
            for q in range(1, Q):
                norm_power(1, q)
            gp.wait_ge(slots_in, 32)
            gp.wait_ge(route_in, 16)
            for n in range(L1):
                nc.gpsimd.tensor_tensor(shared[:, n * HID:(n + 1) * HID], shared[:, n * HID:(n + 1) * HID],
                                        ident, ALU.add).then_inc(shared_ok, 1)
            gp.wait_ge(shared_ok, L1)
            W = L1 * HID

            def merge(q, first_g=0, n_g=GQ):
                slots, at = slots_of(q)
                if q == 2:
                    gp.wait_ge(u_ps, 4 * (q + 1))
                if q == 3:
                    gp.wait_ge(decay_ps, Q)
                with gp.Fori(first_g // STEP, (first_g + n_g) // STEP) as g:
                    experts = [gp.value_load(route_sb[0:1, bass.ds(g * STEP + (q * GQ + k), 1)],
                                             min_val=0, max_val=NE1 - 1) for k in range(STEP)]
                    for k in range(STEP):
                        nc.gpsimd.tensor_tensor(slots[:, bass.ds(g * (STEP * W) + (at + k * W), W)],
                                                routed[:, bass.ds(experts[k] * W, W)], shared[:, :],
                                                ALU.add).then_inc(slot_ok[q], 1)

            merge(0)
            merge(1, 0, 4)
            norm_power(2, 0)
            merge(1, 4, 12)
            for q in range(1, Q):
                norm_power(2, q)

            def mask_levels(q):
                gp.wait_ge(score_ok, q + 1)
                if q >= 2:
                    gp.wait_ge(u_ps, 4 * (q - 1))
                for n in range(3, LEVELS + 1):
                    mask = consts[:, C_MASK + n * P:C_MASK + (n + 1) * P]
                    last = nc.gpsimd.tensor_tensor(
                        level_s[:, q % 2, n, :].rearrange("p (b t) -> p b t", b=BQ),
                        score[:, q % 2, :].rearrange("p (b t) -> p b t", b=BQ),
                        repeated(mask, BQ, P), ALU.mult)
                last.then_inc(level_s_ok, 1)

            def out_factor(q):
                seqs = slice(q * BQ, (q + 1) * BQ)
                gp.wait_ge(rden_ok, 1)
                gp.wait_ge(ms_ok, q + 1)
                nc.gpsimd.tensor_tensor(var[:, 3, seqs], var[:, 3, seqs], rden2[:, seqs], ALU.mult).then_inc(g_order, 1)
                count[0] += 1
                power(4, q, 1.0 / D, 1e-8, var[:, 3, seqs], (g_order, count[0]), g_order)
                count[0] += 1
                gp.wait_ge(g_order, count[0])
                nc.gpsimd.tensor_tensor(factor[:, seqs], rstd[:, 4, seqs], rden[:, seqs], ALU.mult).then_inc(rms_ok, 1)

            gp.wait_ge(levels_in, 16)
            mask_levels(0)
            mask_levels(1)
            merge(3)
            for i in range(Q):
                if 1 <= i < Q - 1:
                    mask_levels(i + 1)
                if i >= 1:
                    out_factor(i - 1)
                if i >= 2:
                    norm_power(3, i - 2)
            merge(2, 0, 8)
            out_factor(Q - 1)
            norm_power(3, Q - 2)
            norm_power(3, Q - 1)
            merge(2, 8, 8)

        @block.scalar
        def _(act):
            def copy_xT(n, q):
                act.wait_ge(xT_ps[n], q + 1)
                src = psum[:, q % 2, 0:C]
                if n == 3:
                    copy_apart(src, q, lambda o, i, part: nc.scalar.activation(o, i, ACT.Copy), xT_ok[3])
                elif n == 1:
                    def affine(o, i, part):
                        return nc.scalar.activation(o, i, ACT.Identity, bias=cols[part, K_BETA:K_BETA + 1],
                                                    scale=cols[part, K_GAMMA:K_GAMMA + 1])

                    affine(xT[:, qs(q)], src, slice(0, P))
                    copy_apart(src, q, affine, xT_ok[1])
                else:
                    nc.scalar.activation(xT[:, qs(q)], src, ACT.Copy).then_inc(xT_ok[n], 1)

            def copy_apart(src, q, copy, done):
                for n in range(HALVES):
                    part = slice(n * D, (n + 1) * D)
                    last = copy(apart[part, q, n, :], src[part], part)
                last.then_inc(done, 1)

            def copy_z(q):
                act.wait_ge(z_ps, q + 1)
                copy_apart(psum[:, 2, 0:C], q, lambda o, i, part: nc.scalar.activation(o, i, ACT.Copy), z_ok)

            def softmax_exp(q):
                act.wait_ge(s_bias, q + 1)
                if q >= 2:
                    act.wait_ge(av_ps, q - 1)
                for j in range(BQ):
                    k = q * BQ + j
                    last = nc.scalar.activation(prob[:, q % 2, j, :], sc[:, q % 2, j, :], ACT.Exp,
                                                bias=nbias[:, k:k + 1], scale=SCALE,
                                                accum_out=psums[:, k:k + 1])
                last.then_inc(prob_ok, 1)

            act.wait_ge(diag_in, 16 * 6)
            act.wait_ge(zeroed, 5)
            for i in range(Q + 1):
                if i < Q:
                    copy_xT(0, i)
                    copy_z(i)
                if i >= 1:
                    softmax_exp(i - 1)

            copy_xT(1, 0)

            def router_tanh(q):
                act.wait_ge(logit_off, q + 1)
                nc.scalar.activation(off[:, q % 2, :, :], off[:, q % 2, :, :], ACT.Tanh).then_inc(tanh_ok, 1)

            def copy_wT(q):
                act.wait_ge(wT_ps, q + 1)
                if q >= 2:
                    act.wait_ge(spread_ps, E * (q - 1))
                    act.wait_ge(y_ps, q - 1)
                nc.scalar.activation(wT_b[0:PARTS * E, q % 2, :], turned_w[0:PARTS * E, 0:512], ACT.Copy)
                nc.scalar.activation(wT_f[0:BQ * E, q % 2, :], psum[0:BQ * E, 1, C:C + P], ACT.Copy).then_inc(wT_ok, 1)

            def gelu(k):
                act.wait_ge(up_ps, k + 1)
                if k >= 4:
                    act.wait_ge(down_ps, k - 3)
                nc.scalar.activation(hid[:, k % 4, :], psum[:, 3 + k % 2, :], ACT.Gelu,
                                     bias=hidw[:, W_B1 + k % E:W_B1 + k % E + 1]).then_inc(up_ok, 1)

            def copy_yT(q):
                act.wait_ge(down_ps, E * (q + 1))
                if q >= 2:
                    act.wait_ge(y_ps, q - 1)
                nc.scalar.activation(yT[:, q % 2, :], psum[:, 7, 0:C], ACT.Copy).then_inc(yT_ok, 1)

            act.wait_ge(hid_in, 32)
            act.wait_ge(zeroed, 6)
            gelu(0)
            gelu(1)
            router_tanh(0)
            copy_wT(0)
            copy_xT(1, 1)
            for k in range(2, Q * E):
                q, e = k // E, k % E
                gelu(k)
                if e == 1:
                    copy_wT(q)
                    if q + 1 < Q:
                        copy_xT(1, q + 1)
                if e == 3 and q >= 1:
                    copy_yT(q - 1)
                if e == 7 and q + 1 < Q:
                    router_tanh(q + 1)
            copy_yT(Q - 1)

            act.wait_ge(setup_ok, 1)

            def gates(q):
                act.wait_ge(gates_ps, q + 1)
                nc.scalar.activation(li[:, qs(q)], psum[:, 2 + q % 2 * 3, 0:C], ACT.Tanh, bias=cols2[:, 0:1],
                                     scale=0.1)
                nc.scalar.activation(sp[:, qs(q)], psum[:, 2 + q % 2 * 3, C:2 * C], ACT.Relu,
                                     bias=cols[:, K_BGF:K_BGF + 1])
                nc.scalar.activation(fs[:, qs(q)], psum[:, 2 + q % 2 * 3, C:2 * C], ACT.Abs,
                                     bias=cols[:, K_BGF:K_BGF + 1])
                nc.scalar.activation(kT[:, qs(q)], psum[:, 3 + q % 2 * 3, 0:C], ACT.Identity, bias=cols2[:, 2:3],
                                     scale=SCALE).then_inc(gates_read, 1)

            def copy_score(q):
                act.wait_ge(score_ps, q + 1)
                if q == 0:
                    act.wait_ge(zeroed, 7)
                if q >= 2:
                    act.wait_ge(level_s_ok, q - 1)
                    act.wait_ge(u_ps, 4 * (q - 1))
                src = psum[:, 5 + q % 2, :].rearrange("p (b t) -> p b t", b=BQ)
                dst = level_s[:, q % 2, :, :].rearrange("p n (b t) -> p n b t", b=BQ)
                for n in range(3):
                    half = P >> (n + 1)
                    for s in range(0, P, 2 * half):
                        at = slice(s + half, s + 2 * half)
                        nc.scalar.activation(dst[s:s + half, n, :, at], src[s:s + half, :, at], ACT.Copy)
                nc.scalar.activation(score[:, q % 2, :], psum[:, 5 + q % 2, :], ACT.Copy).then_inc(score_ok, 1)

            for i in range(Q + 1):
                if i < Q:
                    copy_xT(2, i)
                if 0 <= i - 1 < Q:
                    gates(i - 1)
            act.wait_ge(gates_read, Q)
            nc.scalar.activation(fs[:, :], fs[:, :], ACT.Sigmoid).then_inc(a_order, 1)
            act.wait_ge(vo_ok, Q)
            nc.scalar.activation(vo[:, :, P:2 * P], vo[:, :, P:2 * P], ACT.Sigmoid).then_inc(sig_ok, 1)
            act.wait_ge(a_order, 1)
            for q in range(Q):
                nc.scalar.activation(fs[:, qs(q)], fs[:, qs(q)], ACT.Ln).then_inc(ln_f_ok, 1)

            def decays(q):
                act.wait_ge(expo_ok, q + 1)
                nc.scalar.activation(fs[:, qs(q)], phi[:, qs(q)], ACT.Exp)
                nc.scalar.activation(li[:, qs(q)], li[:, qs(q)], ACT.Exp).then_inc(decay_ok, 1)

            def copy_decays(q):
                act.wait_ge(decay_ps, q + 1)
                if q >= 2:
                    act.wait_ge(vi_ok, q - 1)
                nc.scalar.activation(phi_t[:, q, :], psum[:, 4, 0:C], ACT.Copy)
                nc.scalar.activation(iota_t[:, q % 2, :], psum[:, 4, C:2 * C], ACT.Copy).then_inc(decay_t, 1)

            copy_score(0)
            for i in range(Q + 1):
                if i < Q:
                    decays(i)
                if i >= 1:
                    copy_decays(i - 1)
                if i == 2:
                    copy_score(1)
            act.wait_ge(den_ps, Q)

            def level_decay(q, n):
                if n < 3:
                    act.wait_ge(arg_ps, 3 * q + n + 1)
                if q >= 2:
                    act.wait_ge(u_read, 4 * (q - 2) + n + 1)
                if n == 3:
                    act.wait_ge(decay_t, q + 1)
                    nc.scalar.activation(G[:, q % 2, 6, :], phi_t[:, q, :], ACT.Exp).then_inc(G_ok, 1)
                else:
                    nc.scalar.activation(G[:, q % 2, 2 * n:2 * n + 2, :].rearrange("p n c -> p (n c)"),
                                         psum[:, (3 * q + n) % 2, :], ACT.Exp).then_inc(G_ok, 1)

            def squares(q):
                act.wait_ge(gated_ok, q + 1)
                for b in range(BQ):
                    last = nc.scalar.activation(sq[:, b * D:(b + 1) * D], gated[:, q % 2, b * D:(b + 1) * D],
                                                ACT.Square, accum_out=var[:, 3, q * BQ + b:q * BQ + b + 1])
                last.then_inc(ms_ok, 1)

            for q in range(Q):
                for n in range(4):
                    level_decay(q, n)
                    if n == 0 and q >= 2:
                        squares(q - 2)
                if 1 <= q < Q - 1:
                    copy_score(q + 1)
            squares(Q - 2)
            copy_xT(3, 0)
            squares(Q - 1)
            copy_xT(3, 1)

            def relu_first(q):
                act.wait_ge(f0_ps, q + 1)
                if q == 0:
                    act.wait_ge(u_read, 4 * (Q - 1))
                if q >= 2:
                    act.wait_ge(layer_ps[0], q - 1)
                nc.scalar.activation(f0[:, q % 2, :], psum[:, 2, :], ACT.Relu,
                                     bias=hidw[:, W_BI:W_BI + 1]).then_inc(f0_ok, 1)

            def copy_turned(n, q):
                act.wait_ge(turned_ps[n], q + 1)
                if q == 0 and n == 0:
                    act.wait_ge(u_read, 4 * Q)
                if q >= 2 and n == 0:
                    act.wait_ge(layer_ps[1], q - 1)
                if q >= 2 and n == 1:
                    act.wait_ge(fo_ps, q - 1)
                nc.scalar.activation((f1, f2)[n][:, q % 2, :], psum[:, 5 + n, :], ACT.Copy).then_inc(turned_ok[n], 1)

            relu_first(0)
            for i in range(Q + 1):
                if i + 1 < Q:
                    relu_first(i + 1)
                if i + 2 < Q:
                    copy_xT(3, i + 2)
                if i < Q:
                    copy_turned(0, i)
                if 0 <= i - 1 < Q:
                    copy_turned(1, i - 1)

        @block.tensor
        def _(pe):
            def transpose_x(n, q):
                pe.wait_ge(ln_out[n], q + 1)
                if q >= 2:
                    pe.wait_ge(xT_ok[n], q - 1)
                elif n >= 1:
                    pe.wait_ge(xT_ok[n - 1], Q - 1 + q)
                for b in range(PQ):
                    last = nc.tensor.transpose(psum[:, q % 2, b * P:(b + 1) * P],
                                               xn[:, q * C + b * P:q * C + (b + 1) * P], ident)
                last.then_inc(xT_ps[n], 1)

            pe.wait_ge(consts_in, 16)
            pe.wait_ge(small_in, 32)
            for n in range(HALVES):
                last = nc.tensor.matmul(psum[n * D:(n + 1) * D, 7, 0:D], wqk[:, 0, :], wqk[:, 1, :],
                                        start=True, stop=True)
            last.then_inc(score_w_ps, 1)

            def project(q):
                pe.wait_ge(xT_ok[0], q + 1)
                if q >= 1:
                    pe.wait_ge(z_ok, q)
                nc.tensor.matmul(psum[:, 2, 0:C], score_w[:, :], xT[:, qs(q)], start=True, stop=True).then_inc(z_ps, 1)

            def scores(q):
                pe.wait_ge(z_ok, q + 1)
                if q >= 2:
                    pe.wait_ge(s_masked, q - 1)
                for b in range(PQ):
                    last = nc.tensor.matmul(psum[:, 5 + q % 2, b * 2 * P:(b + 1) * 2 * P],
                                            xT[:, q * C + b * P:q * C + (b + 1) * P],
                                            apart[:, q, :, b * P:(b + 1) * P], start=True, stop=True)
                last.then_inc(s_ps, 1)
                if q >= 2:
                    pe.wait_ge(vs_ok, q - 1)
                for b in range(PQ):
                    last = nc.tensor.matmul(psum[:, 3 + q % 2, b * P:(b + 1) * P],
                                            xT[:, q * C + b * P:q * C + (b + 1) * P], diag[:, M_V0, :],
                                            start=True, stop=True)
                last.then_inc(v_ps, 1)

            def attend(q):
                pe.wait_ge(prob_ok, q + 1)
                pe.wait_ge(vs_ok, q + 1)
                if q >= 1:
                    pe.wait_ge(av_added, q)
                for b in range(PQ):
                    for n in range(HALVES):
                        at = slice(b * P + n * D, b * P + (n + 1) * D)
                        last = nc.tensor.matmul(psum[:, 7, at], prob[:, q % 2, b * HALVES + n, :],
                                                vs[:, q % 2, at], start=True, stop=True)
                last.then_inc(av_ps, 1)

            pe.wait_ge(score_w_ok, 2)
            pe.wait_ge(diag_in, 16 * 6)
            for i in range(Q + 2):
                if i >= 2:
                    attend(i - 2)
                if i < Q:
                    transpose_x(0, i)
                    project(i)
                    scores(i)

            def router(q):
                pe.wait_ge(xT_ok[1], q + 1)
                if q == 0:
                    pe.wait_ge(xT_ok[0], Q)
                else:
                    pe.wait_ge(wT_ok, q)
                for b in range(PQ):
                    last = nc.tensor.matmul(psum[:, 1, b * HALVES * E:(b + 1) * HALVES * E],
                                            xT[:, q * C + b * P:q * C + (b + 1) * P], router_w[:, :],
                                            start=True, stop=True)
                last.then_inc(logit_ps, 1)

            def turn_weights(q):
                pe.wait_ge(weights_ok, q + 1)
                for b in range(PQ):
                    for n in range(HALVES):
                        at = (n * PQ + b) * P
                        nc.tensor.transpose(turned_w[0:PARTS * E, at:at + P],
                                            wsplit[:, q % 2, b * HALVES + n, :, :].rearrange("p a e -> p (a e)"),
                                            ident_b)
                nc.tensor.transpose(psum[0:BQ * E, 1, C:C + P],
                                    wfull[:, q % 2, :, :].rearrange("p b e -> p (b e)"), ident).then_inc(wT_ps, 1)

            def up(k):
                if k == 0:
                    pe.wait_ge(first_in, 64)
                    pe.wait_ge(vs_ok, Q)
                if k % E == 0:
                    pe.wait_ge(xT_ok[1], k // E + 1)
                if k >= 2:
                    pe.wait_ge(up_ok, k - 1)
                nc.tensor.matmul(psum[:, 3 + k % 2, :], first[:, k % E, :],
                                 apart[:, k // E, :, :].rearrange("p h c -> p (h c)"),
                                 start=True, stop=True).then_inc(up_ps, 1)

            def spread(k):
                if k == 0:
                    pe.wait_ge(s_masked, Q)
                if k % E == 0:
                    pe.wait_ge(wT_ok, k // E + 1)
                if k >= 2:
                    pe.wait_ge(weigh_ok, k - 1)
                nc.tensor.matmul(psum[:, 5 + k % 2, :], pick[:, k % E, :], wT_b[:, k // E % 2, :],
                                 start=True, stop=True).then_inc(spread_ps, 1)

            def down(k):
                pe.wait_ge(weigh_ok, k + 1)
                if k == 0:
                    pe.wait_ge(av_added, Q)
                    pe.wait_ge(hid_in, 32)
                elif k % E == 0:
                    pe.wait_ge(yT_ok, k // E)
                e = k % E
                for n in range(HALVES):
                    last = nc.tensor.matmul(psum[n * D:(n + 1) * D, 7, 0:C],
                                            w2[:, e * D:(e + 1) * D],
                                            hid[:, k % 4, n * C:(n + 1) * C], start=e == 0, stop=e == E - 1)
                last.then_inc(down_ps, 1)

            def experts_out(q):
                pe.wait_ge(yT_ok, q + 1)
                if q >= 1:
                    pe.wait_ge(y_added, q)
                nc.tensor.matmul(psum[:, 2, 0:C], wT_f[:, q % 2, :], b2[:, :], start=True, stop=False,
                                 skip_group_check=True)
                for b in range(PQ):
                    last = nc.tensor.matmul(psum[:, 2, b * P:(b + 1) * P], yT[:, q % 2, b * P:(b + 1) * P], ident,
                                            start=False, stop=b == PQ - 1, skip_group_check=True)
                last.then_inc(y_ps, 1)

            pe.wait_ge(pick_in, 16 * (1 + BQ))
            transpose_x(1, 0)
            router(0)
            up(0)
            up(1)
            turn_weights(0)
            pe.wait_ge(z_ok, Q)
            for k in range(Q * E + 2):
                q, e = k // E, k % E
                if k + 2 < Q * E:
                    up(k + 2)
                if k < Q * E:
                    spread(k)
                if k >= 2:
                    down(k - 2)
                if e == 0 and q + 1 < Q:
                    transpose_x(1, q + 1)
                if e == 2 and q + 1 < Q:
                    router(q + 1)
                if e == 3 and q >= 1:
                    experts_out(q - 1)
                if e == 7 and q + 1 < Q:
                    turn_weights(q + 1)
            experts_out(Q - 1)

            def gates(q):
                pe.wait_ge(xT_ok[2], q + 1)
                if q == 0:
                    pe.wait_ge(y_added, Q)
                    pe.wait_ge(up_ok, Q * E)
                    pe.wait_ge(weigh_ok, Q * E)
                    pe.wait_ge(yT_ok, Q)
                if q >= 2:
                    pe.wait_ge(gates_read, q - 1)
                for k, (bank, at) in zip((M_I, M_F, M_K), ((2, 0), (2, C), (3, 0))):
                    nc.tensor.matmul(psum[:, bank + q % 2 * 3, at:at + C], diag[:, k, :], xT[:, qs(q)],
                                     start=True, stop=True)
                if q >= 1:
                    pe.wait_ge(q_ok, q)
                last = nc.tensor.matmul(psum[:, 4, 0:C], diag[:, M_Q, :], xT[:, qs(q)], start=True, stop=True)
                last.then_inc(gates_ps, 1)
                if q >= 1:
                    pe.wait_ge(vo_ok, q)
                for b in range(PQ):
                    last = nc.tensor.matmul(psum[:, 7, b * 2 * P:(b + 1) * 2 * P],
                                            xT[:, q * C + b * P:q * C + (b + 1) * P],
                                            diag[:, M_V:M_O + 1, :].rearrange("p m c -> p (m c)"),
                                            start=True, stop=True)
                last.then_inc(vo_ps, 1)

            def score(q):
                pe.wait_ge(gates_read, q + 1)
                pe.wait_ge(q_ok, q + 1)
                if q < 2:
                    pe.wait_ge(gates_read, Q)
                else:
                    pe.wait_ge(score_ok, q - 1)
                for b in range(PQ):
                    last = nc.tensor.matmul(psum[:, 5 + q % 2, b * 2 * P:(b + 1) * 2 * P],
                                            kT[:, q * C + b * P:q * C + (b + 1) * P],
                                            apart[:, q, :, b * P:(b + 1) * P], start=True, stop=True)
                last.then_inc(score_ps, 1)

            def decays(q):
                pe.wait_ge(decay_ok, q + 1)
                if q == 0:
                    pe.wait_ge(q_ok, Q)
                else:
                    pe.wait_ge(decay_t, q)
                for k, src in enumerate((phi, li)):
                    for b in range(PQ):
                        last = nc.tensor.transpose(psum[:, 4, k * C + b * P:k * C + (b + 1) * P],
                                                   src[:, q * C + b * P:q * C + (b + 1) * P], ident)
                last.then_inc(decay_ps, 1)

            def normaliser(q):
                pe.wait_ge(nq_ok, q + 1)
                if q == 0:
                    pe.wait_ge(vo_ok, Q)
                for b in range(PQ):
                    k = q * BQ + b * HALVES
                    last = nc.tensor.matmul(psum[:, 7, k:k + HALVES],
                                            sp[:, q * C + b * P:q * C + (b + 1) * P],
                                            consts[:, C_HALF:C_HALF + HALVES], start=True, stop=True)
                last.then_inc(den_ps, 1)

            for i in range(Q + 1):
                if i < Q:
                    transpose_x(2, i)
                if 0 <= i - 1 < Q:
                    gates(i - 1)
            score(0)
            score(1)
            for q in range(Q):
                decays(q)
            for q in range(Q):
                normaliser(q)

            def arguments(q, n):
                k = 3 * q + n
                if q == 0 and n == 0:
                    pe.wait_ge(levels_in, 16)
                    pe.wait_ge(decay_t, Q)
                    pe.wait_ge(xT_ok[2], Q)
                if k >= 2:
                    before = k - 2
                    pe.wait_ge(G_ok, 4 * (before // 3) + before % 3 + 1)
                for j in range(2):
                    at = C_SUM + (2 * n + j) * P
                    last = nc.tensor.matmul(psum[:, k % 2, j * C:(j + 1) * C], consts[:, at:at + P],
                                            phi_t[:, q, :], start=True, stop=True)
                last.then_inc(arg_ps, 1)

            def recall(q, n):
                k = 4 * q + n
                if n == 0:
                    pe.wait_ge(level_s_ok, q + 1)
                if n < 3:
                    pe.wait_ge(vg_ok, 3 * q + n + 1)
                if k >= 4:
                    pe.wait_ge(u_read, k - 3)
                elif n == 3:
                    pe.wait_ge(rden_ok, 1)
                for j in range(2):
                    lv = 2 * n + j
                    for b in range(PQ):
                        for s in range(HALVES):
                            at = slice(b * P + s * D, b * P + (s + 1) * D)
                            rhs = (vg[:, (3 * q + n) % 4, j, at] if n < 3 else
                                   vo[:, q * PQ + b, s * D:(s + 1) * D])
                            w = (b * HALVES + s) * P
                            last = nc.tensor.matmul(psum[:, U_BANKS[n], j * C + b * P + s * D:
                                                         j * C + b * P + (s + 1) * D],
                                                    level_s[:, q % 2, lv, w:w + P], rhs, start=True, stop=True)
                last.then_inc(u_ps, 1)

            for i in range(Q + 1):
                for n in range(4):
                    if i < Q and n < 3:
                        arguments(i, n)
                    if i >= 1:
                        recall(i - 1, n)
                    if i == Q and n == 1:
                        transpose_x(3, 0)
                if i < 2:
                    score(i + 2)

            def feed_first(q):
                pe.wait_ge(xT_ok[3], q + 1)
                if q == 0:
                    pe.wait_ge(u_read, 4 * Q - 3)
                else:
                    pe.wait_ge(f0_ok, q)
                nc.tensor.matmul(psum[:, 2, :], wi[:, :], apart[:, q, :, :].rearrange("p h c -> p (h c)"),
                                 start=True, stop=True).then_inc(f0_ps, 1)

            def feed_layer(n, q):
                if q == 0 and n == 0:
                    pe.wait_ge(hot_ok, 2)
                    pe.wait_ge(u_read, 4 * Q - 1)
                if q >= 1:
                    pe.wait_ge(token_ok[n], q)
                for t in range(BQ):
                    nc.tensor.matmul(psum[:, 3 + n, t * P:(t + 1) * P],
                                     one_hot[:, (q * BQ + t) * P:(q * BQ + t + 1) * P],
                                     bias_b[:, n * HID:(n + 1) * HID], start=t == 0, stop=False,
                                     skip_group_check=True)
                pe.wait_ge(slot_ok[q], GQ)
                slots, base = slots_of(q)
                if n == 0:
                    pe.wait_ge(f0_ok, q + 1)
                else:
                    pe.wait_ge(turned_ok[0], q + 1)
                for g in range(GQ):
                    t, r = g // (P // GT), g % (P // GT) * GT
                    w = base + (g * L1 + n) * HID
                    last = nc.tensor.matmul(psum[r:r + GT, 3 + n, t * P:(t + 1) * P],
                                            (f0, f1)[n][:, q % 2, g * GT:(g + 1) * GT], slots[:, w:w + HID],
                                            start=False, stop=g == GQ - 1, skip_group_check=True)
                last.then_inc(layer_ps[n], 1)

            def turn(n, q):
                pe.wait_ge(token_ok[n], q + 1)
                if q == 0 and n == 0:
                    pe.wait_ge(score_ok, Q)
                if q >= 1:
                    pe.wait_ge(turned_ok[n], q)
                for t in range(BQ):
                    last = nc.tensor.transpose(psum[:, 5 + n, t * P:(t + 1) * P],
                                               token[:, n, t * P:(t + 1) * P], ident)
                last.then_inc(turned_ps[n], 1)

            def feed_last(q):
                pe.wait_ge(turned_ok[1], q + 1)
                if q == 0:
                    pe.wait_ge(u_read, 4 * Q)
                else:
                    pe.wait_ge(out_ok, q)
                for b in range(PQ):
                    for n in range(HALVES):
                        at = b * P + n * D
                        last = nc.tensor.matmul(psum[:, 7, at:at + D],
                                                f2[:, q % 2, n * C + b * P:n * C + (b + 1) * P],
                                                hidw[:, W_WO:W_WO + D], start=True, stop=True)
                last.then_inc(fo_ps, 1)

            transpose_x(3, 1)
            feed_first(0)
            for i in range(Q + 2):
                if i < Q:
                    feed_layer(0, i)
                if i + 1 < Q:
                    feed_first(i + 1)
                if i + 2 < Q:
                    transpose_x(3, i + 2)
                if 0 <= i - 1 < Q:
                    feed_layer(1, i - 1)
                if i < Q:
                    turn(0, i)
                if 0 <= i - 1 < Q:
                    turn(1, i - 1)
                if 0 <= i - 2 < Q:
                    feed_last(i - 2)

        @block.vector
        def _(dve):
            count = [0]

            def link(ins):
                count[0] += 1
                ins.then_inc(v_order, 1)
                dve.wait_ge(v_order, count[0])

            nc.vector.memset(diag[:, :, :], 0.0).then_inc(zeroed, 1)
            nc.vector.memset(router_w[:, :], 0.0).then_inc(zeroed, 1)
            nc.vector.memset(b2[:, :], 0.0).then_inc(zeroed, 1)
            nc.vector.memset(bias_rows[:, :], 0.0).then_inc(zeroed, 1)
            nc.vector.memset(score_w[:, :], 0.0).then_inc(score_w_ok, 1)
            nc.vector.memset(apart[:, :, :, :], 0.0).then_inc(zeroed, 1)
            nc.vector.memset(wT_b[:, :, :], 0.0)
            nc.vector.memset(wT_f[:, :, :], 0.0).then_inc(zeroed, 1)
            nc.vector.memset(level_s[:, :, 0:3, :], 0.0).then_inc(zeroed, 1)
            link(nc.vector.memset(nm[:, :, 0:1], 0.0))
            dve.wait_ge(score_w_ps, 1)
            dve.wait_ge(score_w_ok, 1)
            nc.vector.tensor_copy(score_w[0:D, 0:D], psum[0:D, 7, 0:D])
            nc.vector.tensor_copy(score_w[D:P, D:P], psum[D:P, 7, 0:D]).then_inc(score_w_ok, 1)
            dve.wait_ge(small_in, 32)
            dve.wait_ge(diag_in, 16 * 6)
            for n in range(2):
                for s in range(HALVES):
                    nc.vector.tensor_copy(gate_bias[:, (n * HALVES + s) * D:(n * HALVES + s + 1) * D],
                                          rows[:, R_BV + n * D:R_BV + (n + 1) * D])
            link(nc.vector.tensor_tensor(cols2[:, 0:1], cols[:, K_BGI:K_BGI + 1], cols[:, K_IB:K_IB + 1], ALU.add))
            link(nc.vector.tensor_scalar(cols2[:, 0:1], cols2[:, 0:1], 0.1, None, ALU.mult))
            nc.vector.tensor_scalar(cols2[:, 2:3], cols[:, K_BK:K_BK + 1], SCALE, None, ALU.mult).then_inc(setup_ok, 1)

            def feed_biases():
                dve.wait_ge(route_in, 16)
                link(nc.vector.tensor_copy(route_f[:, :], route_sb[:, :]))
                nc.vector.tensor_scalar(one_hot[:, :].rearrange("p (g t) -> p g t", g=GROUPS),
                                        per_seq(route_f[:, :], GROUPS, GT), consts[:, C_ROW:C_ROW + 1], None,
                                        ALU.is_equal).then_inc(hot_ok, 1)
                dve.wait_ge(bias_in, 16 * (PARTS + 1))
                link(nc.vector.tensor_tensor(bias_rows[:, :], bias_rows[:, :], bias_sh[:, :], ALU.add))
                for n, spans in enumerate((((0, P),), ((32, 64), (64, P)), ((64, P),))):
                    for lo, hi in spans:
                        if n > 0:
                            link(nc.vector.tensor_tensor(bias_rows[lo:hi, :], bias_rows[lo:hi, :],
                                                         bias_b[lo:hi, :], ALU.subtract))
                        link(nc.vector.tensor_copy(bias_b[lo:hi, :], bias_rows[lo:hi, :]))
                nc.vector.memset(route_f[:, 0:1], 0.0).then_inc(hot_ok, 1)

            def stats(n, q):
                for b in range(q * BQ, (q + 1) * BQ):
                    last = nc.vector.bn_stats(bn[:, b, :], h[:, b * D:(b + 1) * D])
                link(last)
                for b in range(q * BQ, (q + 1) * BQ):
                    last = nc.vector.bn_aggr(mv[:, n, b, :], bn[:, b, :])
                last.then_inc(ln_stats[n], 1)

            def normalise(n, q):
                dve.wait_ge(ln_rstd[n], q + 1)
                for b in range(q * BQ, (q + 1) * BQ):
                    last = nc.vector.tensor_scalar(xn[:, b * D:(b + 1) * D], h[:, b * D:(b + 1) * D],
                                                   mv[:, n, b, 0:1], rstd[:, n, b:b + 1], ALU.subtract, ALU.mult)
                last.then_inc(ln_out[n], 1)

            def embed(q):
                dve.wait_ge(embed_in[q], 16 * BQ)
                link(nc.vector.tensor_tensor(h[:, qs(q)].rearrange("p (b d) -> p b d", b=BQ),
                                             h[:, qs(q)].rearrange("p (b d) -> p b d", b=BQ),
                                             repeated(consts[:, C_POS:C_POS + D], BQ, D), ALU.add))
                stats(0, q)

            def softmax_bias(q):
                dve.wait_ge(s_ps, q + 1)
                if q >= 2:
                    dve.wait_ge(prob_ok, q - 1)
                nc.vector.tensor_tensor(sc[:, q % 2, :, :],
                                        psum[:, 5 + q % 2, :].rearrange("p (b t) -> p b t", b=BQ),
                                        repeated(consts[:, C_CAUSAL:C_CAUSAL + P], BQ, P),
                                        ALU.subtract).then_inc(s_masked, 1)
                dve.wait_ge(s_masked, q + 1)
                seqs = slice(q * BQ, (q + 1) * BQ)
                link(nc.vector.tensor_reduce(nmax[:, seqs], sc[:, q % 2, :, :], AX.X, ALU.max, negate=True))
                nc.vector.tensor_scalar(nbias[:, seqs], nmax[:, seqs], SCALE, None, ALU.mult).then_inc(s_bias, 1)

            def scale_v(q):
                seqs = slice(q * BQ, (q + 1) * BQ)
                dve.wait_ge(prob_ok, q + 1)
                link(nc.vector.reciprocal(rsum[:, seqs], psums[:, seqs]))
                dve.wait_ge(v_ps, q + 1)
                if q >= 2:
                    dve.wait_ge(av_ps, q - 1)
                nc.vector.tensor_tensor(vs[:, q % 2, :].rearrange("p (b d) -> p b d", b=BQ),
                                        psum[:, 3 + q % 2, 0:C].rearrange("p (b d) -> p b d", b=BQ),
                                        per_seq(rsum[:, seqs]), ALU.mult).then_inc(vs_ok, 1)

            def add_attention(q):
                dve.wait_ge(av_ps, q + 1)
                nc.vector.tensor_tensor(h[:, qs(q)], psum[:, 7, 0:C], h[:, qs(q)], ALU.add).then_inc(av_added, 1)
                dve.wait_ge(av_added, q + 1)
                stats(1, q)

            dve.wait_ge(consts_in, 16)
            for i in range(Q + 2):
                if i < Q:
                    embed(i)
                if i >= 2:
                    scale_v(i - 2)
                    add_attention(i - 2)
                if i < Q:
                    normalise(0, i)
                if 0 <= i - 1 < Q:
                    softmax_bias(i - 1)
                if i >= 2:
                    normalise(1, i - 2)

            def compare(q):
                a = q % 2
                lg, cmp = logit[:, a], ge[:, a]
                dve.wait_ge(logit_ps, q + 1)
                link(nc.vector.tensor_tensor(lg, psum[:, 1, 0:BQ * E].rearrange("p (b e) -> p b e", b=BQ),
                                             repeated(rows[:, R_BR:R_BR + E], BQ, E), ALU.add))
                link(nc.vector.tensor_tensor(cmp, lg.unsqueeze(2).to_broadcast([P, BQ, E, E]),
                                             lg.unsqueeze(3).to_broadcast([P, BQ, E, E]), ALU.is_ge))
                flat = cmp.rearrange("p b e j -> p b (e j)")
                link(nc.vector.tensor_tensor(flat, flat, repeated(consts[:, C_TIE:C_TIE + E * E], BQ, E * E),
                                             ALU.mult))

            def rank(q):
                a = q % 2
                cmp, se, bk = ge[:, a], sel[:, a], back[:, a]
                nc.vector.tensor_reduce(se, cmp, AX.X, ALU.add)
                link(nc.vector.tensor_reduce(bk, cmp.rearrange("p b e j -> p b j e"), AX.X, ALU.add))
                link(nc.vector.tensor_tensor(se, se, bk, ALU.subtract))
                link(nc.vector.tensor_tensor(se, se, repeated(consts[:, C_RANK:C_RANK + E], BQ, E), ALU.is_lt))

            def centre(q):
                a = q % 2
                lg, se, bk = logit[:, a], sel[:, a], back[:, a]
                link(nc.vector.tensor_tensor(bk, se, lg, ALU.mult))
                link(nc.vector.tensor_reduce(lsum[:, a, :], bk, AX.X, ALU.add))
                link(nc.vector.tensor_scalar(lsum[:, a, :], lsum[:, a, :], 0.5, None, ALU.mult))
                nc.vector.tensor_tensor(off[:, a], lg, per_seq(lsum[:, a, :], BQ, E), ALU.subtract).then_inc(logit_off, 1)

            def weights(q):
                a = q % 2
                dve.wait_ge(tanh_ok, q + 1)
                if q >= 2:
                    dve.wait_ge(wT_ps, q - 1)
                link(nc.vector.tensor_scalar(off[:, a], off[:, a], 0.5, 0.5, ALU.mult, ALU.add))
                link(nc.vector.tensor_tensor(wfull[:, a], off[:, a], sel[:, a], ALU.mult))
                link(nc.vector.tensor_copy(wsplit[:, a, :, 0, :], wfull[:, a]))
                link(nc.vector.tensor_tensor(wrest[:, a], wfull[:, a], wsplit[:, a, :, 0, :], ALU.subtract))
                link(nc.vector.tensor_copy(wsplit[:, a, :, 1, :], wrest[:, a]))
                link(nc.vector.tensor_tensor(wrest[:, a], wrest[:, a], wsplit[:, a, :, 1, :], ALU.subtract))
                nc.vector.tensor_copy(wsplit[:, a, :, 2, :], wrest[:, a]).then_inc(weights_ok, 1)

            def weigh(k):
                dve.wait_ge(up_ok, k + 1)
                dve.wait_ge(spread_ps, k + 1)
                nc.vector.tensor_tensor(hid[:, k % 4, :], psum[:, 5 + k % 2, :], hid[:, k % 4, :],
                                        ALU.mult).then_inc(weigh_ok, 1)

            def add_experts(q):
                dve.wait_ge(y_ps, q + 1)
                nc.vector.tensor_tensor(h[:, qs(q)], psum[:, 2, 0:C], h[:, qs(q)], ALU.add).then_inc(y_added, 1)
                dve.wait_ge(y_added, q + 1)
                stats(2, q)

            compare(0)
            rank(0)
            centre(0)
            weights(0)
            for k in range(Q * E):
                q, e = k // E, k % E
                weigh(k)
                if e == 2 and q + 1 < Q:
                    compare(q + 1)
                if e == 3 and q + 1 < Q:
                    rank(q + 1)
                if e == 4 and q + 1 < Q:
                    centre(q + 1)
                if e == 6 and q + 1 < Q:
                    weights(q + 1)
                if e == 5 and q >= 1:
                    add_experts(q - 1)
                if e == 7 and q >= 1:
                    normalise(2, q - 1)
            add_experts(Q - 1)
            normalise(2, Q - 1)

            def add_vo_bias(q):
                dve.wait_ge(vo_ps, q + 1)
                nc.vector.tensor_tensor(vo[:, q * PQ:(q + 1) * PQ, :],
                                        psum[:, 7, :].rearrange("p (b c) -> p b c", b=PQ),
                                        repeated(gate_bias[:, :], PQ, 2 * HALVES * D), ALU.add).then_inc(vo_ok, 1)

            def stabiliser(q):
                dve.wait_ge(ln_f_ok, q + 1)
                nc.vector.tensor_tensor(sp[:, qs(q)], sp[:, qs(q)], fs[:, qs(q)], ALU.subtract)
                link(nc.vector.tensor_scalar(li[:, qs(q)], li[:, qs(q)], -10.0, None, ALU.mult))
                for b in range(q * PQ, (q + 1) * PQ):
                    at = slice(b * P, (b + 1) * P)
                    last = nc.vector.tensor_tensor_scan(nm[:, b, 1:P + 1], sp[:, at], li[:, at], 0.0, ALU.add, ALU.min)
                link(last)
                pairs = slice(q * PQ, (q + 1) * PQ)

                def two(tile):
                    return tile[:, qs(q)].rearrange("p (b t) -> p b t", b=PQ)

                link(nc.vector.tensor_tensor(two(phi), nm[:, pairs, 1:P + 1], nm[:, pairs, 0:P], ALU.subtract))
                nc.vector.tensor_tensor(two(phi), two(phi), two(sp), ALU.subtract)
                nc.vector.tensor_tensor(two(li), nm[:, pairs, 1:P + 1], two(li), ALU.subtract).then_inc(expo_ok, 1)

            def normaliser(q):
                dve.wait_ge(decay_ok, q + 1)
                link(nc.vector.tensor_tensor(sp[:, qs(q)], li[:, qs(q)], kT[:, qs(q)], ALU.mult))
                for b in range(q * PQ, (q + 1) * PQ):
                    at = slice(b * P, (b + 1) * P)
                    last = nc.vector.tensor_tensor_scan(sp[:, at], fs[:, at], sp[:, at], 0.0, ALU.mult, ALU.add)
                link(last)
                nc.vector.tensor_tensor(sp[:, qs(q)], sp[:, qs(q)], qT[:, qs(q)], ALU.mult).then_inc(nq_ok, 1)

            def weigh_v(q):
                dve.wait_ge(decay_t, q + 1)
                nc.vector.tensor_tensor(vo[:, q * PQ:(q + 1) * PQ, 0:P],
                                        vo[:, q * PQ:(q + 1) * PQ, 0:P],
                                        iota_t[:, q % 2, :].rearrange("p (b c) -> p b c", b=PQ),
                                        ALU.mult).then_inc(vi_ok, 1)

            def add_q_bias(q):
                dve.wait_ge(gates_ps, q + 1)
                bias = cols[:, K_BQ:K_BQ + 1]
                nc.vector.tensor_scalar(qT[:, qs(q)], psum[:, 4, 0:C], bias, None, ALU.add)
                for n in range(HALVES):
                    part = slice(n * D, (n + 1) * D)
                    last = nc.vector.tensor_scalar(apart[part, q, n, :], psum[part, 4, 0:C], bias[part], None,
                                                   ALU.add)
                last.then_inc(q_ok, 1)

            for q in range(Q):
                add_q_bias(q)
                add_vo_bias(q)
            feed_biases()
            for i in range(Q + 2):
                if i < Q:
                    stabiliser(i)
                if 0 <= i - 1 < Q:
                    normaliser(i - 1)
                if 0 <= i - 2 < Q:
                    weigh_v(i - 2)
            dve.wait_ge(vi_ok, Q)
            dve.wait_ge(den_ps, Q)
            link(nc.vector.tensor_copy(rden[:, :], psum[:, 7, 0:B]))
            link(nc.vector.scalar_tensor_tensor(rden[:, :], rden[:, :], -1.0, rden[:, :], ALU.mult, ALU.max))
            link(nc.vector.tensor_scalar(rden[:, :], rden[:, :], 1e-6, None, ALU.max))
            link(nc.vector.reciprocal(rden[:, :], rden[:, :]))
            nc.vector.tensor_tensor(rden2[:, :], rden[:, :], rden[:, :], ALU.mult).then_inc(rden_ok, 1)
            dve.wait_ge(decay_t, Q)
            link(nc.vector.memset(G[:, :, LEVELS:LEVELS + 1, :], 1.0))
            dve.wait_ge(sig_ok, 1)

            def level_v(q, n):
                k = 3 * q + n
                dve.wait_ge(G_ok, 4 * q + n + 1)
                if k >= 4:
                    before = k - 4
                    dve.wait_ge(u_ps, 4 * (before // 3) + before % 3 + 1)
                nc.vector.tensor_tensor(
                    vg[:, k % 4, :, :].rearrange("p n (b c) -> p n b c", b=PQ),
                    G[:, q % 2, 2 * n:2 * n + 2, :].rearrange("p n (b c) -> p n b c", b=PQ),
                    vo[:, q * PQ:(q + 1) * PQ, 0:P].unsqueeze(1).to_broadcast([P, 2, PQ, P]),
                    ALU.mult).then_inc(vg_ok, 1)

            def level_u(q, n):
                k = 4 * q + n
                dve.wait_ge(u_ps, k + 1)
                dve.wait_ge(G_ok, k + 1)
                nc.vector.tensor_tensor(ug[:, 2 * n:2 * n + 2, :].rearrange("p n c -> p (n c)"),
                                        psum[:, U_BANKS[n], :],
                                        G[:, q % 2, 2 * n:2 * n + 2, :].rearrange("p n c -> p (n c)"),
                                        ALU.mult).then_inc(u_read, 1)

            def gate_out(q):
                dve.wait_ge(u_read, 4 * q + 4)
                link(nc.vector.tensor_reduce(acc[:, :], ug[:, :, :].rearrange("p n c -> p c n"), AX.X, ALU.add))
                nc.vector.tensor_tensor(gated[:, q % 2, :].rearrange("p (b c) -> p b c", b=PQ),
                                        acc[:, :].rearrange("p (b c) -> p b c", b=PQ),
                                        vo[:, q * PQ:(q + 1) * PQ, P:2 * P], ALU.mult).then_inc(gated_ok, 1)

            def add_recurrence(q):
                dve.wait_ge(rms_ok, q + 1)
                for b in range(BQ):
                    g = gated[:, q % 2, b * D:(b + 1) * D]
                    last = nc.vector.scalar_tensor_tensor(g, g, factor[:, q * BQ + b:q * BQ + b + 1],
                                                          rows[:, R_NS:R_NS + D], ALU.mult, ALU.mult)
                link(last)
                link(nc.vector.tensor_tensor(h[:, qs(q)], h[:, qs(q)], gated[:, q % 2, :], ALU.add))
                stats(3, q)

            def relu_tokens(n, q):
                dve.wait_ge(layer_ps[n], q + 1)
                if q >= 1:
                    dve.wait_ge(turned_ps[n], q)
                nc.vector.tensor_scalar(token[:, n, :], psum[:, 3 + n, :], 0.0, None, ALU.max).then_inc(token_ok[n], 1)

            for i in range(Q + 1):
                for n in range(4):
                    if i < Q and n < 3:
                        level_v(i, n)
                    if 1 <= i <= Q:
                        level_u(i - 1, n)
                if 3 <= i:
                    normalise(3, i - 3)
                if 1 <= i <= Q:
                    gate_out(i - 1)
                if 2 <= i:
                    add_recurrence(i - 2)
            relu_tokens(0, 0)
            add_recurrence(Q - 1)

            normalise(3, Q - 2)

            def add_last_bias(q):
                dve.wait_ge(ln_out[3], q + 1)
                h3 = h[:, qs(q)].rearrange("p (b d) -> p b d", b=BQ)
                nc.vector.tensor_tensor(h3, h3, repeated(rows[:, R_BO:R_BO + D], BQ, D), ALU.add).then_inc(biased, 1)

            for i in range(Q + 2):
                if 0 < i < Q:
                    relu_tokens(0, i)
                if i == 0:
                    normalise(3, Q - 1)
                if 0 <= i - 1 < Q:
                    relu_tokens(1, i - 1)
                if i < Q:
                    add_last_bias(i)
                if 0 <= i - 2 < Q:
                    q = i - 2
                    dve.wait_ge(fo_ps, q + 1)
                    dve.wait_ge(biased, q + 1)
                    nc.vector.tensor_tensor(outs[:, qs(q)], psum[:, 7, 0:C], h[:, qs(q)], ALU.add).then_inc(out_ok, 1)


def kernel(**inputs):
    import concourse.bacc as bacc
    from concourse.bass_utils import run_bass_kernel_spmd

    a = {k: np.asarray(v) for k, v in inputs.items()}
    wg, bg = a["L1_attn_Wg"], a["L1_attn_bg"]
    arrays = {
        "table": a["L0_tok_W"],
        "tokens": a["x"].T,
        "route": a["L1_ffn_route_id"].reshape(Q, PQ, HALVES, P // GT).transpose(0, 2, 1, 3).reshape(GROUPS),
        "consts": shape_constants(),
        "pick": shape_constants_bf16(),
        "wqk": np.stack([a["L0_attn_Wq"], a["L0_attn_Wk"]], 1),
        "diag": np.stack([a["L0_attn_Wv"].T, wg[:, D:2 * D], wg[:, 0:D], a["L1_attn_Wq"], a["L1_attn_Wk"],
                          a["L1_attn_Wv"], wg[:, 2 * D:]], 1),
        "wr": a["L0_ffn_Wr"],
        "first": np.concatenate([a["L0_ffn_W1"].transpose(1, 0, 2), a["L1_ffn_Wi"].T[:, None, :]], 1),
        "cols": np.stack([a["L0_ffn_gamma"], a["L0_ffn_beta"], bg[0:D], a["L1_attn_input_bias"], bg[D:2 * D],
                          a["L1_attn_bq"], a["L1_attn_bk"]], 1),
        "rows": np.concatenate([a["L0_ffn_br"], a["L1_attn_norm_scale"], a["L1_ffn_bo"], a["L1_attn_bv"],
                                bg[2 * D:]]),
        "w2": a["L0_ffn_W2"].transpose(1, 0, 2).reshape(HID, E * D),
        "hid": np.concatenate([a["L1_ffn_Wo"].T, a["L0_ffn_b1"].T, a["L1_ffn_bi"][:, None]], 1),
        "b2": a["L0_ffn_b2"],
        "routed": a["L1_ffn_Wr"].transpose(3, 1, 0, 2).reshape(HID, NE1 * L1 * HID),
        "shared": a["L1_ffn_Ws"][:, 0].transpose(2, 0, 1).reshape(HID, L1 * HID),
        "bias": a["L1_ffn_br"].transpose(1, 0, 2).reshape(NE1, L1 * HID),
        "shared_bias": a["L1_ffn_bs"].reshape(L1 * HID),
    }
    nc = bacc.Bacc("TRN2", target_bir_lowering=False, num_devices=1)
    feeds, args = {}, []
    for name, x in arrays.items():
        x = np.ascontiguousarray(x)
        feeds[f"in_{name}"] = x
        args.append(nc.dram_tensor(f"in_{name}", x.shape, mybir.dt.from_np(x.dtype), kind="ExternalInput").ap())
    out = nc.dram_tensor("out_0", (B, P, D), F32, kind="ExternalOutput").ap()
    tower(nc, *args, out)
    r = run_bass_kernel_spmd(nc, [feeds], core_ids=[0])
    return r.results[0]["out_0"]
```

```python
from contextlib import ExitStack

import numpy as np
import concourse.bass as bass
from concourse import mybir


P = 128
B = 16
D = 64
HALVES = 2
Q = 4
BQ = B // Q
PQ = BQ // HALVES
C = BQ * D
E = 8
HID = 128
NE1 = 16
L1 = 2
GROUPS = 64
GT = B * P // GROUPS
GQ = GROUPS // Q
STEP = 4
PARTS = 3
LEVELS = 7
EPS = 1e-5
SCALE = D ** -0.5
MASKED = 1e10

ALU = mybir.AluOpType
ACT = mybir.ActivationFunctionType
F32 = mybir.dt.float32
BF16 = mybir.dt.bfloat16
I32 = mybir.dt.int32
AX = mybir.AxisListType

C_ID = 0
C_CAUSAL = C_ID + P
C_TIE = C_CAUSAL + P
C_RANK = C_TIE + E * E
C_POS = C_RANK + E
C_HALF = C_POS + D
C_POW = C_HALF + HALVES
C_ROW = C_POW + BQ
C_SUM = C_ROW + 1
C_MASK = C_SUM + LEVELS * P
N_CONST = C_MASK + LEVELS * P

U_BANKS = (2, 3, 4, 7)

(M_V0, M_F, M_I, M_Q, M_K, M_V, M_O) = range(7)
NM = 7
(K_GAMMA, K_BETA, K_BGI, K_IB, K_BGF, K_BQ, K_BK) = range(7)
NK = 7
R_BR = 0
R_NS = R_BR + E
R_BO = R_NS + D
R_BV = R_BO + D
R_BG = R_BV + D
NR = R_BG + D
W_WO = 0
W_B1 = W_WO + D
W_BI = W_B1 + E
NW = W_BI + 1


def shape_constants():
    c = np.zeros((P, N_CONST), np.float32)
    r = np.arange(P)[:, None]
    t = np.arange(P)[None, :]
    c[:, C_ID:C_ID + P] = r == t
    c[:, C_CAUSAL:C_CAUSAL + P] = np.where(t >= r, np.float32(MASKED), np.float32(0))
    for n in range(LEVELS):
        half = P >> (n + 1)
        mid = t // (2 * half) * (2 * half) + half
        left = t < mid
        span = np.where(left, (r > t) & (r < mid), (r >= mid) & (r <= t))
        c[:, C_SUM + n * P:C_SUM + (n + 1) * P] = span
        same = r // (2 * half) == t // (2 * half)
        c[:, C_MASK + n * P:C_MASK + (n + 1) * P] = same & (r % (2 * half) < half) & (t % (2 * half) >= half)
    e = np.arange(E)
    c[:, C_TIE:C_TIE + E * E] = (e[None, :] < e[:, None]).astype(np.float32).reshape(1, E * E)
    c[:, C_RANK:C_RANK + E] = (e - (E - 1) + 2).astype(np.float32)[None, :]
    d = np.arange(D)
    freq = np.power(np.float32(10000.0), -((d - d % 2).astype(np.float32) / np.float32(D)))
    angle = np.arange(P, dtype=np.float32)[:, None] * freq[None, :]
    c[:, C_POS:C_POS + D] = np.where(d % 2 == 0, np.sin(angle), np.cos(angle))
    for h in range(HALVES):
        c[h * D:(h + 1) * D, C_HALF + h] = 1.0
    c[:, C_POW:C_POW + BQ] = -0.5
    row = np.arange(P)
    c[:, C_ROW] = np.where((row % 32 < NE1) & (row < 32 * PARTS), row % 32, -1)
    return c


def shape_constants_bf16():
    c = np.zeros((P, E + 1, P), np.float32)
    for e in range(E):
        for p in range(PARTS):
            c[p * E + e, e, :] = 1
    c[:, E, :] = np.eye(P)
    return c.reshape(P, (E + 1) * P).astype(mybir.dt.np(BF16))


def tower(nc, table, tokens, route, consts_d, pick_d, wqk_d, diag_d, wr_d, first_d, cols_d, rows_d, w2_d, hid_d, b2_d,
          routed_d, shared_d, bias_d, shared_bias_d, out):
    with ExitStack() as ctx:
        def sb(name, shape, dt=F32):
            return ctx.enter_context(nc.sbuf_tensor(name, shape, dt))

        def sem(name):
            return ctx.enter_context(nc.semaphore(name))

        psum = ctx.enter_context(nc.psum_tensor("psum", [P, 8, 512], F32))

        turned_w = psum[:, 1, :].bitcast(BF16)

        consts = sb("consts", [P, N_CONST])
        wqk = sb("wqk", [D, 2, D])
        gone = sb("gone", [P, NM * P + (E + 1) * P // 2])
        GN = 4
        diag = gone[:, 0:NM * P].rearrange("p (m c) -> p m c", m=NM)
        pick = gone[:, NM * P:].bitcast(BF16).rearrange("p (e c) -> p e c", e=E + 1)
        score_w = sb("score_w", [P, P])
        router_w = sb("router_w", [P, HALVES * E])
        wi = sb("wi", [P, HID])
        early = sb("early", [P, GQ * L1 * HID])
        taken = [0]

        def carve(n):
            taken[0] += n
            return early[:, taken[0] - n:taken[0]]

        first = carve(E * HID).rearrange("p (e c) -> p e c", e=E)
        w2 = carve(E * D)
        yT = carve(2 * C).rearrange("p (a c) -> p a c", a=2)
        wT_b = carve(2 * 512 // 2).bitcast(BF16).rearrange("p (a c) -> p a c", a=2)
        wT_f = carve(2 * P).rearrange("p (a c) -> p a c", a=2)
        b2 = carve(C)
        phi = carve(B * D)
        cols = sb("cols", [P, NK])
        gate_cols = sb("gate_cols", [P, 2])
        rows = sb("rows", [P, NR])
        gate_bias = sb("gate_bias", [P, 2 * HALVES * D])
        hidw = sb("hidw", [P, NW])
        ident_b = pick[:, E, :]
        routed = sb("routed", [P, NE1 * L1 * HID])
        shared = sb("shared", [P, L1 * HID])
        slots_a = sb("slots_a", [P, 2 * GQ * L1 * HID])
        bias_rows = sb("bias_rows", [P, L1 * HID])
        bias_sh = sb("bias_sh", [P, L1 * HID])
        bias_b = sb("bias_b", [P, L1 * HID], BF16)
        route_sb = sb("route_sb", [P, GROUPS], I32)
        route_f = sb("route_f", [P, GROUPS])
        one_hot = sb("one_hot", [P, B * P], BF16)
        tok_sb = sb("tok_sb", [P, B], I32)
        ident = consts[:, C_ID:C_ID + P]

        h = sb("h", [P, B * D])
        bn = sb("bn", [P, B, 6])
        mv = sb("mv", [P, 4, B, 2])
        var = sb("var", [P, 5, B])
        rstd = sb("rstd", [P, 5, B])
        shift1 = sb("shift1", [P, B])
        norm = sb("norm", [P, 3, B * D])
        xn = norm[:, 0, :]
        xT = norm[:, 1, :]
        apart = sb("apart", [P, Q, HALVES, C])

        work = sb("work", [P, 5, B * D])
        sc = work[:, 1, :].rearrange("p (a b t) -> p a b t", a=2, b=BQ)
        prob = work[:, 2, :].rearrange("p (a b t) -> p a b t", a=2, b=BQ)
        nmax = sb("nmax", [P, B])
        nbias = sb("nbias", [P, B])
        psums = sb("psums", [P, B])
        rsum = sb("rsum", [P, B])
        vs = sb("vs", [P, 2, C])

        logit = sb("logit", [P, 2, BQ, E])
        ge = work[:, 3, 0:2 * BQ * E * E].rearrange("p (a b e j) -> p a b e j", a=2, b=BQ, e=E)
        sel = sb("sel", [P, 2, BQ, E])
        back = sb("back", [P, 2, BQ, E])
        lsum = sb("lsum", [P, 2, BQ])
        off = sb("off", [P, 2, BQ, E])
        wfull = sb("wfull", [P, 2, BQ, E])
        wrest = sb("wrest", [P, 2, BQ, E])
        wsplit = sb("wsplit", [P, 2, BQ, PARTS, E], BF16)
        hid = sb("hid", [P, 4, 512])

        qT = work[:, 0, :]
        kT = work[:, 4, :]
        li = work[:, 2, :]
        sp = work[:, 3, :]
        fs = work[:, 1, :]
        vo = sb("vo", [P, B // 2, 2 * HALVES * D])
        nm = sb("nm", [P, B // 2, P + 1])
        phi_t = sb("phi_t", [P, Q, C])
        iota_t = sb("iota_t", [P, 2, C])
        half = sb("half", [P, 1])
        qk = norm[:, 2, :]
        own = sb("own", [P, B])
        rden = sb("rden", [P, B])
        rden2 = sb("rden2", [P, B])
        factor = sb("factor", [P, B])
        score = sb("score", [P, 2, BQ * P])
        level_s = sb("level_s", [P, 2, LEVELS + 1, BQ * P])
        slots_b = level_s[:, 0, :, :].rearrange("p n t -> p (n t)")
        G = work[:, 0:4, :].rearrange("p (a n) (m c) -> p a (n m) c", a=2, c=C)
        G_first = early[:, 0:LEVELS * C].rearrange("p (n c) -> p n c", c=C)
        vg = hid[:, :, :].rearrange("p k (m c) -> p k m c", m=2)
        ug = norm[:, 1:3, :].rearrange("p n (m c) -> p (n m) c", c=C)
        acc = sb("acc", [P, C])
        gated = sb("gated", [P, 2, C])
        scaled = vs
        sq = sb("sq", [P, C])

        feed = G[:, :, :, :].rearrange("p a n c -> p (a n c)").rearrange("p (f c) -> p f c", f=8)
        f0 = feed[:, 0:2, :]
        token = feed[:, 2:4, :]
        f1 = feed[:, 4:6, :]
        f2 = feed[:, 6:8, :]
        outs = kT

        tok_in = sem("tok_in")
        consts_in = sem("consts_in")
        levels_in = sem("levels_in")
        small_in = sem("small_in")
        diag_in = sem("diag_in")
        first_in = sem("first_in")
        hid_in = sem("hid_in")
        route_in = sem("route_in")
        slots_in = sem("slots_in")
        embed_in = [sem(f"embed_in{q}") for q in range(Q)]
        out_done = sem("out_done")
        diag_zeroed = sem("diag_zeroed")
        apart_zeroed = sem("apart_zeroed")
        nm_zeroed = sem("nm_zeroed")
        rows_zeroed = sem("rows_zeroed")
        level_zeroed = sem("level_zeroed")
        score_w_ps = sem("score_w_ps")
        score_w_ok = sem("score_w_ok")
        setup_ok = sem("setup_ok")
        ln_stats = [sem(f"ln_stats{n}") for n in range(4)]
        ln_rstd = [sem(f"ln_rstd{n}") for n in range(4)]
        ln_out = [sem(f"ln_out{n}") for n in range(4)]
        x_apart_ok = sem("x_apart_ok")
        xT_ps = [sem(f"xT_ps{n}") for n in range(4)]
        xT_ok = [sem(f"xT_ok{n}") for n in range(4)]
        z_ps = sem("z_ps")
        z_ok = sem("z_ok")
        pick_in = sem("pick_in")
        bias_in = sem("bias_in")
        hot_ok = sem("hot_ok")
        v_ps = sem("v_ps")
        s_ps = sem("s_ps")
        s_masked = sem("s_masked")
        s_bias = sem("s_bias")
        prob_ok = sem("prob_ok")
        vs_ok = sem("vs_ok")
        av_ps = sem("av_ps")
        av_added = sem("av_added")
        logit_ps = sem("logit_ps")
        logit_off = sem("logit_off")
        tanh_ok = sem("tanh_ok")
        weights_ok = sem("weights_ok")
        wT_ps = sem("wT_ps")
        wT_ok = sem("wT_ok")
        up_ps = sem("up_ps")
        up_ok = sem("up_ok")
        spread_ps = sem("spread_ps")
        weigh_ok = sem("weigh_ok")
        down_ps = sem("down_ps")
        yT_ok = sem("yT_ok")
        y_ps = sem("y_ps")
        y_added = sem("y_added")
        if_ps = sem("if_ps")
        gates_ps = sem("gates_ps")
        gates_read = sem("gates_read")
        vo_ps = sem("vo_ps")
        vo_ok = sem("vo_ok")
        sig_ok = sem("sig_ok")
        q_ok = sem("q_ok")
        tanh_f_ok = sem("tanh_f_ok")
        half_ok = sem("half_ok")
        ln_f_ok = sem("ln_f_ok")
        softplus_ok = sem("softplus_ok")
        log_i_ok = sem("log_i_ok")
        scan_ok = sem("scan_ok")
        in_log_ok = sem("in_log_ok")
        expo_ok = sem("expo_ok")
        decay_ok = sem("decay_ok")
        nq_ok = sem("nq_ok")
        score_ps = sem("score_ps")
        score_ok = sem("score_ok")
        decay_ps = sem("decay_ps")
        decay_t = sem("decay_t")
        den_ps = sem("den_ps")
        vi_ok = sem("vi_ok")
        level_s_ok = sem("level_s_ok")
        arg_ps = sem("arg_ps")
        G_ok = sem("G_ok")
        vg_ok = sem("vg_ok")
        u_ps = sem("u_ps")
        u_read = sem("u_read")
        gated_ok = sem("gated_ok")
        scaled_ok = sem("scaled_ok")
        rden_ok = sem("rden_ok")
        qk_ok = sem("qk_ok")
        own_ps = sem("own_ps")
        own_ok = sem("own_ok")
        ms_ok = sem("ms_ok")
        rms_ok = sem("rms_ok")
        shared_ok = sem("shared_ok")
        slot_ok = [sem(f"slot_ok{q}") for q in range(Q)]
        f0_ps = sem("f0_ps")
        f0_ok = sem("f0_ok")
        layer_ps = [sem(f"layer_ps{n}") for n in range(L1)]
        token_ok = [sem(f"token_ok{n}") for n in range(L1)]
        turned_ps = [sem(f"turned_ps{n}") for n in range(L1)]
        turned_ok = [sem(f"turned_ok{n}") for n in range(L1)]
        fo_ps = sem("fo_ps")
        biased = sem("biased")
        out_ok = sem("out_ok")
        v_order = sem("v_order")
        g_order = sem("g_order")
        a_order = sem("a_order")

        def qs(q):
            return slice(q * C, (q + 1) * C)

        def G_of(q):
            return G_first if q == 0 else G[:, q % 2, :, :]

        def slots_of(q, g):
            W = L1 * HID
            if q < 2:
                return slots_a, (q * GQ + g) * W
            if q == 2:
                return (gone, g * W) if g < GN else (slots_b, g * W)
            return early, g * W

        def bank_of(n, q):
            return 0 if n == 1 else q % 2

        def last_bank(q):
            return (7, 0)[q % 2]

        def per_seq(ap, n=BQ, k=D):
            return ap.unsqueeze(2).to_broadcast([P, n, k])

        def repeated(ap, n, k):
            return ap.unsqueeze(1).to_broadcast([P, n, k])

        block = ctx.enter_context(nc.Block())

        @block.sync
        def _(sp):
            sp.dma_start(tok_sb[:, :], tokens).then_inc(tok_in, 16)
            sp.dma_start(wqk[:, :, :], wqk_d).then_inc(small_in, 16)
            sp.dma_start(consts[:, 0:C_SUM], consts_d[:, 0:C_SUM]).then_inc(consts_in, 16)
            sp.dma_start(rows[:, :], rows_d.partition_broadcast(P)).then_inc(small_in, 16)
            sp.wait_ge(diag_zeroed, 1)
            for n in range(HALVES):
                part = slice(n * D, (n + 1) * D)
                sp.dma_start(diag[part, :, part], diag_d).then_inc(diag_in, 16)
                sp.dma_start(router_w[part, n * E:(n + 1) * E], wr_d).then_inc(diag_in, 16)
                sp.dma_start(cols[part, :], cols_d).then_inc(diag_in, 16)
                sp.dma_start(first[part, :, :], first_d[:, 0:E]).then_inc(first_in, 16)
                sp.dma_start(wi[part, :], first_d[:, E]).then_inc(first_in, 16)
            sp.dma_start(w2, w2_d).then_inc(hid_in, 16)
            sp.dma_start(hidw[:, :], hid_d).then_inc(hid_in, 16)
            sp.dma_start(pick[:, :, :].rearrange("p e m -> p (e m)"), pick_d).then_inc(pick_in, 16)
            sp.wait_ge(rows_zeroed, 1)
            for n in range(BQ):
                sp.dma_start(b2[n * E:(n + 1) * E, n * D:(n + 1) * D], b2_d).then_inc(pick_in, 16)
            sp.dma_start(route_sb[:, :], route.partition_broadcast(P)).then_inc(route_in, 16)
            sp.dma_start(shared[:, :], shared_d).then_inc(slots_in, 16)
            sp.dma_start(routed[:, :], routed_d).then_inc(slots_in, 16)
            for n in range(PARTS):
                sp.dma_start(bias_rows[32 * n:32 * n + NE1, :], bias_d).then_inc(bias_in, 16)
            sp.dma_start(bias_sh[:, :], shared_bias_d.partition_broadcast(P)).then_inc(bias_in, 16)
            sp.dma_start(consts[:, C_SUM:], consts_d[:, C_SUM:]).then_inc(levels_in, 16)
            for q in range(Q):
                sp.wait_ge(out_ok, q + 1)
                sp.dma_start(out[q * BQ:(q + 1) * BQ].rearrange("b t d -> t b d"),
                             outs[:, qs(q)].rearrange("p (b d) -> p b d", b=BQ)).then_inc(out_done, 16)
            sp.wait_ge(out_done, 16 * Q)

        @block.gpsimd
        def _(gp):
            def power(n, q, scale, shift, src, wait, done):
                seqs = slice(q * BQ, (q + 1) * BQ)
                gp.wait_ge(*wait)
                nc.gpsimd.tensor_scalar(var[:, n, seqs], src, scale, shift, ALU.mult, ALU.add).then_inc(g_order, 1)
                count[0] += 1
                gp.wait_ge(g_order, count[0])
                nc.gpsimd.tensor_tensor(rstd[:, n, seqs], var[:, n, seqs], consts[:, C_POW:C_POW + BQ],
                                        ALU.pow).then_inc(done, 1)

            count = [0]

            def norm_power(n, q):
                scale, shift = (1.0 + EPS, EPS * EPS) if n == 1 else (1.0, EPS)
                seqs = slice(q * BQ, (q + 1) * BQ)
                if n == 1 or n == 3:
                    power(n, q, scale, shift, mv[:, n, seqs, 1], (ln_stats[n], q + 1), g_order)
                    count[0] += 1
                    nc.gpsimd.tensor_scalar(shift1[:, seqs], mv[:, n, seqs, 0], -1.0, None, ALU.mult).then_inc(g_order, 1)
                    count[0] += 1
                    gp.wait_ge(g_order, count[0])
                    nc.gpsimd.tensor_tensor(shift1[:, seqs], shift1[:, seqs], rstd[:, n, seqs],
                                            ALU.mult).then_inc(ln_rstd[n], 1)
                else:
                    power(n, q, scale, shift, mv[:, n, seqs, 1], (ln_stats[n], q + 1), ln_rstd[n])

            def gather(q):
                for b in range(q * BQ, (q + 1) * BQ):
                    nc.gpsimd.indirect_dma_start(
                        out=h[:, b * D:(b + 1) * D], out_offset=None, in_=table,
                        in_offset=bass.IndirectOffsetOnAxis(ap=tok_sb[:, b:b + 1], axis=0),
                    ).then_inc(embed_in[q], 16)

            gp.wait_ge(tok_in, 16)
            gather(0)
            gather(1)
            gp.wait_ge(consts_in, 16)
            norm_power(0, 0)
            gather(2)
            norm_power(0, 1)
            gather(3)
            norm_power(0, 2)
            nc.gpsimd.memset(b2, 0.0)
            nc.gpsimd.memset(bias_rows[:, :], 0.0)
            nc.gpsimd.memset(wT_b[:, :, :], 0.0)
            nc.gpsimd.memset(wT_f[:, :, :], 0.0).then_inc(rows_zeroed, 1)
            norm_power(0, 3)
            norm_power(1, 0)
            norm_power(1, 1)
            norm_power(1, 2)
            norm_power(1, 3)
            nc.gpsimd.memset(level_s[:, :, 0:LEVELS, :], 0.0).then_inc(level_zeroed, 1)
            gp.wait_ge(slots_in, 32)
            gp.wait_ge(route_in, 16)
            for n in range(L1):
                nc.gpsimd.tensor_tensor(shared[:, n * HID:(n + 1) * HID], shared[:, n * HID:(n + 1) * HID],
                                        ident, ALU.add).then_inc(shared_ok, 1)
            gp.wait_ge(shared_ok, L1)
            W = L1 * HID

            def merge(q, first_g=0, n_g=GQ):
                slots, at = slots_of(q, first_g)
                if q == 2:
                    gp.wait_ge(vo_ps, Q)
                if q == 3:
                    gp.wait_ge(decay_ps, Q)
                    if first_g < LEVELS:
                        gp.wait_ge(u_read, (first_g + n_g) // 2)
                with gp.Fori(0, n_g // STEP) as g:
                    experts = [gp.value_load(route_sb[0:1, bass.ds(g * STEP + (q * GQ + first_g + k), 1)],
                                             min_val=0, max_val=NE1 - 1) for k in range(STEP)]
                    for k in range(STEP):
                        nc.gpsimd.tensor_tensor(slots[:, bass.ds(g * (STEP * W) + (at + k * W), W)],
                                                routed[:, bass.ds(experts[k] * W, W)], shared[:, :],
                                                ALU.add).then_inc(slot_ok[q], 1)

            def load_experts(q, first_g, n_g):
                return [gp.value_load(route_sb[0:1, q * GQ + g:q * GQ + g + 1], min_val=0, max_val=NE1 - 1)
                        for g in range(first_g, first_g + n_g)]

            def merge_some(q, first_g, experts):
                slots, at = slots_of(q, first_g)
                gp.wait_ge(u_ps, 4 * (q + 1))
                for k, expert in enumerate(experts):
                    nc.gpsimd.tensor_tensor(slots[:, at + k * W:at + (k + 1) * W],
                                            routed[:, bass.ds(expert * W, W)], shared[:, :],
                                            ALU.add).then_inc(slot_ok[q], 1)

            merge(0)
            merge(1, 0, 4)
            norm_power(2, 0)
            merge(1, 4, 12)
            for q in range(1, Q - 1):
                norm_power(2, q)
            experts = load_experts(2, GN, GQ - GN)
            thirds = (GQ - GN) // 3
            norm_power(2, Q - 1)

            def mask_levels(q):
                gp.wait_ge(score_ok, q + 1)
                if q >= 2:
                    gp.wait_ge(u_ps, 4 * (q - 1))
                mask = consts[:, C_MASK:C_MASK + LEVELS * P].rearrange("p (n t) -> p n t", t=P)
                dst = level_s[:, q % 2, :, :]
                for n in range(3, LEVELS):
                    span = P >> n
                    right = slice(span // 2, span)
                    blocks = P // span
                    last = nc.gpsimd.tensor_tensor(
                        dst[:, n, :].rearrange("p (b j t) -> p b j t", b=BQ, j=blocks)[:, :, :, right],
                        score[:, q % 2, :].rearrange("p (b j t) -> p b j t", b=BQ, j=blocks)[:, :, :, right],
                        mask[:, n, :].rearrange("p (j t) -> p j t", j=blocks)[:, :, right].unsqueeze(1)
                        .to_broadcast([P, BQ, blocks, span // 2]), ALU.mult)
                last.then_inc(level_s_ok, 1)

            def out_factor(q):
                seqs = slice(q * BQ, (q + 1) * BQ)
                gp.wait_ge(gated_ok, q + 1)
                if q >= 2:
                    gp.wait_ge(ln_stats[3], q - 1)
                nc.gpsimd.tensor_tensor(scaled[:, q % 2, :].rearrange("p (b d) -> p b d", b=BQ),
                                        gated[:, q % 2, :].rearrange("p (b d) -> p b d", b=BQ),
                                        repeated(rows[:, R_NS:R_NS + D], BQ, D), ALU.mult).then_inc(scaled_ok, 1)
                gp.wait_ge(rden_ok, 1)
                gp.wait_ge(ms_ok, q + 1)
                nc.gpsimd.tensor_tensor(var[:, 3, seqs], var[:, 3, seqs], rden2[:, seqs], ALU.mult).then_inc(g_order, 1)
                count[0] += 1
                power(4, q, 1.0 / D, 1e-8, var[:, 3, seqs], (g_order, count[0]), g_order)
                count[0] += 1
                gp.wait_ge(g_order, count[0])
                nc.gpsimd.tensor_tensor(factor[:, seqs], rstd[:, 4, seqs], rden[:, seqs], ALU.mult).then_inc(rms_ok, 1)

            def own_products(q):
                gp.wait_ge(gates_read, q + 1)
                gp.wait_ge(q_ok, q + 1)
                nc.gpsimd.tensor_tensor(qk[:, qs(q)], qT[:, qs(q)], kT[:, qs(q)], ALU.mult).then_inc(qk_ok, 1)

            for q in range(Q):
                gp.wait_ge(tanh_f_ok, q + 1)
                nc.gpsimd.tensor_scalar(li[:, qs(q)], li[:, qs(q)], -10.0, None, ALU.mult).then_inc(log_i_ok, 1)
                if q >= 1:
                    own_products(q - 1)
            def softplus(q):
                gp.wait_ge(gates_read, q + 1)
                gp.wait_ge(ln_f_ok, q + 1)
                nc.gpsimd.tensor_tensor(sp[:, qs(q)], sp[:, qs(q)], fs[:, qs(q)], ALU.subtract).then_inc(softplus_ok, 1)

            softplus(1)
            for q in range(Q):
                gp.wait_ge(scan_ok, q + 1)
                li3 = li[:, qs(q)].rearrange("p (b t) -> p b t", b=PQ)
                nc.gpsimd.tensor_tensor(li3, nm[:, q * PQ:(q + 1) * PQ, 1:P + 1], li3,
                                        ALU.subtract).then_inc(in_log_ok, 1)
                if q < 2:
                    softplus(q + 2)
                if q == 2:
                    merge(2, 0, GN)
            own_products(Q - 1)
            gp.wait_ge(levels_in, 16)
            mask_levels(0)
            mask_levels(1)
            merge(3, 8, 8)
            merge(3, 0, 4)
            mask_levels(2)
            out_factor(0)
            merge(3, 4, 4)
            mask_levels(3)
            out_factor(1)
            norm_power(3, 0)
            merge_some(2, GN, experts[0:thirds])
            out_factor(2)
            norm_power(3, 1)
            merge_some(2, GN + thirds, experts[thirds:2 * thirds])
            norm_power(3, 2)
            out_factor(3)
            merge_some(2, GN + 2 * thirds, experts[2 * thirds:])
            norm_power(3, 3)

        @block.scalar
        def _(act):
            def copy_xT(n, q):
                act.wait_ge(xT_ps[n], q + 1)
                src = psum[:, bank_of(n, q), 0:C]
                if n == 3:
                    copy_apart(src, q, lambda o, i, part: nc.scalar.activation(o, i, ACT.Copy), xT_ok[3])
                elif n == 1:
                    affine(xT[:, qs(q)], src, slice(0, P)).then_inc(xT_ok[1], 1)
                else:
                    nc.scalar.activation(xT[:, qs(q)], src, ACT.Copy).then_inc(xT_ok[n], 1)

            def affine(o, i, part):
                return nc.scalar.activation(o, i, ACT.Identity, bias=cols[part, K_BETA:K_BETA + 1],
                                            scale=cols[part, K_GAMMA:K_GAMMA + 1])

            def copy_x_apart(q):
                copy_apart(psum[:, bank_of(1, q), 0:C], q, affine, x_apart_ok)

            def copy_apart(src, q, copy, done):
                for n in range(HALVES):
                    part = slice(n * D, (n + 1) * D)
                    last = copy(apart[part, q, n, :], src[part], part)
                last.then_inc(done, 1)

            def copy_z(q):
                act.wait_ge(z_ps, q + 1)
                copy_apart(psum[:, 2, 0:C], q, lambda o, i, part: nc.scalar.activation(o, i, ACT.Copy), z_ok)

            def softmax_exp(q):
                act.wait_ge(s_bias, q + 1)
                if q >= 2:
                    act.wait_ge(av_ps, q - 1)
                for j in range(BQ):
                    k = q * BQ + j
                    last = nc.scalar.activation(prob[:, q % 2, j, :], sc[:, q % 2, j, :], ACT.Exp,
                                                bias=nbias[:, k:k + 1], scale=SCALE,
                                                accum_out=psums[:, k:k + 1])
                last.then_inc(prob_ok, 1)

            def normalise(n, q):
                act.wait_ge(ln_rstd[n], q + 1)
                for b in range(q * BQ, (q + 1) * BQ):
                    last = nc.scalar.activation(xn[:, b * D:(b + 1) * D], h[:, b * D:(b + 1) * D], ACT.Identity,
                                                bias=shift1[:, b:b + 1], scale=rstd[:, n, b:b + 1])
                last.then_inc(ln_out[n], 1)

            act.wait_ge(nm_zeroed, 1)
            nc.scalar.activation(nbias[:, 0:1], nm[:, 0, 0:1], ACT.Exp).then_inc(a_order, 1)
            act.wait_ge(diag_in, 16 * 6)
            act.wait_ge(apart_zeroed, 1)
            copy_xT(0, 0)
            copy_z(0)
            copy_xT(0, 1)
            copy_z(1)
            softmax_exp(0)
            copy_xT(0, 2)
            copy_z(2)
            softmax_exp(1)
            copy_xT(0, 3)
            normalise(1, 0)
            copy_z(3)
            copy_xT(1, 0)
            softmax_exp(2)
            copy_x_apart(0)
            normalise(1, 1)
            softmax_exp(3)


            def router_tanh(q):
                act.wait_ge(logit_off, q + 1)
                nc.scalar.activation(off[:, q % 2, :, :], off[:, q % 2, :, :], ACT.Tanh).then_inc(tanh_ok, 1)

            def copy_wT(q):
                act.wait_ge(wT_ps, q + 1)
                if q >= 2:
                    act.wait_ge(spread_ps, E * (q - 1))
                    act.wait_ge(y_ps, q - 1)
                nc.scalar.activation(wT_b[0:PARTS * E, q % 2, :], turned_w[0:PARTS * E, 0:512], ACT.Copy)
                nc.scalar.activation(wT_f[0:BQ * E, q % 2, :], psum[0:BQ * E, 1, C:C + P], ACT.Copy).then_inc(wT_ok, 1)

            def gelu(k):
                act.wait_ge(up_ps, k + 1)
                if k >= 4:
                    act.wait_ge(down_ps, k - 3)
                nc.scalar.activation(hid[:, k % 4, :], psum[:, 3 + k % 2, :], ACT.Gelu,
                                     bias=hidw[:, W_B1 + k % E:W_B1 + k % E + 1]).then_inc(up_ok, 1)

            def copy_yT(q):
                act.wait_ge(down_ps, E * (q + 1))
                if q >= 2:
                    act.wait_ge(y_ps, q - 1)
                nc.scalar.activation(yT[:, q % 2, :], psum[:, 7, 0:C], ACT.Copy).then_inc(yT_ok, 1)

            act.wait_ge(hid_in, 32)
            act.wait_ge(rows_zeroed, 1)
            router_tanh(0)
            gelu(0)
            copy_wT(0)
            gelu(1)
            copy_xT(1, 1)
            for k in range(2, Q * E):
                q, e = k // E, k % E
                gelu(k)
                if e == 2 and q + 1 < Q:
                    copy_x_apart(q + 1)
                if e == 4 and q + 2 < Q:
                    normalise(1, q + 2)
                if e == 1:
                    copy_wT(q)
                    if q + 1 < Q:
                        copy_xT(1, q + 1)
                if e == 3 and q >= 1:
                    copy_yT(q - 1)
                if e == 6 and q + 1 < Q:
                    router_tanh(q + 1)
            copy_yT(Q - 1)

            act.wait_ge(setup_ok, 1)

            def gates_tanh(q):
                act.wait_ge(if_ps, q + 1)
                bank = 2 + q % 2 * 3
                nc.scalar.activation(fs[:, qs(q)], psum[:, bank, C:2 * C], ACT.Abs,
                                     bias=cols[:, K_BGF:K_BGF + 1]).then_inc(a_order, 1)
                nc.scalar.activation(li[:, qs(q)], psum[:, bank, 0:C], ACT.Tanh, bias=gate_cols[:, 0:1], scale=0.1)
                act.wait_ge(a_order, q + 2)
                nc.scalar.activation(fs[:, qs(q)], fs[:, qs(q)], ACT.Tanh, scale=0.5).then_inc(tanh_f_ok, 1)

            def gates_linear(q):
                act.wait_ge(gates_ps, q + 1)
                bank = 2 + q % 2 * 3
                nc.scalar.activation(sp[:, qs(q)], psum[:, bank, C:2 * C], ACT.Relu, bias=cols[:, K_BGF:K_BGF + 1])
                nc.scalar.activation(kT[:, qs(q)], psum[:, bank + 1, 0:C], ACT.Identity, bias=gate_cols[:, 1:2],
                                     scale=SCALE).then_inc(gates_read, 1)

            def copy_score(q):
                act.wait_ge(score_ps, q + 1)
                if q == 0:
                    act.wait_ge(level_zeroed, 1)
                if q >= 2:
                    act.wait_ge(level_s_ok, q - 1)
                    act.wait_ge(u_ps, 4 * (q - 1))
                src = psum[:, 5 + q % 2, :].rearrange("p (b t) -> p b t", b=BQ)
                dst = level_s[:, q % 2, :, :].rearrange("p n (b t) -> p n b t", b=BQ)
                for n in range(3):
                    half = P >> (n + 1)
                    for s in range(0, P, 2 * half):
                        at = slice(s + half, s + 2 * half)
                        nc.scalar.activation(dst[s:s + half, n, :, at], src[s:s + half, :, at], ACT.Copy)
                nc.scalar.activation(score[:, q % 2, :], psum[:, 5 + q % 2, :], ACT.Copy).then_inc(score_ok, 1)

            for i in range(Q + 1):
                if i < Q:
                    copy_xT(2, i)
                if 0 <= i - 1 < Q:
                    gates_tanh(i - 1)
                    if i < Q:
                        gates_linear(i - 1)
            act.wait_ge(tanh_f_ok, Q)
            act.wait_ge(half_ok, 1)
            for q in range(Q):
                nc.scalar.activation(fs[:, qs(q)], fs[:, qs(q)], ACT.Ln, bias=half[:, 0:1],
                                     scale=0.5).then_inc(ln_f_ok, 1)
            nc.scalar.activation(nbias[:, 0:1], nm[:, 0, 0:1], ACT.Exp).then_inc(a_order, 1)
            def decays(q):
                act.wait_ge(expo_ok, q + 1)
                act.wait_ge(in_log_ok, q + 1)
                nc.scalar.activation(fs[:, qs(q)], phi[:, qs(q)], ACT.Exp)
                nc.scalar.activation(li[:, qs(q)], li[:, qs(q)], ACT.Exp).then_inc(decay_ok, 1)

            def copy_decays(q):
                act.wait_ge(decay_ps, q + 1)
                if q >= 2:
                    act.wait_ge(vi_ok, q - 1)
                nc.scalar.activation(phi_t[:, q, :], psum[:, 4, 0:C], ACT.Copy)
                nc.scalar.activation(iota_t[:, q % 2, :], psum[:, 4, C:2 * C], ACT.Copy).then_inc(decay_t, 1)

            def level_decay(q, n):
                if n < 3:
                    act.wait_ge(arg_ps, 3 * q + n + 1)
                if q == 1 or q == 2:
                    act.wait_ge(den_ps, Q)
                if q == 3:
                    act.wait_ge(u_read, 4 * (q - 2) + n + 1)
                if n == 3:
                    act.wait_ge(decay_t, q + 1)
                    nc.scalar.activation(G_of(q)[:, 6, :], phi_t[:, q, :], ACT.Exp).then_inc(G_ok, 1)
                else:
                    nc.scalar.activation(G_of(q)[:, 2 * n:2 * n + 2, :].rearrange("p n c -> p (n c)"),
                                         psum[:, (3 * q + n) % 2, :], ACT.Exp).then_inc(G_ok, 1)

            def squares(q):
                act.wait_ge(gated_ok, q + 1)
                for b in range(BQ):
                    last = nc.scalar.activation(sq[:, b * D:(b + 1) * D], gated[:, q % 2, b * D:(b + 1) * D],
                                                ACT.Square, accum_out=var[:, 3, q * BQ + b:q * BQ + b + 1])
                last.then_inc(ms_ok, 1)

            decays(0)
            gates_linear(Q - 1)
            decays(1)
            copy_decays(0)
            copy_score(0)
            decays(2)
            copy_decays(1)
            level_decay(0, 0)
            copy_score(1)
            decays(3)
            copy_decays(2)
            level_decay(0, 1)
            copy_decays(3)
            level_decay(0, 2)
            level_decay(0, 3)
            act.wait_ge(vo_ok, Q)
            nc.scalar.activation(vo[:, :, P:2 * P], vo[:, :, P:2 * P], ACT.Sigmoid).then_inc(sig_ok, 1)
            for q in range(1, Q):
                for n in range(4):
                    level_decay(q, n)
                    if n == 0 and q >= 2:
                        squares(q - 2)
                if 1 <= q < Q - 1:
                    copy_score(q + 1)
            normalise(3, 0)
            copy_xT(3, 0)
            squares(Q - 2)

            def relu_first(q):
                act.wait_ge(f0_ps, q + 1)
                if q == 0:
                    act.wait_ge(u_read, 4 * (Q - 1))
                if q >= 2:
                    act.wait_ge(layer_ps[0], q - 1)
                nc.scalar.activation(f0[:, q % 2, :], psum[:, 2, :], ACT.Relu,
                                     bias=hidw[:, W_BI:W_BI + 1]).then_inc(f0_ok, 1)

            def copy_turned(n, q):
                act.wait_ge(turned_ps[n], q + 1)
                if q == 0 and n == 0:
                    act.wait_ge(u_read, 4 * Q)
                if q >= 2 and n == 0:
                    act.wait_ge(layer_ps[1], q - 1)
                if q >= 2 and n == 1:
                    act.wait_ge(fo_ps, q - 1)
                nc.scalar.activation((f1, f2)[n][:, q % 2, :], psum[:, 5 + n, :], ACT.Copy).then_inc(turned_ok[n], 1)

            relu_first(0)
            normalise(3, 1)
            copy_xT(3, 1)
            for i in range(Q + 1):
                if 0 < i < Q - 1:
                    copy_xT(3, i + 1)
                if i < Q:
                    copy_turned(0, i)
                if 0 <= i - 1 < Q:
                    copy_turned(1, i - 1)
                if i + 1 < Q:
                    relu_first(i + 1)
                if i == 0:
                    squares(Q - 1)
                if i + 2 < Q:
                    normalise(3, i + 2)

        @block.tensor
        def _(pe):
            def transpose_x(n, q):
                pe.wait_ge(ln_out[n], q + 1)
                if n == 1 and q >= 1:
                    pe.wait_ge(x_apart_ok, q)
                elif q >= 2:
                    pe.wait_ge(xT_ok[n], q - 1)
                elif n == 2:
                    pe.wait_ge(x_apart_ok, Q)
                elif n >= 1:
                    pe.wait_ge(xT_ok[n - 1], Q - 1 + q)
                for b in range(PQ):
                    last = nc.tensor.transpose(psum[:, bank_of(n, q), b * P:(b + 1) * P],
                                               xn[:, q * C + b * P:q * C + (b + 1) * P], ident)
                last.then_inc(xT_ps[n], 1)

            pe.wait_ge(consts_in, 16)
            pe.wait_ge(small_in, 32)
            for n in range(HALVES):
                last = nc.tensor.matmul(psum[n * D:(n + 1) * D, 7, 0:D], wqk[:, 0, :], wqk[:, 1, :],
                                        start=True, stop=True)
            last.then_inc(score_w_ps, 1)

            def project(q):
                pe.wait_ge(xT_ok[0], q + 1)
                if q >= 1:
                    pe.wait_ge(z_ok, q)
                nc.tensor.matmul(psum[:, 2, 0:C], score_w[:, :], xT[:, qs(q)], start=True, stop=True).then_inc(z_ps, 1)

            def scores(q):
                pe.wait_ge(z_ok, q + 1)
                if q >= 2:
                    pe.wait_ge(s_masked, q - 1)
                for b in range(PQ):
                    last = nc.tensor.matmul(psum[:, 5 + q % 2, b * 2 * P:(b + 1) * 2 * P],
                                            xT[:, q * C + b * P:q * C + (b + 1) * P],
                                            apart[:, q, :, b * P:(b + 1) * P], start=True, stop=True)
                last.then_inc(s_ps, 1)
                if q >= 2:
                    pe.wait_ge(vs_ok, q - 1)
                for b in range(PQ):
                    last = nc.tensor.matmul(psum[:, 3 + q % 2, b * P:(b + 1) * P],
                                            xT[:, q * C + b * P:q * C + (b + 1) * P], diag[:, M_V0, :],
                                            start=True, stop=True)
                last.then_inc(v_ps, 1)

            def attend(q):
                pe.wait_ge(prob_ok, q + 1)
                pe.wait_ge(vs_ok, q + 1)
                if q >= 1:
                    pe.wait_ge(av_added, q)
                for b in range(PQ):
                    for n in range(HALVES):
                        at = slice(b * P + n * D, b * P + (n + 1) * D)
                        last = nc.tensor.matmul(psum[:, 7, at], prob[:, q % 2, b * HALVES + n, :],
                                                vs[:, q % 2, at], start=True, stop=True)
                last.then_inc(av_ps, 1)

            pe.wait_ge(score_w_ok, 2)
            pe.wait_ge(diag_in, 16 * 6)
            for i in range(Q):
                transpose_x(0, i)
                project(i)
                if i >= 2:
                    attend(i - 2)
                if i == Q - 1:
                    transpose_x(1, 0)
                scores(i)

            def router(q):
                pe.wait_ge(xT_ok[1], q + 1)
                if q == 0:
                    pe.wait_ge(xT_ok[0], Q)
                else:
                    pe.wait_ge(wT_ok, q)
                for b in range(PQ):
                    last = nc.tensor.matmul(psum[:, 1, b * HALVES * E:(b + 1) * HALVES * E],
                                            xT[:, q * C + b * P:q * C + (b + 1) * P], router_w[:, :],
                                            start=True, stop=True)
                last.then_inc(logit_ps, 1)

            def turn_weights(q):
                pe.wait_ge(weights_ok, q + 1)
                for b in range(PQ):
                    for n in range(HALVES):
                        at = (n * PQ + b) * P
                        nc.tensor.transpose(turned_w[0:PARTS * E, at:at + P],
                                            wsplit[:, q % 2, b * HALVES + n, :, :].rearrange("p a e -> p (a e)"),
                                            ident_b)
                nc.tensor.transpose(psum[0:BQ * E, 1, C:C + P],
                                    wfull[:, q % 2, :, :].rearrange("p b e -> p (b e)"), ident).then_inc(wT_ps, 1)

            def up(k):
                if k < 2:
                    pe.wait_ge(first_in, 64)
                    pe.wait_ge(vs_ok, Q - 1 + k)
                if k % E == 0:
                    pe.wait_ge(x_apart_ok, k // E + 1)
                if k >= 2:
                    pe.wait_ge(up_ok, k - 1)
                nc.tensor.matmul(psum[:, 3 + k % 2, :], first[:, k % E, :],
                                 apart[:, k // E, :, :].rearrange("p h c -> p (h c)"),
                                 start=True, stop=True).then_inc(up_ps, 1)

            def spread(k):
                if k == 0:
                    pe.wait_ge(s_masked, Q)
                if k % E == 0:
                    pe.wait_ge(wT_ok, k // E + 1)
                if k >= 2:
                    pe.wait_ge(weigh_ok, k - 1)
                nc.tensor.matmul(psum[:, 5 + k % 2, :], pick[:, k % E, :], wT_b[:, k // E % 2, :],
                                 start=True, stop=True).then_inc(spread_ps, 1)

            def down(k):
                pe.wait_ge(weigh_ok, k + 1)
                if k == 0:
                    pe.wait_ge(av_added, Q)
                    pe.wait_ge(hid_in, 32)
                elif k % E == 0:
                    pe.wait_ge(yT_ok, k // E)
                e = k % E
                for n in range(HALVES):
                    last = nc.tensor.matmul(psum[n * D:(n + 1) * D, 7, 0:C],
                                            w2[:, e * D:(e + 1) * D],
                                            hid[:, k % 4, n * C:(n + 1) * C], start=e == 0, stop=e == E - 1)
                last.then_inc(down_ps, 1)

            def experts_out(q):
                pe.wait_ge(yT_ok, q + 1)
                if q >= 1:
                    pe.wait_ge(y_added, q)
                nc.tensor.matmul(psum[:, 2, 0:C], wT_f[:, q % 2, :], b2[:, :], start=True, stop=False,
                                 skip_group_check=True)
                for b in range(PQ):
                    last = nc.tensor.matmul(psum[:, 2, b * P:(b + 1) * P], yT[:, q % 2, b * P:(b + 1) * P], ident,
                                            start=False, stop=b == PQ - 1, skip_group_check=True)
                last.then_inc(y_ps, 1)

            router(0)
            attend(Q - 2)
            up(0)
            up(1)
            pe.wait_ge(pick_in, 16 * (1 + BQ))
            turn_weights(0)
            attend(Q - 1)
            spread(0)
            up(2)
            pe.wait_ge(z_ok, Q)
            for k in range(Q * E + 2):
                q, e = k // E, k % E
                if 0 < k and k + 2 < Q * E:
                    up(k + 2)
                if e == 0 and k >= 2:
                    down(k - 2)
                if 0 < k < Q * E:
                    spread(k)
                if e != 0 and k >= 2:
                    down(k - 2)
                if e == 0 and q + 1 < Q:
                    transpose_x(1, q + 1)
                if e == 1 and q + 1 < Q:
                    router(q + 1)
                if e == 3 and q >= 1:
                    experts_out(q - 1)
                if e == 7 and q + 1 < Q:
                    turn_weights(q + 1)
            experts_out(Q - 1)

            def gates(q):
                pe.wait_ge(xT_ok[2], q + 1)
                if q == 0:
                    pe.wait_ge(y_added, Q)
                    pe.wait_ge(up_ok, Q * E)
                    pe.wait_ge(weigh_ok, Q * E)
                    pe.wait_ge(yT_ok, Q)
                if q >= 2:
                    pe.wait_ge(gates_read, q - 1)
                bank = 2 + q % 2 * 3
                for k, at in ((M_I, 0), (M_F, C)):
                    last = nc.tensor.matmul(psum[:, bank, at:at + C], diag[:, k, :], xT[:, qs(q)],
                                            start=True, stop=True)
                last.then_inc(if_ps, 1)
                nc.tensor.matmul(psum[:, bank + 1, 0:C], diag[:, M_K, :], xT[:, qs(q)], start=True, stop=True)
                if q >= 1:
                    pe.wait_ge(q_ok, q)
                last = nc.tensor.matmul(psum[:, 4, 0:C], diag[:, M_Q, :], xT[:, qs(q)], start=True, stop=True)
                last.then_inc(gates_ps, 1)
                if q >= 1:
                    pe.wait_ge(vo_ok, q)
                for b in range(PQ):
                    last = nc.tensor.matmul(psum[:, 7, b * 2 * P:(b + 1) * 2 * P],
                                            xT[:, q * C + b * P:q * C + (b + 1) * P],
                                            diag[:, M_V:M_O + 1, :].rearrange("p m c -> p (m c)"),
                                            start=True, stop=True)
                last.then_inc(vo_ps, 1)

            def score(q):
                pe.wait_ge(gates_read, q + 1)
                pe.wait_ge(q_ok, q + 1)
                if q < 2:
                    pe.wait_ge(gates_read, Q)
                else:
                    pe.wait_ge(score_ok, q - 1)
                for b in range(PQ):
                    last = nc.tensor.matmul(psum[:, 5 + q % 2, b * 2 * P:(b + 1) * 2 * P],
                                            kT[:, q * C + b * P:q * C + (b + 1) * P],
                                            apart[:, q, :, b * P:(b + 1) * P], start=True, stop=True)
                last.then_inc(score_ps, 1)

            def decays(q):
                pe.wait_ge(decay_ok, q + 1)
                if q == 0:
                    pe.wait_ge(q_ok, Q)
                else:
                    pe.wait_ge(decay_t, q)
                for k, src in enumerate((phi, li)):
                    for b in range(PQ):
                        last = nc.tensor.transpose(psum[:, 4, k * C + b * P:k * C + (b + 1) * P],
                                                   src[:, q * C + b * P:q * C + (b + 1) * P], ident)
                last.then_inc(decay_ps, 1)

            def normaliser(q):
                pe.wait_ge(nq_ok, q + 1)
                if q == 0:
                    pe.wait_ge(vo_ok, Q)
                for b in range(PQ):
                    k = q * BQ + b * HALVES
                    last = nc.tensor.matmul(psum[:, 7, k:k + HALVES],
                                            sp[:, q * C + b * P:q * C + (b + 1) * P],
                                            consts[:, C_HALF:C_HALF + HALVES], start=True, stop=True)
                last.then_inc(den_ps, 1)

            def own_scores(q):
                pe.wait_ge(qk_ok, q + 1)
                if q == 0:
                    pe.wait_ge(vo_ok, Q)
                for b in range(PQ):
                    k = B + q * BQ + b * HALVES
                    last = nc.tensor.matmul(psum[:, 7, k:k + HALVES],
                                            qk[:, q * C + b * P:q * C + (b + 1) * P],
                                            consts[:, C_HALF:C_HALF + HALVES], start=True, stop=True)
                last.then_inc(own_ps, 1)

            for i in range(Q + 1):
                if i < Q:
                    transpose_x(2, i)
                if 0 <= i - 1 < Q:
                    gates(i - 1)
            for q in range(Q - 1):
                own_scores(q)
            def arguments(q, n):
                k = 3 * q + n
                if q == 0 and n == 0:
                    pe.wait_ge(levels_in, 16)
                    pe.wait_ge(xT_ok[2], Q)
                pe.wait_ge(decay_t, q + 1)
                if k >= 2:
                    before = k - 2
                    pe.wait_ge(G_ok, 4 * (before // 3) + before % 3 + 1)
                for j in range(2):
                    at = C_SUM + (2 * n + j) * P
                    last = nc.tensor.matmul(psum[:, k % 2, j * C:(j + 1) * C], consts[:, at:at + P],
                                            phi_t[:, q, :], start=True, stop=True)
                last.then_inc(arg_ps, 1)

            def recall(q, n):
                k = 4 * q + n
                if n == 0:
                    pe.wait_ge(level_s_ok, q + 1)
                if n < 3:
                    pe.wait_ge(vg_ok, 3 * q + n + 1)
                if k >= 4:
                    pe.wait_ge(u_read, k - 3)
                elif n == 3:
                    pe.wait_ge(rden_ok, 1)
                for lv in range(2 * n, min(2 * n + 2, LEVELS)):
                    j = lv % 2
                    for b in range(PQ):
                        for s in range(HALVES):
                            at = slice(b * P + s * D, b * P + (s + 1) * D)
                            rhs = (vg[:, (3 * q + n) % 4, j, at] if n < 3 else
                                   vo[:, q * PQ + b, s * D:(s + 1) * D])
                            w = (b * HALVES + s) * P
                            last = nc.tensor.matmul(psum[:, U_BANKS[n], j * C + b * P + s * D:
                                                         j * C + b * P + (s + 1) * D],
                                                    level_s[:, q % 2, lv, w:w + P], rhs, start=True, stop=True)
                last.then_inc(u_ps, 1)

            decays(0)
            score(0)
            decays(1)
            arguments(0, 0)
            score(1)
            decays(2)
            arguments(0, 1)
            decays(3)
            arguments(0, 2)
            own_scores(Q - 1)
            for q in range(Q):
                normaliser(q)
            score(2)
            for i in range(1, Q + 1):
                for n in range(4):
                    if i < Q and n < 3:
                        arguments(i, n)
                    recall(i - 1, n)
                    if i == Q and n == 1:
                        transpose_x(3, 0)
                if i == 1:
                    score(3)

            def feed_first(q):
                pe.wait_ge(xT_ok[3], q + 1)
                if q == 0:
                    pe.wait_ge(u_read, 4 * Q - 3)
                else:
                    pe.wait_ge(f0_ok, q)
                nc.tensor.matmul(psum[:, 2, :], wi[:, :], apart[:, q, :, :].rearrange("p h c -> p (h c)"),
                                 start=True, stop=True).then_inc(f0_ps, 1)

            def feed_layer(n, q):
                if q == 0 and n == 0:
                    pe.wait_ge(hot_ok, 2)
                    pe.wait_ge(u_read, 4 * Q - 1)
                if q >= 1:
                    pe.wait_ge(token_ok[n], q)
                for t in range(BQ):
                    nc.tensor.matmul(psum[:, 3 + n, t * P:(t + 1) * P],
                                     one_hot[:, (q * BQ + t) * P:(q * BQ + t + 1) * P],
                                     bias_b[:, n * HID:(n + 1) * HID], start=t == 0, stop=False,
                                     skip_group_check=True)
                pe.wait_ge(slot_ok[q], GQ)
                if n == 0:
                    pe.wait_ge(f0_ok, q + 1)
                else:
                    pe.wait_ge(turned_ok[0], q + 1)
                for g in range(GQ):
                    t, r = g // (P // GT), g % (P // GT) * GT
                    slots, w = slots_of(q, g)
                    w += n * HID
                    last = nc.tensor.matmul(psum[r:r + GT, 3 + n, t * P:(t + 1) * P],
                                            (f0, f1)[n][:, q % 2, g * GT:(g + 1) * GT], slots[:, w:w + HID],
                                            start=False, stop=g == GQ - 1, skip_group_check=True)
                last.then_inc(layer_ps[n], 1)

            def turn(n, q):
                pe.wait_ge(token_ok[n], q + 1)
                if q == 0 and n == 0:
                    pe.wait_ge(score_ok, Q)
                if q >= 1:
                    pe.wait_ge(turned_ok[n], q)
                for t in range(BQ):
                    last = nc.tensor.transpose(psum[:, 5 + n, t * P:(t + 1) * P],
                                               token[:, n, t * P:(t + 1) * P], ident)
                last.then_inc(turned_ps[n], 1)

            def feed_last(q):
                pe.wait_ge(turned_ok[1], q + 1)
                if q == 0:
                    pe.wait_ge(u_read, 4 * Q)
                elif q == 1:
                    pe.wait_ge(xT_ok[3], Q - 1)
                else:
                    pe.wait_ge(out_ok, q - 1)
                for b in range(PQ):
                    for n in range(HALVES):
                        at = b * P + n * D
                        last = nc.tensor.matmul(psum[:, last_bank(q), at:at + D],
                                                f2[:, q % 2, n * C + b * P:n * C + (b + 1) * P],
                                                hidw[:, W_WO:W_WO + D], start=True, stop=True)
                last.then_inc(fo_ps, 1)

            feed_first(0)
            for i in range(Q + 1):
                if i < Q:
                    feed_layer(0, i)
                if 0 <= i - 1 < Q:
                    feed_layer(1, i - 1)
                if i + 1 < Q:
                    transpose_x(3, i + 1)
                if i < Q:
                    turn(0, i)
                if i == Q:
                    feed_last(Q - 3)
                if 0 <= i - 1 < Q:
                    turn(1, i - 1)
                if i + 1 < Q:
                    feed_first(i + 1)
                if 0 <= i - 2 < Q - 3:
                    feed_last(i - 2)
            feed_last(Q - 2)
            feed_last(Q - 1)

        @block.vector
        def _(dve):
            count = [0]

            def link(ins):
                count[0] += 1
                ins.then_inc(v_order, 1)
                dve.wait_ge(v_order, count[0])

            nc.vector.memset(router_w[:, :], 0.0)
            nc.vector.memset(diag[:, :, :], 0.0).then_inc(diag_zeroed, 1)
            nc.vector.memset(score_w[:, :], 0.0).then_inc(score_w_ok, 1)
            nc.vector.memset(nm[:, :, 0:1], 0.0).then_inc(nm_zeroed, 1)
            nc.vector.memset(apart[:, :, :, :], 0.0).then_inc(apart_zeroed, 1)
            nc.vector.memset(half[:, :], 0.5).then_inc(half_ok, 1)
            dve.wait_ge(score_w_ps, 1)
            dve.wait_ge(score_w_ok, 1)
            nc.vector.tensor_copy(score_w[0:D, 0:D], psum[0:D, 7, 0:D])
            nc.vector.tensor_copy(score_w[D:P, D:P], psum[D:P, 7, 0:D]).then_inc(score_w_ok, 1)
            def gate_biases():
                dve.wait_ge(small_in, 32)
                dve.wait_ge(diag_in, 16 * 6)
                for n in range(2):
                    for s in range(HALVES):
                        nc.vector.tensor_copy(gate_bias[:, (n * HALVES + s) * D:(n * HALVES + s + 1) * D],
                                              rows[:, R_BV + n * D:R_BV + (n + 1) * D])
                link(nc.vector.tensor_tensor(gate_cols[:, 0:1], cols[:, K_BGI:K_BGI + 1], cols[:, K_IB:K_IB + 1], ALU.add))
                link(nc.vector.tensor_scalar(gate_cols[:, 0:1], gate_cols[:, 0:1], 0.1, None, ALU.mult))
                nc.vector.tensor_scalar(gate_cols[:, 1:2], cols[:, K_BK:K_BK + 1], SCALE, None, ALU.mult).then_inc(setup_ok, 1)

            def feed_one_hot():
                dve.wait_ge(route_in, 16)
                link(nc.vector.tensor_copy(route_f[:, :], route_sb[:, :]))
                nc.vector.tensor_scalar(one_hot[:, :].rearrange("p (g t) -> p g t", g=GROUPS),
                                        per_seq(route_f[:, :], GROUPS, GT), consts[:, C_ROW:C_ROW + 1], None,
                                        ALU.is_equal).then_inc(hot_ok, 1)

            def feed_biases():
                dve.wait_ge(bias_in, 16 * (PARTS + 1))
                link(nc.vector.tensor_tensor(bias_rows[:, :], bias_rows[:, :], bias_sh[:, :], ALU.add))
                for n, spans in enumerate((((0, P),), ((32, 64), (64, P)), ((64, P),))):
                    for lo, hi in spans:
                        if n > 0:
                            link(nc.vector.tensor_tensor(bias_rows[lo:hi, :], bias_rows[lo:hi, :],
                                                         bias_b[lo:hi, :], ALU.subtract))
                        link(nc.vector.tensor_copy(bias_b[lo:hi, :], bias_rows[lo:hi, :]))
                nc.vector.memset(route_f[:, 0:1], 0.0).then_inc(hot_ok, 1)

            def stats(n, q):
                for b in range(q * BQ, (q + 1) * BQ):
                    last = nc.vector.bn_stats(bn[:, b, :], h[:, b * D:(b + 1) * D])
                link(last)
                for b in range(q * BQ, (q + 1) * BQ):
                    last = nc.vector.bn_aggr(mv[:, n, b, :], bn[:, b, :])
                last.then_inc(ln_stats[n], 1)

            def normalise(n, q):
                dve.wait_ge(ln_rstd[n], q + 1)
                for b in range(q * BQ, (q + 1) * BQ):
                    last = nc.vector.tensor_scalar(xn[:, b * D:(b + 1) * D], h[:, b * D:(b + 1) * D],
                                                   mv[:, n, b, 0:1], rstd[:, n, b:b + 1], ALU.subtract, ALU.mult)
                last.then_inc(ln_out[n], 1)

            def embed(q):
                dve.wait_ge(embed_in[q], 16 * BQ)
                link(nc.vector.tensor_tensor(h[:, qs(q)].rearrange("p (b d) -> p b d", b=BQ),
                                             h[:, qs(q)].rearrange("p (b d) -> p b d", b=BQ),
                                             repeated(consts[:, C_POS:C_POS + D], BQ, D), ALU.add))
                stats(0, q)

            def softmax_bias(q):
                dve.wait_ge(s_ps, q + 1)
                if q >= 2:
                    dve.wait_ge(prob_ok, q - 1)
                nc.vector.tensor_tensor(sc[:, q % 2, :, :],
                                        psum[:, 5 + q % 2, :].rearrange("p (b t) -> p b t", b=BQ),
                                        repeated(consts[:, C_CAUSAL:C_CAUSAL + P], BQ, P),
                                        ALU.subtract).then_inc(s_masked, 1)
                dve.wait_ge(s_masked, q + 1)
                seqs = slice(q * BQ, (q + 1) * BQ)
                link(nc.vector.tensor_reduce(nmax[:, seqs], sc[:, q % 2, :, :], AX.X, ALU.max, negate=True))
                nc.vector.tensor_scalar(nbias[:, seqs], nmax[:, seqs], SCALE, None, ALU.mult).then_inc(s_bias, 1)

            def scale_v(q):
                seqs = slice(q * BQ, (q + 1) * BQ)
                dve.wait_ge(prob_ok, q + 1)
                link(nc.vector.reciprocal(rsum[:, seqs], psums[:, seqs]))
                dve.wait_ge(v_ps, q + 1)
                if q >= 2:
                    dve.wait_ge(av_ps, q - 1)
                nc.vector.tensor_tensor(vs[:, q % 2, :].rearrange("p (b d) -> p b d", b=BQ),
                                        psum[:, 3 + q % 2, 0:C].rearrange("p (b d) -> p b d", b=BQ),
                                        per_seq(rsum[:, seqs]), ALU.mult).then_inc(vs_ok, 1)

            def add_attention(q):
                dve.wait_ge(av_ps, q + 1)
                nc.vector.tensor_tensor(h[:, qs(q)], psum[:, 7, 0:C], h[:, qs(q)], ALU.add).then_inc(av_added, 1)
                dve.wait_ge(av_added, q + 1)
                stats(1, q)

            dve.wait_ge(consts_in, 16)
            def compare(q):
                a = q % 2
                lg, cmp = logit[:, a], ge[:, a]
                dve.wait_ge(logit_ps, q + 1)
                link(nc.vector.tensor_tensor(lg, psum[:, 1, 0:BQ * E].rearrange("p (b e) -> p b e", b=BQ),
                                             repeated(rows[:, R_BR:R_BR + E], BQ, E), ALU.add))
                link(nc.vector.tensor_tensor(cmp, lg.unsqueeze(2).to_broadcast([P, BQ, E, E]),
                                             lg.unsqueeze(3).to_broadcast([P, BQ, E, E]), ALU.is_ge))
                flat = cmp.rearrange("p b e j -> p b (e j)")
                link(nc.vector.tensor_tensor(flat, flat, repeated(consts[:, C_TIE:C_TIE + E * E], BQ, E * E),
                                             ALU.mult))

            def rank(q):
                a = q % 2
                cmp, se, bk = ge[:, a], sel[:, a], back[:, a]
                nc.vector.tensor_reduce(se, cmp, AX.X, ALU.add)
                link(nc.vector.tensor_reduce(bk, cmp.rearrange("p b e j -> p b j e"), AX.X, ALU.add))
                link(nc.vector.tensor_tensor(se, se, bk, ALU.subtract))
                link(nc.vector.tensor_tensor(se, se, repeated(consts[:, C_RANK:C_RANK + E], BQ, E), ALU.is_lt))

            def centre(q):
                a = q % 2
                lg, se, bk = logit[:, a], sel[:, a], back[:, a]
                link(nc.vector.tensor_tensor(bk, se, lg, ALU.mult))
                link(nc.vector.tensor_reduce(lsum[:, a, :], bk, AX.X, ALU.add))
                link(nc.vector.tensor_scalar(lsum[:, a, :], lsum[:, a, :], 0.5, None, ALU.mult))
                nc.vector.tensor_tensor(off[:, a], lg, per_seq(lsum[:, a, :], BQ, E), ALU.subtract).then_inc(logit_off, 1)

            def weights(q):
                a = q % 2
                dve.wait_ge(tanh_ok, q + 1)
                if q >= 2:
                    dve.wait_ge(wT_ps, q - 1)
                link(nc.vector.tensor_scalar(off[:, a], off[:, a], 0.5, 0.5, ALU.mult, ALU.add))
                link(nc.vector.tensor_tensor(wfull[:, a], off[:, a], sel[:, a], ALU.mult))
                link(nc.vector.tensor_copy(wsplit[:, a, :, 0, :], wfull[:, a]))
                link(nc.vector.tensor_tensor(wrest[:, a], wfull[:, a], wsplit[:, a, :, 0, :], ALU.subtract))
                link(nc.vector.tensor_copy(wsplit[:, a, :, 1, :], wrest[:, a]))
                link(nc.vector.tensor_tensor(wrest[:, a], wrest[:, a], wsplit[:, a, :, 1, :], ALU.subtract))
                nc.vector.tensor_copy(wsplit[:, a, :, 2, :], wrest[:, a]).then_inc(weights_ok, 1)

            def weigh(k):
                dve.wait_ge(up_ok, k + 1)
                dve.wait_ge(spread_ps, k + 1)
                nc.vector.tensor_tensor(hid[:, k % 4, :], psum[:, 5 + k % 2, :], hid[:, k % 4, :],
                                        ALU.mult).then_inc(weigh_ok, 1)

            def add_experts(q):
                dve.wait_ge(y_ps, q + 1)
                nc.vector.tensor_tensor(h[:, qs(q)], psum[:, 2, 0:C], h[:, qs(q)], ALU.add).then_inc(y_added, 1)
                dve.wait_ge(y_added, q + 1)
                stats(2, q)

            embed(0)
            normalise(0, 0)
            embed(1)
            gate_biases()
            normalise(0, 1)
            embed(2)
            softmax_bias(0)
            scale_v(0)
            normalise(0, 2)
            softmax_bias(1)
            embed(3)
            add_attention(0)
            scale_v(1)
            normalise(0, 3)
            softmax_bias(2)
            add_attention(1)
            scale_v(2)
            softmax_bias(3)
            compare(0)
            rank(0)
            centre(0)
            scale_v(3)
            weights(0)
            add_attention(2)
            for k in range(Q * E):
                q, e = k // E, k % E
                weigh(k)
                if k == 0:
                    add_attention(3)
                if e == 1 and q + 1 < Q:
                    compare(q + 1)
                if e == 2 and q + 1 < Q:
                    rank(q + 1)
                if e == 3 and q + 1 < Q:
                    centre(q + 1)
                if e == 5 and q + 1 < Q:
                    weights(q + 1)
                if k == (Q - 1) * E + 1:
                    feed_one_hot()
                if k == (Q - 1) * E + 2:
                    feed_biases()
                if e == 4 and q >= 1:
                    add_experts(q - 1)
                if e == 7 and q >= 1:
                    normalise(2, q - 1)
            add_experts(Q - 1)
            normalise(2, Q - 1)

            def add_vo_bias(q):
                dve.wait_ge(vo_ps, q + 1)
                nc.vector.tensor_tensor(vo[:, q * PQ:(q + 1) * PQ, :],
                                        psum[:, 7, :].rearrange("p (b c) -> p b c", b=PQ),
                                        repeated(gate_bias[:, :], PQ, 2 * HALVES * D), ALU.add).then_inc(vo_ok, 1)

            def stabiliser(q):
                if q == 0:
                    dve.wait_ge(ln_f_ok, 1)
                    link(nc.vector.tensor_tensor(sp[:, qs(q)], sp[:, qs(q)], fs[:, qs(q)], ALU.subtract))
                else:
                    dve.wait_ge(softplus_ok, q)
                dve.wait_ge(log_i_ok, q + 1)
                for b in range(q * PQ, (q + 1) * PQ):
                    at = slice(b * P, (b + 1) * P)
                    last = nc.vector.tensor_tensor_scan(nm[:, b, 1:P + 1], sp[:, at], li[:, at], 0.0, ALU.add, ALU.min)
                last.then_inc(scan_ok, 1)
                dve.wait_ge(scan_ok, q + 1)
                pairs = slice(q * PQ, (q + 1) * PQ)

                def two(tile):
                    return tile[:, qs(q)].rearrange("p (b t) -> p b t", b=PQ)

                link(nc.vector.tensor_tensor(two(phi), nm[:, pairs, 1:P + 1], nm[:, pairs, 0:P], ALU.subtract))
                nc.vector.tensor_tensor(two(phi), two(phi), two(sp), ALU.subtract).then_inc(expo_ok, 1)

            def normaliser(q):
                dve.wait_ge(decay_ok, q + 1)
                link(nc.vector.tensor_tensor(sp[:, qs(q)], li[:, qs(q)], kT[:, qs(q)], ALU.mult))
                for b in range(q * PQ, (q + 1) * PQ):
                    at = slice(b * P, (b + 1) * P)
                    last = nc.vector.tensor_tensor_scan(sp[:, at], fs[:, at], sp[:, at], 0.0, ALU.mult, ALU.add)
                link(last)
                nc.vector.tensor_tensor(sp[:, qs(q)], sp[:, qs(q)], qT[:, qs(q)], ALU.mult).then_inc(nq_ok, 1)

            def weigh_v(q):
                dve.wait_ge(decay_t, q + 1)
                nc.vector.tensor_tensor(vo[:, q * PQ:(q + 1) * PQ, 0:P],
                                        vo[:, q * PQ:(q + 1) * PQ, 0:P],
                                        iota_t[:, q % 2, :].rearrange("p (b c) -> p b c", b=PQ),
                                        ALU.mult).then_inc(vi_ok, 1)

            def add_q_bias(q):
                dve.wait_ge(gates_ps, q + 1)
                bias = cols[:, K_BQ:K_BQ + 1]
                nc.vector.tensor_scalar(qT[:, qs(q)], psum[:, 4, 0:C], bias, None, ALU.add)
                for n in range(HALVES):
                    part = slice(n * D, (n + 1) * D)
                    last = nc.vector.tensor_scalar(apart[part, q, n, :], psum[part, 4, 0:C], bias[part], None,
                                                   ALU.add)
                last.then_inc(q_ok, 1)

            for q in range(Q):
                add_q_bias(q)
                add_vo_bias(q)
            def level_v(q, n):
                k = 3 * q + n
                dve.wait_ge(G_ok, 4 * q + n + 1)
                dve.wait_ge(vi_ok, q + 1)
                if k >= 4:
                    before = k - 4
                    dve.wait_ge(u_ps, 4 * (before // 3) + before % 3 + 1)
                nc.vector.tensor_tensor(
                    vg[:, k % 4, :, :].rearrange("p n (b c) -> p n b c", b=PQ),
                    G_of(q)[:, 2 * n:2 * n + 2, :].rearrange("p n (b c) -> p n b c", b=PQ),
                    vo[:, q * PQ:(q + 1) * PQ, 0:P].unsqueeze(1).to_broadcast([P, 2, PQ, P]),
                    ALU.mult).then_inc(vg_ok, 1)

            def level_u(q, n):
                k = 4 * q + n
                dve.wait_ge(u_ps, k + 1)
                dve.wait_ge(G_ok, k + 1)
                levels = slice(2 * n, min(2 * n + 2, LEVELS))
                width = (levels.stop - levels.start) * C
                nc.vector.tensor_tensor(ug[:, levels, :].rearrange("p n c -> p (n c)"),
                                        psum[:, U_BANKS[n], 0:width],
                                        G_of(q)[:, levels, :].rearrange("p n c -> p (n c)"),
                                        ALU.mult).then_inc(u_read, 1)

            def own_step(q):
                seqs = own[:, q * BQ:(q + 1) * BQ].rearrange("p (b s) -> p b s", b=PQ)
                nc.vector.tensor_tensor(
                    ug[:, LEVELS, :].rearrange("p (b s c) -> p b s c", b=PQ, s=HALVES),
                    vo[:, q * PQ:(q + 1) * PQ, 0:P].rearrange("p b (s c) -> p b s c", s=HALVES),
                    seqs.unsqueeze(3).to_broadcast([P, PQ, HALVES, D]), ALU.mult).then_inc(own_ok, 1)

            def gate_out(q):
                dve.wait_ge(sig_ok, 1)
                dve.wait_ge(u_read, 4 * q + 4)
                dve.wait_ge(own_ok, q + 1)
                link(nc.vector.tensor_reduce(acc[:, :], ug[:, :, :].rearrange("p n c -> p c n"), AX.X, ALU.add))
                nc.vector.tensor_tensor(gated[:, q % 2, :].rearrange("p (b c) -> p b c", b=PQ),
                                        acc[:, :].rearrange("p (b c) -> p b c", b=PQ),
                                        vo[:, q * PQ:(q + 1) * PQ, P:2 * P], ALU.mult).then_inc(gated_ok, 1)

            def add_recurrence(q):
                dve.wait_ge(rms_ok, q + 1)
                dve.wait_ge(scaled_ok, q + 1)
                for b in range(BQ):
                    k = q * BQ + b
                    last = nc.vector.scalar_tensor_tensor(h[:, k * D:(k + 1) * D],
                                                          scaled[:, q % 2, b * D:(b + 1) * D],
                                                          factor[:, k:k + 1], h[:, k * D:(k + 1) * D],
                                                          ALU.mult, ALU.add)
                link(last)
                stats(3, q)

            def relu_tokens(n, q):
                dve.wait_ge(layer_ps[n], q + 1)
                if q >= 1:
                    dve.wait_ge(turned_ps[n], q)
                nc.vector.tensor_scalar(token[:, n, :], psum[:, 3 + n, :], 0.0, None, ALU.max).then_inc(token_ok[n], 1)

            stabiliser(0)
            stabiliser(1)
            stabiliser(2)
            normaliser(0)
            normaliser(1)
            weigh_v(0)
            stabiliser(3)
            level_v(0, 0)
            normaliser(2)
            weigh_v(1)
            level_v(0, 1)
            normaliser(3)
            weigh_v(2)
            level_v(0, 2)
            weigh_v(3)
            dve.wait_ge(den_ps, Q)
            dve.wait_ge(own_ps, Q)
            link(nc.vector.tensor_copy(own[:, :], psum[:, 7, B:2 * B]))
            link(nc.vector.tensor_copy(rden[:, :], psum[:, 7, 0:B]))
            link(nc.vector.scalar_tensor_tensor(rden[:, :], rden[:, :], -1.0, rden[:, :], ALU.mult, ALU.max))
            link(nc.vector.tensor_scalar(rden[:, :], rden[:, :], 1e-6, None, ALU.max))
            link(nc.vector.reciprocal(rden[:, :], rden[:, :]))
            nc.vector.tensor_tensor(rden2[:, :], rden[:, :], rden[:, :], ALU.mult).then_inc(rden_ok, 1)

            for i in range(1, Q):
                for n in range(4):
                    if n < 3:
                        level_v(i, n)
                    level_u(i - 1, n)
                    if n == 0:
                        own_step(i - 1)
                gate_out(i - 1)
                if i == Q - 1:
                    level_u(i, 0)
                if 2 <= i:
                    add_recurrence(i - 2)
            own_step(Q - 1)
            for n in range(1, 4):
                level_u(Q - 1, n)
            add_recurrence(Q - 2)
            relu_tokens(0, 0)
            gate_out(Q - 1)
            relu_tokens(0, 1)
            relu_tokens(1, 0)
            add_recurrence(Q - 1)


            def add_last_bias(q):
                dve.wait_ge(ln_out[3], q + 1)
                h3 = h[:, qs(q)].rearrange("p (b d) -> p b d", b=BQ)
                nc.vector.tensor_tensor(h3, h3, repeated(rows[:, R_BO:R_BO + D], BQ, D), ALU.add).then_inc(biased, 1)

            def add_feed(q):
                dve.wait_ge(fo_ps, q + 1)
                dve.wait_ge(biased, q + 1)
                nc.vector.tensor_tensor(outs[:, qs(q)], psum[:, last_bank(q), 0:C], h[:, qs(q)],
                                        ALU.add).then_inc(out_ok, 1)

            for i in range(Q + 1):
                if 2 <= i < Q:
                    relu_tokens(0, i)
                if 1 <= i - 1 < Q:
                    relu_tokens(1, i - 1)
                if i < Q:
                    add_last_bias(i)
                if 0 <= i - 2 < Q - 3:
                    add_feed(i - 2)
            for q in range(Q - 3, Q):
                add_feed(q)


def kernel(**inputs):
    import concourse.bacc as bacc
    from concourse.bass_utils import run_bass_kernel_spmd

    a = {k: np.asarray(v) for k, v in inputs.items()}
    wg, bg = a["L1_attn_Wg"], a["L1_attn_bg"]
    arrays = {
        "table": a["L0_tok_W"],
        "tokens": a["x"].T,
        "route": a["L1_ffn_route_id"].reshape(Q, PQ, HALVES, P // GT).transpose(0, 2, 1, 3).reshape(GROUPS),
        "consts": shape_constants(),
        "pick": shape_constants_bf16(),
        "wqk": np.stack([a["L0_attn_Wq"], a["L0_attn_Wk"]], 1),
        "diag": np.stack([a["L0_attn_Wv"].T, wg[:, D:2 * D], wg[:, 0:D], a["L1_attn_Wq"], a["L1_attn_Wk"],
                          a["L1_attn_Wv"], wg[:, 2 * D:]], 1),
        "wr": a["L0_ffn_Wr"],
        "first": np.concatenate([a["L0_ffn_W1"].transpose(1, 0, 2), a["L1_ffn_Wi"].T[:, None, :]], 1),
        "cols": np.stack([a["L0_ffn_gamma"], a["L0_ffn_beta"], bg[0:D], a["L1_attn_input_bias"], bg[D:2 * D],
                          a["L1_attn_bq"], a["L1_attn_bk"]], 1),
        "rows": np.concatenate([a["L0_ffn_br"], a["L1_attn_norm_scale"], a["L1_ffn_bo"], a["L1_attn_bv"],
                                bg[2 * D:]]),
        "w2": a["L0_ffn_W2"].transpose(1, 0, 2).reshape(HID, E * D),
        "hid": np.concatenate([a["L1_ffn_Wo"].T, a["L0_ffn_b1"].T, a["L1_ffn_bi"][:, None]], 1),
        "b2": a["L0_ffn_b2"],
        "routed": a["L1_ffn_Wr"].transpose(3, 1, 0, 2).reshape(HID, NE1 * L1 * HID),
        "shared": a["L1_ffn_Ws"][:, 0].transpose(2, 0, 1).reshape(HID, L1 * HID),
        "bias": a["L1_ffn_br"].transpose(1, 0, 2).reshape(NE1, L1 * HID),
        "shared_bias": a["L1_ffn_bs"].reshape(L1 * HID),
    }
    nc = bacc.Bacc("TRN2", target_bir_lowering=False, num_devices=1)
    feeds, args = {}, []
    for name, x in arrays.items():
        x = np.ascontiguousarray(x)
        feeds[f"in_{name}"] = x
        args.append(nc.dram_tensor(f"in_{name}", x.shape, mybir.dt.from_np(x.dtype), kind="ExternalInput").ap())
    out = nc.dram_tensor("out_0", (B, P, D), F32, kind="ExternalOutput").ap()
    tower(nc, *args, out)
    r = run_bass_kernel_spmd(nc, [feeds], core_ids=[0])
    return r.results[0]["out_0"]
```
